# Optimizing a Trainium2 kernel written in Bass

```python
import numpy as np
import jax
import jax.numpy as jnp

def _softmax(x, axis=-1):
    return jax.nn.softmax(x, axis=axis)

def _gelu(x):
    return jax.nn.gelu(x, approximate=True)

def _silu(x):
    return jax.nn.silu(x)

def _sigmoid(x):
    return jax.nn.sigmoid(x)

def _layernorm(x, axis=-1, eps=1e-05):
    m = jnp.mean(x, axis=axis, keepdims=True)
    v = jnp.var(x, axis=axis, keepdims=True)
    return (x - m) / jnp.sqrt(v + eps)

def _scatter_add(tgt, idx, src, axis=0):
    return tgt.at[idx].add(src)

def _segment_sum(src, seg, n):
    return jax.ops.segment_sum(src, seg, n)
kernel_name = 'mk_early_fusion_embed_d1_tok_img1024_r4_8e3681'

def setup_inputs(seed: int=0):
    np.random.seed(seed)
    _w = jnp.asarray

    def _rec_inputs():
        import jax
        import jax.numpy as jnp
        _rk = jax.random.key(seed)
        x = 7.22013e-05 + 1.00017 * jax.random.normal(jax.random.fold_in(_rk, 1), (8, 64, 256, 4), jnp.float32)
        x_txt = jax.random.randint(jax.random.fold_in(_rk, 51), (8, 128), 0, 12564, jnp.int32)
        return (x, x_txt)
    x, x_txt = _rec_inputs()

    def _L0_tok_setup():
        import jax, jax.numpy as jnp
        import numpy as np
        B, F, L, H, D = (8, 64, 256, 4, 64)
        MODEL = H * F
        WIN = 128

        def _local_mask():
            m = np.ones((L, L), dtype=bool)
            m = np.tril(m, WIN - 1)
            m = np.triu(m, -(WIN - 1))
            return jnp.asarray(m)

        def _flatten(y):
            n = y.shape[0]
            return y.transpose(0, 2, 3, 1).reshape(n, L, -1)
        key = jax.random.key(seed)
        ks = jax.random.split(key, 12)
        s = lambda n: 1.0 / np.sqrt(n)
        xav = np.sqrt(6.0 / (L + L))
        return {'x': jax.random.normal(ks[0], (B, F, L, H), jnp.float32), 'Wq_w': jax.random.normal(ks[1], (D, F), jnp.float32) * s(F), 'Wq_b': jnp.zeros((D,), jnp.float32), 'Wk_w': jax.random.normal(ks[2], (D, F), jnp.float32) * s(F), 'Wk_b': jnp.zeros((D,), jnp.float32), 'Wv_w': jax.random.normal(ks[3], (D, F), jnp.float32) * s(F), 'Wv_b': jnp.zeros((D,), jnp.float32), 'w_bias': jax.random.uniform(ks[4], (L, L), jnp.float32, -xav, xav), 'out_w': jax.random.normal(ks[5], (H * D, MODEL), jnp.float32) * s(H * D), 'out_b': jnp.zeros((MODEL,), jnp.float32), 'ln_g': jnp.ones((MODEL,), jnp.float32), 'ln_b': jnp.zeros((MODEL,), jnp.float32), 'local_mask': _local_mask()}
    _L0_tok_all = _L0_tok_setup()
    _L0_tok_in = {k: v for k, v in _L0_tok_all.items() if k in ('Wq_w', 'Wq_b', 'Wk_w', 'Wk_b', 'Wv_w', 'Wv_b', 'w_bias', 'out_w', 'out_b', 'ln_g', 'ln_b', 'local_mask')}
    del _L0_tok_all

    def _L0_txt_setup():
        import jax, jax.numpy as jnp
        import numpy as np
        VOCAB = 50257
        CUTOFFS = [5000, 10000, 50257]
        BAND_DIMS = [256, 64, 64]
        OUT_DIM = 256
        PAD_IDX = 0
        key = jax.random.key(seed)
        ks = jax.random.split(key, 8)
        tokens = jax.random.randint(ks[0], (8, 1024), 0, VOCAB, dtype=jnp.int32)
        prev = 0
        params = {}
        for i, (c, d) in enumerate(zip(CUTOFFS, BAND_DIMS)):
            size = c - prev
            E = jax.random.normal(ks[1 + 2 * i], (size, d), dtype=jnp.float32) * d ** (-0.5)
            if i == 0:
                E = E.at[PAD_IDX].set(0.0)
            bound = float(np.sqrt(6.0 / (d + OUT_DIM)))
            W = jax.random.uniform(ks[2 + 2 * i], (d, OUT_DIM), dtype=jnp.float32, minval=-bound, maxval=bound)
            params[f'E{i}'] = E
            params[f'W{i}'] = W
            prev = c
        return {'tokens': tokens, **params}
    _L0_txt_all = _L0_txt_setup()
    _L0_txt_in = {k: v for k, v in _L0_txt_all.items() if k in ('E0', 'W0', 'E1', 'W1', 'E2', 'W2')}
    del _L0_txt_all

    def _L0_attn_setup():
        import jax, jax.numpy as jnp
        import numpy as np
        B, N, D, H = (2, 512, 256, 16)
        HD = D // H
        SCALING = (D / H) ** 0.5
        EPS = 1e-05
        key = jax.random.key(seed)
        k1, k2, k3 = jax.random.split(key, 3)
        return {'z': jax.random.normal(k1, (B, N, D), dtype=jnp.float32), 'ln_scale': jnp.ones((D,), dtype=jnp.float32), 'ln_bias': jnp.zeros((D,), dtype=jnp.float32), 'w_qkv': jax.random.normal(k2, (D, 3 * D), dtype=jnp.float32) * D ** (-0.5), 'w_proj': jax.random.normal(k3, (D, D), dtype=jnp.float32) * D ** (-0.5), 'b_proj': jnp.zeros((D,), dtype=jnp.float32)}
    _L0_attn_all = _L0_attn_setup()
    _L0_attn_in = {k: v for k, v in _L0_attn_all.items() if k in ('ln_scale', 'ln_bias', 'w_qkv', 'w_proj', 'b_proj')}
    del _L0_attn_all

    def _L0_ffn_setup():
        import jax, jax.numpy as jnp
        import numpy as np
        NUM_EXPERTS = 8
        CAPACITY_FACTOR = 1.0
        key = jax.random.key(seed)
        k1, k2, k3, k4 = jax.random.split(key, 4)
        B, S, D, E, F = (8, 512, 256, NUM_EXPERTS, 1024)
        x = jax.random.normal(k1, (B, S, D), dtype=jnp.float32)
        router_w = jax.random.normal(k2, (D, E), dtype=jnp.float32) * D ** (-0.5)
        w1 = jax.random.normal(k3, (E, D, F), dtype=jnp.float32) * D ** (-0.5)
        w2 = jax.random.normal(k4, (E, F, D), dtype=jnp.float32) * F ** (-0.5)
        return {'x': x, 'router_w': router_w, 'w1': w1, 'w2': w2}
    _L0_ffn_all = _L0_ffn_setup()
    _L0_ffn_in = {k: v for k, v in _L0_ffn_all.items() if k in ('router_w', 'w1', 'w2')}
    del _L0_ffn_all
    return {'x': x, 'x_txt': x_txt, 'L0_tok_Wq_w': _L0_tok_in['Wq_w'], 'L0_tok_Wq_b': _L0_tok_in['Wq_b'], 'L0_tok_Wk_w': _L0_tok_in['Wk_w'], 'L0_tok_Wk_b': _L0_tok_in['Wk_b'], 'L0_tok_Wv_w': _L0_tok_in['Wv_w'], 'L0_tok_Wv_b': _L0_tok_in['Wv_b'], 'L0_tok_w_bias': _L0_tok_in['w_bias'], 'L0_tok_out_w': _L0_tok_in['out_w'], 'L0_tok_out_b': _L0_tok_in['out_b'], 'L0_tok_ln_g': _L0_tok_in['ln_g'], 'L0_tok_ln_b': _L0_tok_in['ln_b'], 'L0_tok_local_mask': _L0_tok_in['local_mask'], 'L0_txt_E0': _L0_txt_in['E0'], 'L0_txt_W0': _L0_txt_in['W0'], 'L0_txt_E1': _L0_txt_in['E1'], 'L0_txt_W1': _L0_txt_in['W1'], 'L0_txt_E2': _L0_txt_in['E2'], 'L0_txt_W2': _L0_txt_in['W2'], 'L0_attn_ln_scale': _L0_attn_in['ln_scale'], 'L0_attn_ln_bias': _L0_attn_in['ln_bias'], 'L0_attn_w_qkv': _L0_attn_in['w_qkv'], 'L0_attn_w_proj': _L0_attn_in['w_proj'], 'L0_attn_b_proj': _L0_attn_in['b_proj'], 'L0_ffn_router_w': _L0_ffn_in['router_w'], 'L0_ffn_w1': _L0_ffn_in['w1'], 'L0_ffn_w2': _L0_ffn_in['w2']}

def reference(x, x_txt, L0_tok_Wq_w, L0_tok_Wq_b, L0_tok_Wk_w, L0_tok_Wk_b, L0_tok_Wv_w, L0_tok_Wv_b, L0_tok_w_bias, L0_tok_out_w, L0_tok_out_b, L0_tok_ln_g, L0_tok_ln_b, L0_tok_local_mask, L0_txt_E0, L0_txt_W0, L0_txt_E1, L0_txt_W1, L0_txt_E2, L0_txt_W2, L0_attn_ln_scale, L0_attn_ln_bias, L0_attn_w_qkv, L0_attn_w_proj, L0_attn_b_proj, L0_ffn_router_w, L0_ffn_w1, L0_ffn_w2):
    import jax
    import jax.numpy as jnp

    def _L0_tok_ref(x, Wq_w, Wq_b, Wk_w, Wk_b, Wv_w, Wv_b, w_bias, out_w, out_b, ln_g, ln_b, local_mask):
        import jax, jax.numpy as jnp
        import numpy as np
        B, F, L, H, D = (8, 64, 256, 4, 64)
        MODEL = H * F
        WIN = 128

        def _local_mask():
            m = np.ones((L, L), dtype=bool)
            m = np.tril(m, WIN - 1)
            m = np.triu(m, -(WIN - 1))
            return jnp.asarray(m)

        def _flatten(y):
            n = y.shape[0]
            return y.transpose(0, 2, 3, 1).reshape(n, L, -1)

        def proj(w, b):
            y = jnp.einsum('nclh,dc->ndlh', x, w) + b[None, :, None, None]
            return _flatten(y)
        q = proj(Wq_w, Wq_b)
        k = proj(Wk_w, Wk_b)
        v = proj(Wv_w, Wv_b)
        wb = w_bias * local_mask.astype(w_bias.dtype)
        ew = jnp.exp(wb)
        ek = jnp.exp(k)
        num = jnp.einsum('ts,nsd->ntd', ew, ek * v)
        den = jnp.einsum('ts,nsd->ntd', ew, ek)
        y = jax.nn.sigmoid(q) * num / den
        h = y @ out_w + out_b + _flatten(x)
        mu = jnp.mean(h, axis=-1, keepdims=True)
        var = jnp.mean(jnp.square(h - mu), axis=-1, keepdims=True)
        return (h - mu) * jax.lax.rsqrt(var + 1e-05) * ln_g + ln_b

    def _L0_txt_ref(tokens, E0, W0, E1, W1, E2, W2):
        import jax, jax.numpy as jnp
        import numpy as np
        VOCAB = 50257
        CUTOFFS = [5000, 10000, 50257]
        BAND_DIMS = [256, 64, 64]
        OUT_DIM = 256
        PAD_IDX = 0
        Es = [E0, E1, E2]
        Ws = [W0, W1, W2]
        out = jnp.zeros(tokens.shape + (OUT_DIM,), dtype=jnp.float32)
        prev = 0
        for E, W, c in zip(Es, Ws, CUTOFFS):
            rel = jnp.clip(tokens - prev, 0, E.shape[0] - 1)
            emb = jnp.einsum('bsd,de->bse', E[rel], W)
            mask = (tokens >= prev) & (tokens < c)
            out = jnp.where(mask[..., None], emb, out)
            prev = c
        return out

    def _L0_attn_ref(z, ln_scale, ln_bias, w_qkv, w_proj, b_proj):
        import jax, jax.numpy as jnp
        import numpy as np
        B, N, D, H = (2, 512, 256, 16)
        HD = D // H
        SCALING = (D / H) ** 0.5
        EPS = 1e-05
        b, n, d = z.shape
        mu = jnp.mean(z, axis=-1, keepdims=True)
        var = jnp.mean(jnp.square(z - mu), axis=-1, keepdims=True)
        zn = (z - mu) / jnp.sqrt(var + EPS) * ln_scale + ln_bias
        qkv = zn @ w_qkv
        qkv5 = qkv.reshape(b, n, H, HD, 3)
        q = jnp.transpose(qkv5[..., 0], (0, 2, 1, 3))
        k = jnp.transpose(qkv5[..., 1], (0, 2, 1, 3))
        v = jnp.transpose(qkv5[..., 2], (0, 2, 1, 3))
        scores = jnp.einsum('bhqd,bhkd->bhqk', q, k) / SCALING
        att = jax.nn.softmax(scores, axis=-1)
        out = jnp.einsum('bhal,bhlv->bhav', att, v)
        out = jnp.transpose(out, (0, 2, 1, 3)).reshape(b, n, d)
        out = out @ w_proj + b_proj
        return z + out

    def _L0_ffn_ref(x, router_w, w1, w2):
        import jax, jax.numpy as jnp
        import numpy as np
        NUM_EXPERTS = 8
        CAPACITY_FACTOR = 1.0
        B, S, D = x.shape
        E = router_w.shape[1]
        T = B * S
        C = int(CAPACITY_FACTOR * T / E)
        x_flat = x.reshape(T, D)
        logits = x_flat @ router_w
        probs = jax.nn.softmax(logits, axis=-1)
        expert_idx = jnp.argmax(probs, axis=-1)
        gate = jnp.take_along_axis(probs, expert_idx[:, None], axis=1)[:, 0]
        onehot = jax.nn.one_hot(expert_idx, E, dtype=jnp.float32)
        pos_all = jnp.cumsum(onehot, axis=0) - 1.0
        pos = jnp.take_along_axis(pos_all, expert_idx[:, None], axis=1)[:, 0]
        pos = pos.astype(jnp.int32)
        keep = (pos < C).astype(x_flat.dtype)
        pos_c = jnp.clip(pos, 0, C - 1)
        expert_in = jnp.zeros((E, C, D), dtype=x_flat.dtype)
        expert_in = expert_in.at[expert_idx, pos_c].add(x_flat * keep[:, None])
        hidden = jax.nn.gelu(jnp.einsum('ecd,edf->ecf', expert_in, w1))
        expert_out = jnp.einsum('ecf,efd->ecd', hidden, w2)
        y = expert_out[expert_idx, pos_c] * (gate * keep)[:, None]
        return y.reshape(B, S, D)
    h = _L0_tok_ref(x, L0_tok_Wq_w, L0_tok_Wq_b, L0_tok_Wk_w, L0_tok_Wk_b, L0_tok_Wv_w, L0_tok_Wv_b, L0_tok_w_bias, L0_tok_out_w, L0_tok_out_b, L0_tok_ln_g, L0_tok_ln_b, L0_tok_local_mask)
    h = jnp.concatenate([h, _L0_txt_ref(x_txt, L0_txt_E0, L0_txt_W0, L0_txt_E1, L0_txt_W1, L0_txt_E2, L0_txt_W2)], axis=1)
    h = h + _L0_attn_ref(_layernorm(h, axis=-1), L0_attn_ln_scale, L0_attn_ln_bias, L0_attn_w_qkv, L0_attn_w_proj, L0_attn_b_proj)
    h = h + _L0_ffn_ref(_layernorm(h, axis=-1), L0_ffn_router_w, L0_ffn_w1, L0_ffn_w2)
    return h

_drawn_inputs = setup_inputs


def setup_inputs(seed=0):
    import zlib

    import numpy as np

    out = dict(_drawn_inputs(seed))
    spreads = {'L0_tok_Wq_b': (0.0, 0.677),
     'L0_tok_Wk_b': (0.0, 0.8),
     'L0_tok_Wv_b': (0.0, 0.1),
     'L0_tok_out_b': (0.0, 0.1),
     'L0_tok_ln_g': (1.0, 0.2),
     'L0_tok_ln_b': (0.0, 0.1),
     'L0_attn_ln_scale': (1.0, 0.2),
     'L0_attn_ln_bias': (0.0, 0.1),
     'L0_attn_b_proj': (0.0, 0.1)}
    factors = {'L0_tok_w_bias': 8.0}
    for name, (base, spread) in spreads.items():
        noise = np.random.default_rng([zlib.crc32(name.encode()), seed]).standard_normal(out[name].shape)
        drawn = base * np.exp(spread * noise) if base else spread * noise
        out[name] = jnp.asarray(drawn.astype(out[name].dtype))
    for name, factor in factors.items():
        out[name] = (out[name] * factor).astype(out[name].dtype)
    return out
```

```python
from contextlib import ExitStack

import concourse.bass as bass
from concourse import mybir

F32 = mybir.dt.float32
F32R = mybir.dt.float32r
I32 = mybir.dt.int32
U32 = mybir.dt.uint32
U8 = mybir.dt.uint8
ALU = mybir.AluOpType
ACT = mybir.ActivationFunctionType
AX = mybir.AxisListType

P = 128
B = 8
L = 256
LT = L // P
C = 64
D = 256
DT = D // P
N = 384
NT = N // P
NH = 16
HD = 16
HALF = NH // 2
GRP = 4
NG = NH // GRP
VC = HD + 1
EXPERTS = 8
FF = 1024
FT = FF // P
TOK = B * N
CAP = TOK // EXPERTS
CT = CAP // P
EPS = 1e-5
BANDS = [0, 5000, 10000, 50257]
SCALE = 1.0 / (D / NH) ** 0.5
PRING = 16
SRING = 2
TRING = 3

FUSION_SLOTS = {1: ["kv0", "kv1", "q"], 2: ["den", "num"], 3: ["aft", "text"], 4: ["aft_norm"], 6: ["stats"], 7: ["zn"],
                8: ["zt"], 9: ["qk0", "qk1"], 10: ["qk2", "qk3"]}
FINISH_SLOTS = {0: ["ot0", "ot1"], 1: ["ot2", "ot3"], 2: ["ont0", "ont1"], 3: ["proj0", "proj1"], 5: ["xn"], 6: ["xt0", "xt1"],
                8: ["route"], 9: ["pick"], 11: ["count"], 12: ["slots"]}


def bank_positions(slots, in_bank):
    place, at = {}, 0
    for tasks in slots.values():
        for name in tasks:
            place[name] = at
            at += in_bank.get(name, 1)
    return place, at


FUSION_AT, N_FUSION = bank_positions(FUSION_SLOTS, {"text": 2, "zt": 2, "aft_norm": 0, "stats": 0, "zn": 0})
FINISH_AT, N_FINISH = bank_positions(FINISH_SLOTS, {"xn": 0, "pick": 0, "slots": 0})


def early_fusion_kernel(nc, a, out):
    x_cl, x_lc, tokens = a["x_cl"], a["x_lc"], a["tokens"]
    E = [a["E0"], a["E1"], a["E2"]]

    qk_dram = nc.dram_tensor("qk_parts", [2, 2, 2 * D, N], F32, kind="Internal").ap()
    hb_dram = nc.dram_tensor("residual_in", [B, N, D], F32, kind="Internal").ap()
    h1_dram = nc.dram_tensor("residual_out", [TOK, D], F32, kind="Internal").ap()
    xe_dram = nc.dram_tensor("expert_in", [2 * TOK, D], F32, kind="Internal").ap()
    ye_dram = nc.dram_tensor("expert_out", [TOK, D], F32, kind="Internal").ap()

    with ExitStack() as ctx:
        def sb(name, shape, dt=F32):
            return ctx.enter_context(nc.sbuf_tensor(name, shape, dt))

        def bank(name):
            return ctx.enter_context(nc.psum_tensor(name, [P, 512], F32))

        def sem(name):
            return ctx.enter_context(nc.semaphore(name))

        ident = sb("ident", [P, P])
        upper = sb("upper", [P, P])
        ones = sb("ones", [P, P])
        wkv = sb("wkv", [P, 2, P])
        wq = sb("wq", [P, P])
        nbq = sb("nbq", [P, 1])
        rows = sb("rows", [P, 1536])
        kv_bias, out_b = rows[:, 0:512], rows[:, 512:768]
        ln_g, ln_b, b_proj = rows[:, 768:1024], rows[:, 1024:1280], rows[:, 1280:1536]
        ewT = sb("ewT", [P, LT, L])
        out_w = sb("out_w", [P, DT, D])
        w_txt = sb("w_txt", [P, 3, D])
        cols = sb("cols", [P, 2, DT])
        w_qkv = sb("w_qkv", [P, DT, 3 * D])
        w_proj = sb("w_proj", [P, DT, D])
        w_r = sb("w_r", [P, DT, EXPERTS])
        mhalf = sb("mhalf", [P, NT])
        iota8 = sb("iota8", [P, EXPERTS])
        trash = sb("trash", [P, B * NT])
        mask8 = sb("mask8", [P, LT, L], U8)
        gi = sb("gi", [P, 3], I32)
        msk = sb("msk", [P, 3])
        tok_i = sb("tok_i", [P, B], I32)
        tok_f = sb("tok_f", [P, B])
        rel_f = sb("rel_f", [P, 3, B])
        rel_i = sb("rel_i", [P, 3, B], I32)
        band = sb("band", [P, 3, B])
        band_t = sb("band_t", [P, 3, B])
        xc = sb("xc", [P, DT, L])
        xr = sb("xr", [P, LT, D])
        emb = sb("emb", [P, N])
        kvs = sb("kvs", [P, 512])
        embT = kvs[:, 0:N]
        ekv = sb("ekv", [P, LT, 512])
        zn = ekv[:, :, :].rearrange("p a b -> p (a b)")[:, 0:NT * D].rearrange("p (t d) -> p t d", t=NT)
        eq = sb("eq", [P, DT, L])
        yT = sb("yT", [P, DT, L])
        h = sb("h", [P, NT, D])
        hb = sb("hb", [P, NT, D])
        st_a = sb("st_a", [P, LT, 6])
        mv_a = sb("mv_a", [P, LT, 2])
        r_a = sb("r_a", [P, LT])
        st_b = sb("st_b", [P, NT, 6])
        mv_b = sb("mv_b", [P, NT, 2])
        r_b = sb("r_b", [P, NT])
        r_c = sb("r_c", [P, NT])
        r_bc = sb("r_bc", [P, NT])
        zT = sb("zT", [P, DT, N])
        hi = sb("hi", [P, 2, N], F32R)
        lo = sb("lo", [P, 2, N], F32R)
        v_aug = sb("v_aug", [P, 2, NT, NH, VC])
        mx = sb("mx", [P, NT, NH])
        nmx = sb("nmx", [P, NT, 2, NH])
        mT = sb("mT", [2 * NH, N], F32R)
        probs = sb("probs", [P, PRING, N])
        oS = sb("oS", [P, NG, N])
        rden = sb("rden", [P, NT, GRP])
        oN = sb("oN", [P, NT, D])
        tT = sb("tT", [P, DT, N])
        h1 = sb("h1", [P, NT, D])
        st_d = sb("st_d", [P, NT, 6])
        mv_d = sb("mv_d", [P, NT, 2])
        r_d = sb("r_d", [P, NT])
        xn = sb("xn", [P, NT, D])
        lg = sb("lg", [P, NT, EXPERTS])
        m8 = sb("m8", [P, NT, 8])
        i8 = sb("i8", [P, NT, 8], U32)
        ei = sb("ei", [P, NT])
        oh = sb("oh", [P, NT, EXPERTS])
        df = sb("df", [P, NT, EXPERTS])
        ex = sb("ex", [P, NT, EXPERTS])
        se = sb("se", [P, NT])
        run = sb("run", [P, NT + 1, EXPERTS])
        cp = sb("cp", [P, NT, EXPERTS])
        pos = sb("pos", [P, NT])
        keep = sb("keep", [P, NT])
        slot = sb("slot", [P, NT])
        sk = sb("sk", [P, NT])
        drop = sb("drop", [P, NT])
        si = sb("si", [P, NT], I32)
        gate = sb("gate", [P, B * NT])
        gidx = sb("gidx", [P, B * NT], I32)
        stacks = ExitStack()
        qst = stacks.enter_context(nc.sbuf_tensor("qst", [P, 4, HALF, N], F32R))
        kst = stacks.enter_context(nc.sbuf_tensor("kst", [P, 4, HALF, N], F32R))
        stacks.close()
        w1s = [sb(f"w1s{i}", [P, DT, FF]) for i in range(2)]
        w2s = [sb(f"w2s{i}", [P, FT, D]) for i in range(2)]
        hid = [sb(f"hid{i}", [P, FT, CAP]) for i in range(2)]
        h1f = sb("h1f", [P, B * NT, D])
        xe = [sb(f"xe{i}", [P, CT, D])[:, :, :] for i in range(2)]
        xeT = sb("xeT", [P, DT, CAP])
        ye = sb("ye", [P, CT, D])[:, :, :]
        yg = probs[:, :, :].rearrange("p a b -> p (a b)")[:, 0:4 * D].rearrange("p (n d) -> p n d", n=4)

        s_bank = [bank(f"s_bank{i}") for i in range(SRING)]
        t_bank = [bank(f"t_bank{i}") for i in range(TRING)]
        o_bank = bank("o_bank")
        f_bank = bank("f_bank")
        n_bank = bank("n_bank")

        names = """waits_apart consts_loaded tok_loaded mask_loaded zeroed mhalf_done ident_done upper_done iota_done trash_done counts_zeroed
        stacks_zeroed stacks_ready v_ones_done o_bank_cleared wmask_done ewT_done nbq_done band_steps bands_done xe_cleared
        xc_loaded xr_loaded xr_biased emb_loaded emb_masked index_done
        ek_done ekv_done den_inverted st_a_done mv_a_done r_a_step r_a_done h_norm h_scaled h_gained
        st_b_done mv_b_done r_b_step r_b_done zn_done hb_step hb_done hb_stored hi_done
        fusion_full fusion_taken v_full v_taken s_full s_taken nmx_hi nmx_done m_full m_taken
        t_full p_ready o_full o_taken
        finish_full finish_taken rden_done hb_back h1_stored st_d_done mv_d_done r_d_step r_d_done xn_done
        m8_done df_done ex_done i8_done ei_done oh_done run_done se_done slot_step gate_done slots_done scattered
        xeT_full xeT_taken hid_full hid_taken y_full y_taken ye_stored h1_loaded combined out_stored""".split()
        s = {n: sem(n) for n in names}
        part_stored = [sem("part_stored0"), sem("part_stored1")]
        qk_loaded = [[sem(f"qk_loaded{p}{q}") for q in range(2)] for p in range(2)]
        m_loaded = [sem("m_loaded0"), sem("m_loaded1")]
        w1_loaded = [sem("w1_loaded0"), sem("w1_loaded1")]
        w2_loaded = [sem("w2_loaded0"), sem("w2_loaded1")]
        xe_loaded = [sem("xe_loaded0"), sem("xe_loaded1")]
        gathered = [sem(f"gathered{i}") for i in range(4)]
        N_CONSTS = 17

        block = ctx.enter_context(nc.Block())

        def wait(eng, name, value):
            if not (isinstance(value, int) and value <= 0):
                eng.wait_ge(s[name] if isinstance(name, str) else name, value)

        def wait_apart(eng, name, value):
            wait(eng, name, value)
            if not isinstance(value, int):
                eng.sem_inc(s["waits_apart"], 1)

        def pipeline(eng, body):
            def one(it):
                body(it, it % 2, lambda k: (it + k) // 2, it + 2 < B, 0 <= it + 1 < B, 0 <= it < B, it >= 1)
            for it in range(-2, 2):
                one(it)
            with eng.Fori(1, (B - 2) // 2) as j:
                for i in range(2):
                    body(j * 2 + i, i, lambda k, i=i: j + (i + k) // 2, True, True, True, True)
            for it in range(B - 2, B + 1):
                one(it)

        def over_experts(eng, body):
            for e in (0, 1):
                body(e, e, 0)
            with eng.Fori(1, EXPERTS // 2) as j:
                for i in range(2):
                    body(j * 2 + i, i, j)
            for e in (EXPERTS, EXPERTS + 1):
                body(e, e % 2, e // 2)

        def is_real(e):
            return not isinstance(e, int) or 0 <= e < EXPERTS

        @block.sync
        def _(sp):
            for dst, src in ((rows[:, :], a["rows"]), (cols[:, :, :], a["cols"]), (nbq[0:C, :], a["bq"]), (nbq[C:P, :], a["bq"])):
                sp.dma_start(dst, src).then_inc(s["consts_loaded"], 16)
            sp.dma_start(tok_i[:, :], tokens).then_inc(s["tok_loaded"], 16)
            sp.wait_ge(s["zeroed"], 2)
            for i in range(2):
                d = slice(C * i, C * i + C)
                sp.dma_start(wkv[d, 0, d], a["WkT"]).then_inc(s["consts_loaded"], 16)
                sp.dma_start(wkv[d, 1, d], a["WvT"]).then_inc(s["consts_loaded"], 16)
                sp.dma_start(wq[d, d], a["WqT"]).then_inc(s["consts_loaded"], 16)
            for dst, src in (
                (out_w[:, :, :], a["out_w"].rearrange("(t p) n -> p t n", p=P)),
                (w_txt[:, 0:2, :], a["W0"].rearrange("(t p) n -> p t n", p=P)),
                (w_txt[0:64, 2, :], a["W1"]), (w_txt[64:128, 2, :], a["W2"]),
                (w_qkv[:, :, :], a["w_qkv"].rearrange("(t p) n -> p t n", p=P)),
                (w_proj[:, :, :], a["w_proj"].rearrange("(t p) n -> p t n", p=P)),
                (w_r[:, :, :], a["router_w"].rearrange("(t p) n -> p t n", p=P)),
            ):
                sp.dma_start(dst, src).then_inc(s["consts_loaded"], 16)
            sp.wait_ge(s["stacks_zeroed"], 2)
            for i in range(2):
                sp.dma_start(xe_dram[i * TOK // 2:(i + 1) * TOK // 2, :].rearrange("(p r) d -> p (r d)", p=32),
                             qst[96:P, :, :, :].bitcast(F32).rearrange("p a b c -> p (a b c)")).then_inc(s["xe_cleared"], 16)

            def body(it, par, pair, fusion, shift, attend, finish):
                if fusion:
                    b = it + 2
                    wait_apart(sp, "fusion_full", N_FUSION * (b - 1) + FUSION_AT["q"] + 1)
                    sp.dma_start(xc[:, :, :], x_cl[b].rearrange("(t p) l -> p t l", p=P)).then_inc(s["xc_loaded"], 16)
                    wait_apart(sp, "fusion_taken", N_FUSION * (b - 1) + FUSION_AT["aft"] + 1)
                    sp.dma_start(xr[:, :, :], x_lc[b].rearrange("(t p) c -> p t c", p=P)).then_inc(s["xr_loaded"], 16)
                if finish:
                    bf = it - 1
                    wait_apart(sp, "h1_stored", bf * 16)
                    wait_apart(sp, "xn_done", bf)
                    sp.dma_start(h1[:, :, :], hb_dram[bf].rearrange("(t p) d -> p t d", p=P)).then_inc(s["hb_back"], 16)
                if fusion:
                    wait_apart(sp, "hb_done", b + 1)
                    sp.dma_start(hb_dram[b].rearrange("(t p) d -> p t d", p=P), hb[:, :, :]).then_inc(s["hb_stored"], 16)
                if finish:
                    wait_apart(sp, "finish_taken", N_FINISH * bf + FINISH_AT["proj1"] + 1)
                    sp.dma_start(h1_dram[bass.ds(bf * N, N), :].rearrange("(t p) d -> p t d", p=P), h1[:, :, :]).then_inc(s["h1_stored"], 16)
                if fusion:
                    for n in range(4):
                        qk, row = n // 2, (n % 2) * P
                        wait_apart(sp, "hi_done", 4 * b + n + 1)
                        sp.dma_start(qk_dram[par, qk, row:row + P, :], hi[:, n % 2, :].bitcast(F32)).then_inc(part_stored[n % 2], 16)
                        wait_apart(sp, "fusion_taken", N_FUSION * b + FUSION_AT[f"qk{n}"] + 1)
                        sp.dma_start(qk_dram[par, qk, D + row:D + row + P, :], lo[:, n % 2, :].bitcast(F32)).then_inc(part_stored[n % 2], 16)
                    wait_apart(sp, part_stored[0], 64 * (b + 1))
                    wait_apart(sp, part_stored[1], 64 * (b + 1))

                def load_stacks(half):
                    if attend:
                        wait_apart(sp, "t_full", NH * NT * it + (half + 1) * HALF * NT)
                    sl = 2 * par + half
                    q_rows, k_rows = (qk_dram[par, i].rearrange("(p h) n -> p h n", h=NH)[:, half * HALF:(half + 1) * HALF, :] for i in range(2))
                    for stack, r0, r1, src in ((qst, 0, 32, q_rows), (qst, 32, 64, q_rows), (kst, 0, 32, k_rows),
                                               (kst, 32, 48, k_rows[16:32]), (kst, 48, 64, k_rows[0:16])):
                        sp.dma_start(stack[r0:r1, sl, :, :].bitcast(F32), src).then_inc(qk_loaded[par][half], 16)
                    sp.dma_start(qst[64:66, sl, :, :].bitcast(F32), kst[66:68, sl, :, :].bitcast(F32)).then_inc(qk_loaded[par][half], 16)

                if fusion:
                    sp.wait_ge(s["stacks_ready"], 1)
                    load_stacks(0)
                if shift:
                    wait_apart(sp, "m_taken", it + 2)
                    for half in range(2):
                        for part in range(2):
                            r = part * NH + half * HALF
                            sp.dma_start(qst[64 + part:65 + part, 2 * (1 - par) + half, :, :].bitcast(F32), mT[r:r + HALF, :].bitcast(F32))\
                                .then_inc(m_loaded[1 - par], 16)
                if fusion:
                    load_stacks(1)

            pipeline(sp, body)

            sp.wait_ge(s["t_full"], B * NH * NT)
            sp.wait_ge(s["h1_stored"], 16 * B)
            sp.dma_start(h1f[:, :, :], h1_dram.rearrange("(n p) d -> p n d", p=P)).then_inc(s["h1_loaded"], 16)
            sp.wait_ge(s["scattered"], 16 * B * NT)

            def expert(e, par, pair):
                if is_real(e):
                    wait_apart(sp, "xeT_full", 2 * (e - 1))
                    sp.dma_start(xe[par], xe_dram[bass.ds(e * CAP, CAP), :].rearrange("(t p) d -> p t d", p=P)).then_inc(xe_loaded[par], 16)
                    wait_apart(sp, "hid_full", FT * (e - 1))
                    sp.dma_start(w1s[par][:, :, :], a["w1"][e].rearrange("(t p) f -> p t f", p=P)).then_inc(w1_loaded[par], 16)
                    wait_apart(sp, "y_full", 2 * (e - 1))
                    sp.dma_start(w2s[par][:, :, :], a["w2"][e].rearrange("(t p) d -> p t d", p=P)).then_inc(w2_loaded[par], 16)
                if is_real(e - 2) and not (isinstance(e, int) and e < 2):
                    wait_apart(sp, "y_taken", 2 * (e - 1))
                    sp.dma_start(ye_dram[bass.ds((e - 2) * CAP, CAP), :].rearrange("(t p) d -> p t d", p=P), ye).then_inc(s["ye_stored"], 16)

            over_experts(sp, expert)
            for b in range(B):
                sp.wait_ge(s["combined"], (b + 1) * NT)
                sp.dma_start(out[b].rearrange("(t p) d -> p t d", p=P), h1f[:, b * NT:(b + 1) * NT, :]).then_inc(s["out_stored"], 16)
            sp.wait_ge(s["out_stored"], 16 * B)

        @block.gpsimd
        def _(pool):
            pool.memset(wkv[:, :, :], 0.0).then_inc(s["zeroed"], 1)
            pool.memset(wq[:, :], 0.0).then_inc(s["zeroed"], 1)
            pool.memset(ident[:, :], 0.0).then_inc(s["zeroed"], 1)
            pool.memset(ones[:, :], 1.0).then_inc(s["zeroed"], 1)
            pool.memset(mhalf[:, :], -0.5).then_inc(s["mhalf_done"], 1)
            pool.wait_ge(s["zeroed"], 4)
            pool.affine_select(out=ident[:, :], in_=ident[:, :], compare_op=ALU.not_equal, fill=1.0, base=0,
                               pattern=[[-1, P]], channel_multiplier=1).then_inc(s["ident_done"], 1)
            pool.affine_select(out=upper[:, :], in_=ones[:, :], compare_op=ALU.is_ge, fill=0.0, base=0,
                               pattern=[[1, P]], channel_multiplier=-1).then_inc(s["upper_done"], 1)
            pool.iota(iota8[:, :], pattern=[[1, EXPERTS]], base=0, channel_multiplier=0,
                      allow_small_or_imprecise_dtypes=True).then_inc(s["iota_done"], 1)
            pool.iota(trash[:, :], pattern=[[P, B * NT]], base=TOK, channel_multiplier=1,
                      allow_small_or_imprecise_dtypes=True).then_inc(s["trash_done"], 1)
            pool.memset(run[:, NT, :], 0.0).then_inc(s["counts_zeroed"], 1)

            def gather(b):
                wait(pool, "bands_done", 1)
                wait_apart(pool, "emb_masked", 3 * b)
                wait_apart(pool, "fusion_full", N_FUSION * (b - 1) + FUSION_AT["text"] + 1)
                pool.tensor_copy(gi[:, :], rel_i[:, :, bass.ds(b, 1)].rearrange("p a b -> p (a b)")).then_inc(s["index_done"], 1)
                pool.tensor_copy(msk[:, :], band[:, :, bass.ds(b, 1)].rearrange("p a b -> p (a b)")).then_inc(s["index_done"], 1)
                wait_apart(pool, "index_done", 2 * b + 2)
                for i, (c0, c1) in enumerate(((0, 256), (256, 320), (320, 384))):
                    pool.indirect_dma_start(emb[:, c0:c1], None, E[i], bass.IndirectOffsetOnAxis(ap=gi[:, i:i + 1], axis=0))\
                        .then_inc(s["emb_loaded"], 16)

            pool.wait_ge(s["counts_zeroed"], 1)
            pool.memset(qst[64:P, :, :, :].bitcast(F32), 0.0).then_inc(s["stacks_zeroed"], 1)
            pool.memset(kst[64:P, :, :, :].bitcast(F32), 0.0).then_inc(s["stacks_zeroed"], 1)
            pool.wait_ge(s["stacks_zeroed"], 2)
            pool.memset(kst[64:66, :, :, :].bitcast(F32), 1.0).then_inc(s["stacks_ready"], 1)
            pool.wait_ge(s["stacks_ready"], 1)
            pool.memset(v_aug[:, :, :, :, HD:VC], 1.0).then_inc(s["v_ones_done"], 1)
            pool.wait_ge(s["consts_loaded"], 16 * N_CONSTS)
            pool.wait_ge(s["mhalf_done"], 1)

            def body(it, par, pair, fusion, shift, attend, finish):
                if fusion:
                    b = it + 2
                    gather(b)
                    wait(pool, "xr_loaded", 16 * (b + 1))
                    for t in range(LT):
                        pool.tensor_tensor(xr[:, t, :], xr[:, t, :], out_b, ALU.add).then_inc(s["xr_biased"], 1)
                    wait_apart(pool, "emb_loaded", 48 * (b + 1))
                    for i, (c0, c1) in enumerate(((0, 256), (256, 320), (320, 384))):
                        pool.tensor_scalar(emb[:, c0:c1], emb[:, c0:c1], msk[:, i:i + 1], None, ALU.mult).then_inc(s["emb_masked"], 1)
                    wait_apart(pool, "mv_a_done", LT * (b + 1))
                    pool.tensor_scalar(r_a[:, :], mv_a[:, :, 1], EPS, None, ALU.add).then_inc(s["r_a_step"], 1)
                    wait(pool, "r_a_step", b + 1)
                    pool.tensor_tensor(r_a[:, :], r_a[:, :], mhalf[:, 0:LT], ALU.pow).then_inc(s["r_a_done"], 1)
                    for t in range(LT):
                        wait(pool, "h_norm", LT * b + t + 1)
                        pool.tensor_tensor(h[:, t, :], h[:, t, :], ln_g, ALU.mult).then_inc(s["h_scaled"], 1)
                    for t in range(LT):
                        wait(pool, "h_scaled", LT * b + t + 1)
                        pool.tensor_tensor(h[:, t, :], h[:, t, :], ln_b, ALU.add).then_inc(s["h_gained"], 1)
                if finish:
                    b = it - 1
                    wait(pool, "mv_d_done", NT * (b + 1))
                    wait_apart(pool, "xn_done", b)
                    pool.tensor_scalar(r_d[:, :], mv_d[:, :, 1], EPS, None, ALU.add).then_inc(s["r_d_step"], 1)
                    wait(pool, "r_d_step", b + 1)
                    pool.tensor_tensor(r_d[:, :], r_d[:, :], mhalf[:, :], ALU.pow).then_inc(s["r_d_done"], 1)
                if fusion:
                    b = it + 2
                    wait_apart(pool, "mv_b_done", NT * (b + 1))
                    pool.tensor_scalar(r_b[:, :], mv_b[:, :, 1], EPS, None, ALU.add).then_inc(s["r_b_step"], 1)
                    wait(pool, "r_b_step", 6 * b + 1)
                    pool.tensor_tensor(r_b[:, :], r_b[:, :], mhalf[:, :], ALU.pow).then_inc(s["r_b_step"], 1)
                    wait(pool, "r_b_step", 6 * b + 2)
                    pool.tensor_tensor(r_c[:, :], r_b[:, :], r_b[:, :], ALU.mult).then_inc(s["r_b_step"], 1)
                    wait(pool, "r_b_step", 6 * b + 3)
                    pool.tensor_tensor(r_c[:, :], r_c[:, :], mv_b[:, :, 1], ALU.mult).then_inc(s["r_b_step"], 1)
                    wait_apart(pool, "r_b_step", 6 * b + 4)
                    pool.tensor_scalar(r_c[:, :], r_c[:, :], EPS, None, ALU.add).then_inc(s["r_b_step"], 1)
                    wait(pool, "r_b_step", 6 * b + 5)
                    pool.tensor_tensor(r_c[:, :], r_c[:, :], mhalf[:, :], ALU.pow).then_inc(s["r_b_step"], 1)
                    wait(pool, "r_b_step", 6 * b + 6)
                    wait(pool, "zn_done", NT * b)
                    pool.tensor_tensor(r_bc[:, :], r_b[:, :], r_c[:, :], ALU.mult).then_inc(s["r_b_done"], 1)
                    wait_apart(pool, "hb_stored", 16 * b)
                    for t in range(NT):
                        pool.tensor_scalar(hb[:, t, :], h[:, t, :], mv_b[:, t, 0:1], r_b[:, t:t + 1], ALU.subtract, ALU.mult)\
                            .then_inc(s["hb_step"], 1)
                    for t in range(NT):
                        wait(pool, "hb_step", 6 * b + t + 1)
                        pool.tensor_tensor(hb[:, t, :], hb[:, t, :], h[:, t, :], ALU.add).then_inc(s["hb_step"], 1)
                    for t in range(NT):
                        wait(pool, "hb_step", 6 * b + NT + t + 1)
                        last = pool.tensor_tensor(hb[:, t, :], hb[:, t, :], b_proj, ALU.add)
                    last.then_inc(s["hb_done"], 1)
                if finish:
                    b = it - 1
                    pool.wait_ge(s["xe_cleared"], 32)
                    wait_apart(pool, "slots_done", b + 1)
                    for t in range(NT):
                        pool.indirect_dma_start(xe_dram, bass.IndirectOffsetOnAxis(ap=si[:, t:t + 1], axis=0), xn[:, t, :], None)\
                            .then_inc(s["scattered"], 16)

            pipeline(pool, body)

            pool.wait_ge(s["o_full"], NG * B)
            pool.wait_ge(s["slots_done"], B)
            pool.wait_ge(s["ye_stored"], 16 * EXPERTS)
            for n in range(B * NT):
                wait_apart(pool, "combined", n - 3)
                pool.indirect_dma_start(yg[:, n % 4, :], None, ye_dram, bass.IndirectOffsetOnAxis(ap=gidx[:, n:n + 1], axis=0))\
                    .then_inc(gathered[n % 4], 16)

        @block.scalar
        def _(act):
            act.dma_start(ewT[:, :, :], a["w_biasT"].rearrange("(t p) l -> p t l", p=P)).then_inc(s["mask_loaded"], 16)
            act.dma_start(mask8[:, :, :], a["maskT"].rearrange("(t p) l -> p t l", p=P)).then_inc(s["mask_loaded"], 16)
            act.wait_ge(s["wmask_done"], 2)
            nc.scalar.activation(ewT[:, :, :], ewT[:, :, :], ACT.Exp).then_inc(s["ewT_done"], 1)
            act.wait_ge(s["nbq_done"], 1)
            act.wait_ge(s["v_ones_done"], 1)

            def fusion_task(name, b):
                base = N_FUSION * b + FUSION_AT[name]
                if name in ("kv0", "kv1"):
                    t = int(name[2])
                    wait(act, "fusion_taken", base + 1)
                    nc.scalar.activation(ekv[:, t, 0:D], kvs[:, 0:D], ACT.Exp).then_inc(s["ek_done"], 1)
                if name == "q":
                    wait(act, "fusion_full", base + 1)
                    nc.scalar.activation(eq[:, :, :].rearrange("p a b -> p (a b)"), f_bank[:, :], ACT.Exp, bias=nbq[:, 0:1], scale=-1.0)\
                        .then_inc(s["fusion_taken"], 1)
                if name == "text":
                    wait(act, "fusion_full", base + 1)
                    wait(act, "ekv_done", LT * (b + 1))
                    nc.scalar.copy(embT, f_bank[:, 0:N]).then_inc(s["fusion_taken"], 1)
                    wait(act, "fusion_full", base + 2)
                    wait(act, "hb_done", b)
                    nc.scalar.copy(h[:, 2, :], f_bank[:, 0:D]).then_inc(s["fusion_taken"], 1)
                if name == "zt":
                    for i in range(DT):
                        wait(act, "fusion_full", base + i + 1)
                        wait(act, "v_full", 2 * b)
                        nc.scalar.activation(zT[:, i, :], f_bank[:, 0:N], ACT.Identity, bias=cols[:, 1, i:i + 1], scale=cols[:, 0, i:i + 1])\
                            .then_inc(s["fusion_taken"], 1)
                if name[:2] == "qk":
                    n = int(name[2])
                    wait(act, "fusion_full", base + 1)
                    wait(act, part_stored[n % 2], 64 * b + 32 * (n // 2))
                    nc.scalar.copy(hi[:, n % 2, :], f_bank[:, 0:N]).then_inc(s["hi_done"], 1)

            def finish_task(name, b):
                if name in ("ont0", "ont1", "xt0", "xt1"):
                    wait(act, "finish_full", N_FINISH * b + FINISH_AT[name] + 1)
                    nc.scalar.copy(tT[:, int(name[-1]), :], n_bank[:, 0:N]).then_inc(s["finish_taken"], 1)
                if name == "route":
                    wait(act, "df_done", b + 1)
                    nc.scalar.activation(ex[:, :, :], df[:, :, :], ACT.Exp).then_inc(s["ex_done"], 1)

            def body(it, par, pair, fusion, shift, attend, finish):
                if shift:
                    b = it + 1
                    for i, (t0, t1) in enumerate(((0, 2), (2, 3))):
                        wait(act, "v_full", 2 * b + i + 1)
                        wait(act, "o_full", NG * it)
                        nc.scalar.copy(v_aug[:, 1 - par, t0:t1, :, 0:HD],
                                       f_bank[:, 0:(t1 - t0) * D].rearrange("p (t h d) -> p t h d", t=t1 - t0, d=HD)).then_inc(s["v_taken"], 1)

                def take_o(g):
                    wait(act, "o_full", NG * it + g + 1)
                    if g == 0:
                        wait(act, "finish_full", N_FINISH * (it - 1) + FINISH_AT["ot3"] + 1)
                    nc.scalar.copy(oS[:, g, :], o_bank[:, 0:N]).then_inc(s["o_taken"], 1)

                for step in range(NH):
                    if attend:
                        for t in range(NT):
                            n = step * NT + t
                            wait(act, "t_full", NH * NT * it + n + 1)
                            wait(act, "o_full", NG * it + (n - PRING) // (GRP * NT) + 1)
                            nc.scalar.activation(probs[:, n % PRING, :], t_bank[n % TRING][:, 0:N], ACT.Exp, scale=SCALE)\
                                .then_inc(s["p_ready"], 1)
                        if step and step % GRP == 0:
                            take_o(step // GRP - 1)
                    if fusion:
                        for name in FUSION_SLOTS.get(step, ()):
                            fusion_task(name, it + 2)
                    if finish:
                        for name in FINISH_SLOTS.get(step, ()):
                            finish_task(name, it - 1)
                if attend:
                    take_o(NG - 1)

            pipeline(act, body)

            def expert(e, par, pair):
                if is_real(e):
                    wait(act, "y_full", 2 * (e - 1))
                    for f in range(FT):
                        wait(act, "hid_full", FT * e + f + 1)
                        nc.scalar.activation(hid[par][:, f, :], t_bank[f % 2][:, 0:CAP], ACT.Gelu_apprx_tanh).then_inc(s["hid_taken"], 1)

            over_experts(act, expert)

        @block.tensor
        def _(pe):
            pe.wait_ge(s["consts_loaded"], 16 * N_CONSTS)
            pe.wait_ge(s["ident_done"], 1)
            pe.wait_ge(s["upper_done"], 1)
            pe.wait_ge(s["ewT_done"], 1)
            pe.wait_ge(s["o_bank_cleared"], 1)

            def transpose3(to, src):
                for t in range(NT):
                    last = pe.transpose(to[0:src(t).shape[1], t * P:(t + 1) * P], src(t), ident[:, :])
                return last

            def fusion_task(name, b):
                base = N_FUSION * b + FUSION_AT[name]
                if name in ("aft_norm", "stats", "zn"):
                    return
                wait(pe, "fusion_taken", base)
                if name == "kv0":
                    wait(pe, "m_taken", b - 1)
                    wait(pe, "v_taken", 2 * b)
                    wait(pe, "xc_loaded", 16 * (b + 1))
                if name in ("kv0", "kv1"):
                    t = int(name[2])
                    for i in range(DT):
                        last = pe.matmul(f_bank[:, :].rearrange("p (k c) -> p k c", k=2)[:, :, i * P:(i + 1) * P],
                                         xc[:, i, t * P:(t + 1) * P], wkv[:, :, :], start=True, stop=True)
                    last.then_inc(s["fusion_full"], 1)
                if name == "q":
                    for i in range(DT):
                        last = pe.matmul(f_bank[:, i * L:(i + 1) * L], wq[:, :], xc[:, i, :], start=True, stop=True)
                    last.then_inc(s["fusion_full"], 1)
                if name in ("den", "num"):
                    c0 = D if name == "num" else 0
                    wait(pe, "ekv_done" if name == "num" else "ek_done", LT * (b + 1))
                    for i in range(DT):
                        for t in range(LT):
                            last = pe.matmul(f_bank[:, i * L:(i + 1) * L], ekv[:, t, c0 + i * P:c0 + (i + 1) * P], ewT[:, t, :],
                                             start=t == 0, stop=t == LT - 1)
                    last.then_inc(s["fusion_full"], 1)
                if name == "aft":
                    for t in range(LT):
                        for i in range(DT):
                            last = pe.matmul(f_bank[:, t * D:(t + 1) * D], yT[:, i, t * P:(t + 1) * P], out_w[:, i, :],
                                             start=i == 0, stop=i == DT - 1)
                    last.then_inc(s["fusion_full"], 1)
                if name == "text":
                    wait(pe, "emb_masked", 3 * (b + 1))
                    transpose3(f_bank, lambda t: emb[:, t * P:(t + 1) * P]).then_inc(s["fusion_full"], 1)
                    wait(pe, "fusion_taken", base + 1)
                    for i in range(3):
                        last = pe.matmul(f_bank[:, 0:D], embT[:, i * P:(i + 1) * P], w_txt[:, i, :], start=i == 0, stop=i == 2)
                    last.then_inc(s["fusion_full"], 1)
                if name == "zt":
                    wait(pe, "zn_done", NT * (b + 1))
                    for i in range(DT):
                        wait(pe, "fusion_taken", base + i)
                        transpose3(f_bank, lambda t: zn[:, t, i * P:(i + 1) * P]).then_inc(s["fusion_full"], 1)
                if name[:2] == "qk":
                    n = int(name[2])
                    for i in range(DT):
                        last = pe.matmul(f_bank[:, 0:N], w_qkv[:, i, n * P:(n + 1) * P], zT[:, i, :], start=i == 0, stop=i == DT - 1)
                    last.then_inc(s["fusion_full"], 1)

            def finish_task(name, b):
                base = N_FINISH * b + FINISH_AT[name]
                if name in ("xn", "pick", "slots"):
                    return
                wait(pe, "finish_taken", base)
                if name[:2] == "ot":
                    g = int(name[2])
                    wait(pe, "o_taken", NG * b + g + 1)
                    transpose3(n_bank, lambda t: oS[:, g, t * P:(t + 1) * P]).then_inc(s["finish_full"], 1)
                if name[:3] == "ont":
                    i = int(name[3])
                    transpose3(n_bank, lambda t: oN[:, t, i * P:(i + 1) * P]).then_inc(s["finish_full"], 1)
                if name[:4] == "proj":
                    t0, t1 = ((0, 2), (2, 3))[int(name[4])]
                    for t in range(t0, t1):
                        for i in range(DT):
                            last = pe.matmul(n_bank[:, (t - t0) * D:(t - t0 + 1) * D], tT[:, i, t * P:(t + 1) * P], w_proj[:, i, :],
                                             start=i == 0, stop=i == DT - 1)
                    last.then_inc(s["finish_full"], 1)
                if name[:2] == "xt":
                    i = int(name[2])
                    wait(pe, "xn_done", b + 1)
                    transpose3(n_bank, lambda t: xn[:, t, i * P:(i + 1) * P]).then_inc(s["finish_full"], 1)
                if name == "route":
                    for t in range(NT):
                        for i in range(DT):
                            last = pe.matmul(n_bank[:, t * EXPERTS:(t + 1) * EXPERTS], tT[:, i, t * P:(t + 1) * P], w_r[:, i, :],
                                             start=i == 0, stop=i == DT - 1)
                    last.then_inc(s["finish_full"], 1)
                if name == "count":
                    wait(pe, "run_done", (NT + 1) * (b + 1))
                    pe.matmul(n_bank[:, 0:NT * EXPERTS], upper[:, :], oh[:, :, :], start=True, stop=False)
                    pe.matmul(n_bank[:, 0:NT * EXPERTS], ones[:, :], run[:, 0:NT, :], start=False, stop=True).then_inc(s["finish_full"], 1)

            def body(it, par, pair, fusion, shift, attend, finish):
                if shift:
                    b = it + 1
                    wait(pe, "fusion_taken", N_FUSION * (b + 1))
                    wait(pe, "m_taken", b)
                    for i, (t0, t1) in enumerate(((0, 2), (2, 3))):
                        wait(pe, "v_taken", 2 * b + i)
                        for t in range(t0, t1):
                            for k in range(DT):
                                last = pe.matmul(f_bank[:, (t - t0) * D:(t - t0 + 1) * D], zT[:, k, t * P:(t + 1) * P],
                                                 w_qkv[:, k, 2 * D:3 * D], start=k == 0, stop=k == DT - 1)
                        last.then_inc(s["v_full"], 1)

                def attend_v(g):
                    wait(pe, "p_ready", NH * NT * it + (g + 1) * GRP * NT)
                    wait(pe, "v_taken", 2 * (it + 1))
                    wait(pe, "o_taken", NG * it + g)
                    for t in range(NT):
                        for k in range(GRP):
                            head = g * GRP + k
                            last = pe.matmul(o_bank[32 * k:32 * k + VC, 0:N], v_aug[:, par, t, head, :], probs[:, (head * NT + t) % PRING, :],
                                             start=t == 0, stop=t == NT - 1)
                    last.then_inc(s["o_full"], 1)

                for step in range(NH):
                    half, head = step // HALF, step % HALF
                    if shift:
                        b, sl = it + 1, 2 * (1 - par) + half
                        if head == 0:
                            wait(pe, qk_loaded[1 - par][half], 96 * (pair(1) + 1))
                        for t in range(NT):
                            n = step * NT + t
                            wait(pe, "s_taken", NH * NT * b + n + 1 - SRING)
                            pe.matmul(s_bank[n % SRING][:, 0:N], qst[:, sl, head, t * P:(t + 1) * P], kst[:, sl, head, :],
                                      start=True, stop=True).then_inc(s["s_full"], 1)
                    if attend:
                        sl = 2 * par + half
                        if step == 0:
                            wait(pe, m_loaded[par], 64 * (pair(0) + 1))
                        for t in range(NT):
                            n = step * NT + t
                            wait(pe, "p_ready", NH * NT * it + n + 1 - TRING)
                            pe.matmul(t_bank[n % TRING][:, 0:N], kst[:, sl, head, t * P:(t + 1) * P], qst[:, sl, head, :],
                                      start=True, stop=True).then_inc(s["t_full"], 1)
                        if step and step % GRP == 0:
                            attend_v(step // GRP - 1)
                    if fusion:
                        for name in FUSION_SLOTS.get(step, ()):
                            fusion_task(name, it + 2)
                    if finish:
                        for name in FINISH_SLOTS.get(step, ()):
                            finish_task(name, it - 1)
                if attend:
                    attend_v(NG - 1)
                if shift:
                    wait(pe, "fusion_taken", N_FUSION * (it + 3) if fusion else N_FUSION * B)
                    wait(pe, "v_taken", 2 * (it + 2))
                    wait(pe, "nmx_done", it + 2)
                    transpose3(f_bank, lambda t: nmx[:, t, :, :].rearrange("p a h -> p (a h)")).then_inc(s["m_full"], 1)

            pipeline(pe, body)
            pe.wait_ge(s["p_ready"], B * NH * NT)
            pe.wait_ge(s["s_taken"], B * NH * NT)
            pe.wait_ge(s["m_taken"], B)

            def expert(e, par, pair):
                if is_real(e):
                    for i in range(DT):
                        wait(pe, "xeT_taken", 2 * e + i)
                        wait(pe, xe_loaded[par], 16 * (pair + 1))
                        transpose3(f_bank, lambda t: xe[par][:, t, i * P:(i + 1) * P]).then_inc(s["xeT_full"], 1)
                    wait(pe, "xeT_taken", 2 * e + 2)
                    wait(pe, w1_loaded[par], 16 * (pair + 1))
                    for f in range(FT):
                        wait(pe, "hid_taken", FT * e + f - 1)
                        for i in range(DT):
                            last = pe.matmul(t_bank[f % 2][:, 0:CAP], w1s[par][:, i, f * P:(f + 1) * P], xeT[:, i, :],
                                             start=i == 0, stop=i == DT - 1)
                        last.then_inc(s["hid_full"], 1)
                if is_real(e - 1):
                    wait(pe, w2_loaded[1 - par], 16 * (pair + par))
                    wait(pe, "hid_taken", FT * e)
                    for part, (t0, t1) in enumerate(((0, 2), (2, 3))):
                        wait(pe, "y_taken", 2 * (e - 2) + part + 1)
                        for t in range(t0, t1):
                            for f in range(FT):
                                last = pe.matmul(s_bank[part][:, (t - t0) * D:(t - t0 + 1) * D], hid[1 - par][:, f, t * P:(t + 1) * P],
                                                 w2s[1 - par][:, f, :], start=f == 0, stop=f == FT - 1)
                        last.then_inc(s["y_full"], 1)

            over_experts(pe, expert)

        @block.vector
        def _(dve):
            nc.vector.memset(o_bank[:, :], 0.0).then_inc(s["o_bank_cleared"], 1)
            dve.wait_ge(s["tok_loaded"], 16)
            nc.vector.tensor_copy(tok_f[:, :], tok_i[:, :]).then_inc(s["band_steps"], 1)
            dve.wait_ge(s["band_steps"], 1)
            for i in range(3):
                low, high = float(BANDS[i]), float(BANDS[i + 1])
                nc.vector.tensor_scalar(rel_f[:, i, :], tok_f[:, :], low, 0.0, ALU.subtract, ALU.max).then_inc(s["band_steps"], 1)
                nc.vector.tensor_scalar(band[:, i, :], tok_f[:, :], low, None, ALU.is_ge).then_inc(s["band_steps"], 1)
                nc.vector.tensor_scalar(band_t[:, i, :], tok_f[:, :], high, None, ALU.is_lt).then_inc(s["band_steps"], 1)
            dve.wait_ge(s["band_steps"], 10)
            for i in range(3):
                nc.vector.tensor_scalar(rel_i[:, i, :], rel_f[:, i, :], float(BANDS[i + 1] - BANDS[i] - 1), None, ALU.min)
            nc.vector.tensor_tensor(band[:, :, :], band[:, :, :], band_t[:, :, :], ALU.mult).then_inc(s["bands_done"], 1)
            dve.wait_ge(s["mask_loaded"], 32)
            nc.vector.tensor_copy(eq[:, :, :], mask8[:, :, :]).then_inc(s["wmask_done"], 1)
            dve.wait_ge(s["wmask_done"], 1)
            nc.vector.tensor_tensor(ewT[:, :, :], ewT[:, :, :], eq[:, :, :], ALU.mult).then_inc(s["wmask_done"], 1)
            dve.wait_ge(s["consts_loaded"], 16 * N_CONSTS)
            nc.vector.tensor_scalar(nbq[:, :], nbq[:, :], -1.0, None, ALU.mult).then_inc(s["nbq_done"], 1)
            dve.wait_ge(s["iota_done"], 1)
            dve.wait_ge(s["trash_done"], 1)
            dve.wait_ge(s["counts_zeroed"], 1)
            flat = lambda v: v.rearrange("p a b -> p (a b)")

            def fusion_task(name, b):
                base = N_FUSION * b + FUSION_AT[name]
                if name in ("kv0", "kv1"):
                    t = int(name[2])
                    wait(dve, "fusion_full", base + 1)
                    if t == 1:
                        wait(dve, "ek_done", LT * b + 1)
                        wait(dve, "ekv_done", LT * b + 1)
                    nc.vector.tensor_tensor(kvs[:, :], f_bank[:, :], kv_bias, ALU.add).then_inc(s["fusion_taken"], 1)
                    wait(dve, "ek_done", LT * b + t + 1)
                    nc.vector.tensor_tensor(ekv[:, t, D:2 * D], ekv[:, t, 0:D], kvs[:, D:2 * D], ALU.mult).then_inc(s["ekv_done"], 1)
                if name == "den":
                    wait(dve, "fusion_full", base + 1)
                    nc.vector.scalar_tensor_tensor(out=flat(eq[:, :, :]), in0=flat(eq[:, :, :]), scalar=1.0, in1=f_bank[:, :],
                                                   op0=ALU.add, op1=ALU.mult).then_inc(s["fusion_taken"], 1)
                    wait(dve, "fusion_taken", base + 1)
                    nc.vector.reciprocal(eq[:, :, :], eq[:, :, :]).then_inc(s["den_inverted"], 1)
                if name == "num":
                    wait(dve, "fusion_full", base + 1)
                    wait(dve, "den_inverted", b + 1)
                    nc.vector.tensor_tensor(flat(yT[:, :, :]), f_bank[:, :], flat(eq[:, :, :]), ALU.mult).then_inc(s["fusion_taken"], 1)
                if name == "aft":
                    wait(dve, "fusion_full", base + 1)
                    wait(dve, "xr_biased", LT * (b + 1))
                    wait(dve, "hb_done", b)
                    nc.vector.tensor_tensor(flat(h[:, 0:LT, :]), f_bank[:, :], flat(xr[:, :, :]), ALU.add).then_inc(s["fusion_taken"], 1)
                    wait(dve, "fusion_taken", base + 1)
                    for t in range(LT):
                        nc.vector.bn_stats(st_a[:, t, :], h[:, t, :]).then_inc(s["st_a_done"], 1)
                    for t in range(LT):
                        wait_apart(dve, "st_a_done", LT * b + t + 1)
                        nc.vector.bn_aggr(mv_a[:, t, :], st_a[:, t, :]).then_inc(s["mv_a_done"], 1)
                if name == "aft_norm":
                    wait(dve, "r_a_done", b + 1)
                    for t in range(LT):
                        nc.vector.tensor_scalar(h[:, t, :], h[:, t, :], mv_a[:, t, 0:1], r_a[:, t:t + 1], ALU.subtract, ALU.mult)\
                            .then_inc(s["h_norm"], 1)
                if name == "stats":
                    wait(dve, "fusion_taken", N_FUSION * b + FUSION_AT["text"] + 2)
                    wait(dve, "h_gained", LT * (b + 1))
                    for t in range(NT):
                        nc.vector.bn_stats(st_b[:, t, :], h[:, t, :]).then_inc(s["st_b_done"], 1)
                    for t in range(NT):
                        wait(dve, "st_b_done", NT * b + t + 1)
                        wait_apart(dve, "hb_step", 6 * b)
                        nc.vector.bn_aggr(mv_b[:, t, :], st_b[:, t, :]).then_inc(s["mv_b_done"], 1)
                if name == "zn":
                    wait(dve, "r_b_done", b + 1)
                    wait(dve, "fusion_full", N_FUSION * b + FUSION_AT["num"] + 1)
                    for t in range(NT):
                        nc.vector.tensor_scalar(zn[:, t, :], h[:, t, :], mv_b[:, t, 0:1], r_bc[:, t:t + 1], ALU.subtract, ALU.mult)\
                            .then_inc(s["zn_done"], 1)
                if name[:2] == "qk":
                    n = int(name[2])
                    wait(dve, "hi_done", 4 * b + n + 1)
                    nc.vector.tensor_tensor(lo[:, n % 2, :], f_bank[:, 0:N], hi[:, n % 2, :].bitcast(F32), ALU.subtract).then_inc(s["fusion_taken"], 1)

            def finish_task(name, b):
                base = N_FINISH * b + FINISH_AT[name]
                if name[:2] == "ot":
                    g = int(name[2])
                    v = n_bank[:, 0:N].rearrange("p (t k c) -> p t k c", t=NT, k=GRP)
                    wait(dve, "finish_full", base + 1)
                    nc.vector.reciprocal(rden[:, :, :], v[:, :, :, HD]).then_inc(s["rden_done"], 1)
                    wait(dve, "rden_done", NG * b + g + 1)
                    nc.vector.tensor_tensor(oN[:, :, g * GRP * HD:(g + 1) * GRP * HD].rearrange("p t (k d) -> p t k d", k=GRP), v[:, :, :, 0:HD],
                                            rden[:, :, :, None].broadcast_to([P, NT, GRP, HD]), ALU.mult).then_inc(s["finish_taken"], 1)
                if name[:4] == "proj":
                    t0, t1 = ((0, 2), (2, 3))[int(name[4])]
                    wait(dve, "finish_full", base + 1)
                    wait(dve, "hb_back", 16 * (b + 1))
                    nc.vector.tensor_tensor(h1[:, t0:t1, :], n_bank[:, 0:(t1 - t0) * D].rearrange("p (t d) -> p t d", d=D), h1[:, t0:t1, :], ALU.add)\
                        .then_inc(s["finish_taken"], 1)
                    wait(dve, "finish_taken", base + 1)
                    for t in range(t0, t1):
                        nc.vector.bn_stats(st_d[:, t, :], h1[:, t, :]).then_inc(s["st_d_done"], 1)
                    for t in range(t0, t1):
                        wait_apart(dve, "st_d_done", NT * b + t + 1)
                        nc.vector.bn_aggr(mv_d[:, t, :], st_d[:, t, :]).then_inc(s["mv_d_done"], 1)
                if name == "xn":
                    wait(dve, "r_d_done", b + 1)
                    wait(dve, "scattered", 16 * NT * b)
                    for t in range(NT):
                        last = nc.vector.tensor_scalar(xn[:, t, :], h1[:, t, :], mv_d[:, t, 0:1], r_d[:, t:t + 1], ALU.subtract, ALU.mult)
                    last.then_inc(s["xn_done"], 1)
                if name == "route":
                    wait(dve, "finish_full", base + 1)
                    nc.vector.tensor_copy(flat(lg[:, :, :]), n_bank[:, 0:NT * EXPERTS]).then_inc(s["finish_taken"], 1)
                    wait_apart(dve, "finish_taken", base + 1)
                    for t in range(NT):
                        last = nc.vector.max(m8[:, t, :], lg[:, t, :])
                    last.then_inc(s["m8_done"], 1)
                    wait(dve, "m8_done", b + 1)
                    nc.vector.tensor_tensor(df[:, :, :], lg[:, :, :], m8[:, :, 0:1].broadcast_to([P, NT, EXPERTS]), ALU.subtract).then_inc(s["df_done"], 1)
                    for t in range(NT):
                        last = nc.vector.max_index(i8[:, t, :], m8[:, t, :], lg[:, t, :])
                    last.then_inc(s["i8_done"], 1)
                    wait(dve, "i8_done", b + 1)
                    nc.vector.tensor_copy(ei[:, :], i8[:, :, 0]).then_inc(s["ei_done"], 1)
                    wait(dve, "ei_done", b + 1)
                    nc.vector.tensor_tensor(oh[:, :, :], iota8[:, None, :].broadcast_to([P, NT, EXPERTS]),
                                            ei[:, :, None].broadcast_to([P, NT, EXPERTS]), ALU.is_equal).then_inc(s["oh_done"], 1)
                    wait(dve, "run_done", (NT + 1) * b)
                    nc.vector.tensor_copy(run[:, 0, :], run[:, NT, :]).then_inc(s["run_done"], 1)
                    wait(dve, "oh_done", b + 1)
                    for t in range(NT):
                        wait(dve, "run_done", (NT + 1) * b + t + 1)
                        nc.vector.tensor_tensor(run[:, t + 1, :], run[:, t, :], oh[:, t, :], ALU.add).then_inc(s["run_done"], 1)
                if name == "pick":
                    wait(dve, "ex_done", b + 1)
                    nc.vector.reduce_sum(se[:, :], ex[:, :, :], axis=AX.X).then_inc(s["se_done"], 1)
                    wait(dve, "se_done", 2 * b + 1)
                    nc.vector.reciprocal(se[:, :], se[:, :]).then_inc(s["se_done"], 1)
                if name == "count":
                    wait(dve, "finish_full", base + 1)
                    nc.vector.tensor_tensor(cp[:, :, :], n_bank[:, 0:NT * EXPERTS].rearrange("p (t e) -> p t e", e=EXPERTS), oh[:, :, :], ALU.mult)\
                        .then_inc(s["finish_taken"], 1)
                if name == "slots":
                    def done(i):
                        return 6 * b + i
                    wait(dve, "finish_taken", base)
                    nc.vector.reduce_sum(pos[:, :], cp[:, :, :], axis=AX.X).then_inc(s["slot_step"], 1)
                    wait(dve, "slot_step", done(1))
                    nc.vector.tensor_scalar(keep[:, :], pos[:, :], float(CAP), None, ALU.is_le).then_inc(s["slot_step"], 1)
                    nc.vector.scalar_tensor_tensor(out=slot[:, :], in0=ei[:, :], scalar=float(CAP), in1=pos[:, :], op0=ALU.mult, op1=ALU.add)\
                        .then_inc(s["slot_step"], 1)
                    wait(dve, "slot_step", done(3))
                    nc.vector.scalar_tensor_tensor(out=sk[:, :], in0=slot[:, :], scalar=-1.0, in1=keep[:, :], op0=ALU.add, op1=ALU.mult)\
                        .then_inc(s["slot_step"], 1)
                    nc.vector.tensor_scalar(drop[:, :], keep[:, :], -1.0, 1.0, ALU.mult, ALU.add).then_inc(s["slot_step"], 1)
                    wait(dve, "slot_step", done(5))
                    nc.vector.tensor_tensor(drop[:, :], drop[:, :], trash[:, bass.ds(b * NT, NT)], ALU.mult).then_inc(s["slot_step"], 1)
                    nc.vector.tensor_copy(gidx[:, bass.ds(b * NT, NT)], sk[:, :])
                    wait(dve, "se_done", 2 * b + 2)
                    nc.vector.tensor_tensor(gate[:, bass.ds(b * NT, NT)], keep[:, :], se[:, :], ALU.mult).then_inc(s["gate_done"], 1)
                    wait(dve, "slot_step", done(6))
                    nc.vector.tensor_tensor(si[:, :], sk[:, :], drop[:, :], ALU.add).then_inc(s["slots_done"], 1)

            def body(it, par, pair, fusion, shift, attend, finish):
                for step in range(NH):
                    if shift:
                        for t in range(NT):
                            n = step * NT + t
                            wait(dve, "s_full", NH * NT * (it + 1) + n + 1)
                            nc.vector.reduce_max(mx[:, t, step:step + 1], s_bank[n % SRING][:, 0:N], axis=AX.X).then_inc(s["s_taken"], 1)
                    if fusion:
                        for name in FUSION_SLOTS.get(step, ()):
                            fusion_task(name, it + 2)
                    if finish:
                        for name in FINISH_SLOTS.get(step, ()):
                            finish_task(name, it - 1)
                if shift:
                    b = it + 1
                    wait(dve, "s_taken", NH * NT * (b + 1))
                    wait(dve, "m_full", b)
                    nc.vector.tensor_scalar(nmx[:, :, 0, :].bitcast(F32R), mx[:, :, :], -1.0, None, ALU.mult).then_inc(s["nmx_hi"], 1)
                    wait(dve, "nmx_hi", b + 1)
                    nc.vector.scalar_tensor_tensor(out=nmx[:, :, 1, :].bitcast(F32R), in0=mx[:, :, :], scalar=-1.0, in1=nmx[:, :, 0, :],
                                                   op0=ALU.mult, op1=ALU.subtract).then_inc(s["nmx_done"], 1)
                    wait(dve, "m_full", b + 1)
                    if attend:
                        wait(dve, m_loaded[par], 64 * (pair(0) + 1))
                    nc.vector.tensor_copy(mT[:, :], f_bank[0:2 * NH, 0:N]).then_inc(s["m_taken"], 1)

            pipeline(dve, body)

            def expert(e, par, pair):
                if is_real(e):
                    for i in range(DT):
                        wait(dve, "xeT_full", 2 * e + i + 1)
                        wait(dve, "hid_full", FT * e)
                        nc.vector.tensor_copy(xeT[:, i, :], f_bank[:, 0:CAP]).then_inc(s["xeT_taken"], 1)
                if is_real(e - 1):
                    for part, (t0, t1) in enumerate(((0, 2), (2, 3))):
                        wait(dve, "y_full", 2 * (e - 1) + part + 1)
                        wait(dve, "ye_stored", 16 * (e - 1))
                        nc.vector.tensor_copy(ye[:, t0:t1, :], s_bank[part][:, 0:(t1 - t0) * D].rearrange("p (t d) -> p t d", d=D))\
                            .then_inc(s["y_taken"], 1)

            over_experts(dve, expert)
            dve.wait_ge(s["h1_loaded"], 16)
            dve.wait_ge(s["gate_done"], B)
            for n in range(B * NT):
                dve.wait_ge(gathered[n % 4], 16 * (n // 4 + 1))
                nc.vector.scalar_tensor_tensor(out=h1f[:, n, :], in0=yg[:, n % 4, :], scalar=gate[:, n:n + 1], in1=h1f[:, n, :],
                                               op0=ALU.mult, op1=ALU.add).then_inc(s["combined"], 1)


def kernel(**inputs):
    import numpy as np

    import concourse.bacc as bacc
    from concourse.bass_utils import run_bass_kernel_spmd

    g = {k: np.asarray(v) for k, v in inputs.items()}
    heads = D // C
    x = g["x"]
    row = np.concatenate([np.tile(g["L0_tok_Wk_b"], heads), np.tile(g["L0_tok_Wv_b"], heads), g["L0_tok_out_b"], g["L0_tok_ln_g"],
                          g["L0_tok_ln_b"], g["L0_attn_b_proj"]])
    w5 = g["L0_attn_w_qkv"].reshape(D, NH, HD, 3)
    w_qkv = np.concatenate([w5[..., 0].transpose(0, 2, 1).reshape(D, D), w5[..., 1].transpose(0, 2, 1).reshape(D, D),
                            w5[..., 2].reshape(D, D)], axis=1)
    arrays = {
        "x_cl": x.transpose(0, 3, 1, 2).reshape(B, D, L),
        "x_lc": x.transpose(0, 2, 3, 1).reshape(B, L, D),
        "tokens": g["x_txt"].T,
        "rows": np.broadcast_to(row, (P, row.size)),
        "cols": np.stack([g["L0_attn_ln_scale"].reshape(DT, P).T, g["L0_attn_ln_bias"].reshape(DT, P).T], axis=1),
        "bq": g["L0_tok_Wq_b"].reshape(C, 1),
        "WkT": g["L0_tok_Wk_w"].T, "WvT": g["L0_tok_Wv_w"].T, "WqT": g["L0_tok_Wq_w"].T,
        "w_biasT": g["L0_tok_w_bias"].T, "maskT": g["L0_tok_local_mask"].T,
        "out_w": g["L0_tok_out_w"],
        "E0": g["L0_txt_E0"], "E1": g["L0_txt_E1"], "E2": g["L0_txt_E2"],
        "W0": g["L0_txt_W0"], "W1": g["L0_txt_W1"], "W2": g["L0_txt_W2"],
        "w_qkv": w_qkv, "w_proj": g["L0_attn_w_proj"],
        "router_w": g["L0_ffn_router_w"], "w1": g["L0_ffn_w1"], "w2": g["L0_ffn_w2"],
    }
    nc = bacc.Bacc("TRN2", target_bir_lowering=False, num_devices=1)
    nc.disable_value_cache = True
    feeds, aps = {}, {}
    for name, array in arrays.items():
        array = np.ascontiguousarray(array)
        feeds[f"in_{name}"] = array
        aps[name] = nc.dram_tensor(f"in_{name}", list(array.shape), mybir.dt.from_np(array.dtype), kind="ExternalInput").ap()
    out = nc.dram_tensor("out", [B, N, D], F32, kind="ExternalOutput").ap()
    early_fusion_kernel(nc, aps, out)
    result = run_bass_kernel_spmd(nc, [feeds], core_ids=[0])
    return result.results[0]["out"]
```

```python
from contextlib import ExitStack

import concourse.bass as bass
from concourse import mybir

F32 = mybir.dt.float32
F32R = mybir.dt.float32r
I32 = mybir.dt.int32
U32 = mybir.dt.uint32
U8 = mybir.dt.uint8
ALU = mybir.AluOpType
ACT = mybir.ActivationFunctionType
AX = mybir.AxisListType

P = 128
B = 8
L = 256
LT = L // P
C = 64
D = 256
DT = D // P
N = 384
NT = N // P
NH = 16
HD = 16
HALF = NH // 2
GRP = 4
NG = NH // GRP
VC = HD + 1
EXPERTS = 8
FF = 1024
FT = FF // P
TOK = B * N
CAP = TOK // EXPERTS
CT = CAP // P
EPS = 1e-5
BANDS = [0, 5000, 10000, 50257]
SCALE = 1.0 / (D / NH) ** 0.5
PRING = 16
SRING = 2
TRING = 2

STEPS = NH * NT
LAG = 1
FUSION_SLOTS = {0: "kv0", 1: "ekv0", 2: "kv1", 3: "ekv1", 4: "q", 6: "den", 7: "inv0", 8: "inv1", 9: "inv2", 10: "inv3", 11: "num",
                13: "aft", 14: "aft_stats", 15: "text_t", 17: "text", 18: "aft_norm0", 19: "aft_norm1", 20: "stats2", 22: "stats0", 23: "stats1",
                26: "zn0", 27: "zn1", 28: "zn2", 30: "zt0", 32: "zt1", 34: "qk0", 36: "qk1", 38: "qk2", 40: "qk3"}
FINISH_SLOTS = {1: "ot0", 3: "ot1", 5: "ot2", 7: "ot3", 9: "ont0", 11: "ont1", 14: "proj0", 16: "proj1", 20: "xn0", 21: "xn1", 22: "xn2",
                23: "xt0", 25: "xt1", 28: "route", 29: "best", 30: "chosen", 31: "totals", 32: "pick", 33: "count", 35: "slots"}
NOT_IN_BANK = ("ekv0", "ekv1", "inv0", "inv1", "inv2", "inv3", "aft_stats", "aft_norm0", "aft_norm1", "stats0", "stats1", "stats2",
               "zn0", "zn1", "zn2", "xn0", "xn1", "xn2", "best", "chosen", "totals", "pick", "slots")
MAX1_AT, V_AT, MAX0_AT = 3, (20, 22), 28


def bank_positions(slots):
    place, at = {}, 0
    for name in slots.values():
        place[name] = at
        at += name not in NOT_IN_BANK
    return place, at


FUSION_AT, N_FUSION = bank_positions(FUSION_SLOTS)
FINISH_AT, N_FINISH = bank_positions(FINISH_SLOTS)


def early_fusion_kernel(nc, a, out):
    x_cl, x_lc, tokens = a["x_cl"], a["x_lc"], a["tokens"]
    E = [a["E0"], a["E1"], a["E2"]]

    qk_dram = nc.dram_tensor("qk_parts", [2, 2, 2, 2, P, N], F32, kind="Internal").ap()
    hb_dram = nc.dram_tensor("residual_in", [B, N, D], F32, kind="Internal").ap()
    h1_dram = nc.dram_tensor("residual_out", [TOK, D], F32, kind="Internal").ap()
    xe_dram = nc.dram_tensor("expert_in", [2 * TOK, D], F32, kind="Internal").ap()
    ye_dram = nc.dram_tensor("expert_out", [TOK, D], F32, kind="Internal").ap()

    with ExitStack() as ctx:
        def sb(name, shape, dt=F32):
            return ctx.enter_context(nc.sbuf_tensor(name, shape, dt))

        def bank(name):
            return ctx.enter_context(nc.psum_tensor(name, [P, 512], F32))

        def sem(name):
            return ctx.enter_context(nc.semaphore(name))

        ident = sb("ident", [P, P])
        upper = sb("upper", [P, P])
        ones = sb("ones", [P, P])
        wkv = sb("wkv", [P, 2, P])
        wq = sb("wq", [P, P])
        nbq = sb("nbq", [P, 1])
        rows = sb("rows", [P, 1536])
        kv_bias, out_b = rows[:, 0:512], rows[:, 512:768]
        ln_g, ln_b, b_proj = rows[:, 768:1024], rows[:, 1024:1280], rows[:, 1280:1536]
        ewT = sb("ewT", [P, LT, L])
        out_w = sb("out_w", [P, DT, D])
        w_txt = sb("w_txt", [P, 3, D])
        cols = sb("cols", [P, 2, DT])
        w_qkv = sb("w_qkv", [P, DT, 3 * D])
        w_proj = sb("w_proj", [P, DT, D])
        w_r = sb("w_r", [P, DT, EXPERTS])
        mhalf = sb("mhalf", [P, NT])
        iota8 = sb("iota8", [P, EXPERTS])
        trash = sb("trash", [P, B * NT])
        mask8 = sb("mask8", [P, LT, L], U8)
        gi = sb("gi", [P, 3], I32)
        msk = sb("msk", [P, 3])
        tok_i = sb("tok_i", [P, B], I32)
        tok_f = sb("tok_f", [P, B])
        rel_f = sb("rel_f", [P, 3, B])
        rel_i = sb("rel_i", [P, 3, B], I32)
        band = sb("band", [P, 3, B])
        band_t = sb("band_t", [P, 3, B])
        xc = sb("xc", [P, DT, L])
        xr = sb("xr", [P, LT, D])
        emb = sb("emb", [P, N])
        kvs = sb("kvs", [P, 512])
        embT = kvs[:, 0:N]
        ekv = sb("ekv", [P, LT, 512])
        zn = ekv[:, :, :].rearrange("p a b -> p (a b)")[:, 0:NT * D].rearrange("p (t d) -> p t d", t=NT)
        eq = sb("eq", [P, DT, L])
        yT = sb("yT", [P, DT, L])
        h = sb("h", [P, NT, D])
        hb = sb("hb", [P, NT, D])
        st_a = sb("st_a", [P, LT, 6])
        mv_a = sb("mv_a", [P, LT, 2])
        r_a = sb("r_a", [P, LT])
        st_b = sb("st_b", [P, NT, 6])
        mv_b = sb("mv_b", [P, NT, 2])
        r_b = sb("r_b", [P, NT])
        r_c = sb("r_c", [P, NT])
        r_bc = sb("r_bc", [P, NT])
        zT = sb("zT", [P, DT, N])
        hi = sb("hi", [P, 2, N], F32R)
        lo = sb("lo", [P, 2, N], F32R)
        v_aug = sb("v_aug", [P, 2, NT, NH, VC])
        mx = sb("mx", [P, NT, NH])
        nmx = sb("nmx", [P, NT, 2, 2, HALF])
        mT = sb("mT", [2 * HALF, 2, N], F32R)
        probs = sb("probs", [P, PRING, N])
        oS = sb("oS", [P, NG, N])
        rden = sb("rden", [P, NT, GRP])
        oN = sb("oN", [P, NT, D])
        tT = sb("tT", [P, DT, N])
        h1 = sb("h1", [P, NT, D])
        st_d = sb("st_d", [P, NT, 6])
        mv_d = sb("mv_d", [P, NT, 2])
        r_d = sb("r_d", [P, NT])
        xn = sb("xn", [P, NT, D])
        lg = sb("lg", [P, NT, EXPERTS])
        m8 = sb("m8", [P, NT, 8])
        i8 = sb("i8", [P, NT, 8], U32)
        ei = sb("ei", [P, NT])
        oh = sb("oh", [P, NT, EXPERTS])
        df = sb("df", [P, NT, EXPERTS])
        ex = sb("ex", [P, NT, EXPERTS])
        se = sb("se", [P, NT])
        run = sb("run", [P, NT + 1, EXPERTS])
        cp = sb("cp", [P, NT, EXPERTS])
        pos = sb("pos", [P, NT])
        keep = sb("keep", [P, NT])
        slot = sb("slot", [P, NT])
        sk = sb("sk", [P, NT])
        drop = sb("drop", [P, NT])
        si = sb("si", [P, NT], I32)
        gate = sb("gate", [P, B * NT])
        gidx = sb("gidx", [P, B * NT], I32)
        stacks = ExitStack()
        qst = stacks.enter_context(nc.sbuf_tensor("qst", [P, 4, HALF, N], F32R))
        kst = stacks.enter_context(nc.sbuf_tensor("kst", [P, 4, HALF, N], F32R))
        stacks.close()
        w1s = [sb(f"w1s{i}", [P, DT, FF]) for i in range(2)]
        w2s = [sb(f"w2s{i}", [P, FT, D]) for i in range(2)]
        hid = [sb(f"hid{i}", [P, FT, CAP]) for i in range(2)]
        h1f = sb("h1f", [P, B * NT, D])
        xe = [sb(f"xe{i}", [P, CT, D])[:, :, :] for i in range(2)]
        xeT = sb("xeT", [P, DT, CAP])
        ye = sb("ye", [P, CT, D])[:, :, :]
        yg = probs[:, :, :].rearrange("p a b -> p (a b)")[:, 0:4 * D].rearrange("p (n d) -> p n d", n=4)

        s_bank = [bank(f"s_bank{i}") for i in range(SRING)]
        t_bank = [bank(f"t_bank{i}") for i in range(TRING)]
        o_bank = bank("o_bank")
        f_bank = bank("f_bank")
        v_bank = bank("v_bank")
        n_bank = bank("n_bank")

        names = """waits_apart consts_loaded tok_loaded mask_loaded zeroed mhalf_done ident_done upper_done iota_done trash_done counts_zeroed
        stacks_zeroed stacks_ready v_ones_done o_bank_cleared wmask_done ewT_done nbq_done band_steps bands_done xe_cleared
        xc_loaded xr_loaded xr_biased emb_loaded emb_masked index_done
        ek_done ekv_done den_inverted st_a_done mv_a_done r_a_step r_a_done h_norm h_scaled h_gained
        st_b_done mv_b_done r_b_step r_b_done zn_done hb_step hb_done hb_stored hi_done
        fusion_full fusion_taken v_full v_taken s_full s_taken nmx_hi nmx_done m_full m_taken
        t_full p_ready o_full o_taken
        finish_full finish_taken rden_done hb_back h1_stored st_d_done mv_d_done r_d_step r_d_done xn_done
        m8_done df_done ex_done i8_done ei_done oh_done run_done se_done slot_step gate_done slots_done scattered
        xeT_full xeT_taken hid_full hid_taken y_full y_taken ye_stored h1_loaded combined out_stored""".split()
        s = {n: sem(n) for n in names}
        part_stored = [sem("part_stored0"), sem("part_stored1")]
        qk_loaded = [[sem(f"qk_loaded{p}{q}") for q in range(2)] for p in range(2)]
        m_loaded = [[sem(f"m_loaded{p}{q}") for q in range(2)] for p in range(2)]
        w1_loaded = [sem("w1_loaded0"), sem("w1_loaded1")]
        w2_loaded = [sem("w2_loaded0"), sem("w2_loaded1")]
        xe_loaded = [sem("xe_loaded0"), sem("xe_loaded1")]
        gathered = [sem(f"gathered{i}") for i in range(4)]
        N_CONSTS = 17

        block = ctx.enter_context(nc.Block())

        def wait(eng, name, value):
            if not (isinstance(value, int) and value <= 0):
                eng.wait_ge(s[name] if isinstance(name, str) else name, value)

        def wait_apart(eng, name, value):
            wait(eng, name, value)
            if not isinstance(value, int):
                eng.sem_inc(s["waits_apart"], 1)

        def pipeline(eng, body):
            def one(it):
                body(it, it % 2, lambda k: (it + k) // 2, it + 2 < B, 0 <= it + 1 < B, 0 <= it < B, it >= 1)
            for it in range(-2, 2):
                one(it)
            with eng.Fori(1, (B - 2) // 2) as j:
                for i in range(2):
                    body(j * 2 + i, i, lambda k, i=i: j + (i + k) // 2, True, True, True, True)
            for it in range(B - 2, B + 1):
                one(it)

        def over_experts(eng, body):
            for e in (0, 1):
                body(e, e, 0)
            with eng.Fori(1, EXPERTS // 2) as j:
                for i in range(2):
                    body(j * 2 + i, i, j)
            for e in (EXPERTS, EXPERTS + 1):
                body(e, e % 2, e // 2)

        def is_real(e):
            return not isinstance(e, int) or 0 <= e < EXPERTS

        @block.sync
        def _(sp):
            for dst, src in ((rows[:, :], a["rows"]), (cols[:, :, :], a["cols"]), (nbq[0:C, :], a["bq"]), (nbq[C:P, :], a["bq"])):
                sp.dma_start(dst, src).then_inc(s["consts_loaded"], 16)
            sp.dma_start(tok_i[:, :], tokens).then_inc(s["tok_loaded"], 16)
            sp.dma_start(xc[:, :, :], x_cl[0].rearrange("(t p) l -> p t l", p=P)).then_inc(s["xc_loaded"], 16)
            sp.dma_start(xr[:, :, :], x_lc[0].rearrange("(t p) c -> p t c", p=P)).then_inc(s["xr_loaded"], 16)
            sp.wait_ge(s["zeroed"], 2)
            for i in range(2):
                d = slice(C * i, C * i + C)
                sp.dma_start(wkv[d, 0, d], a["WkT"]).then_inc(s["consts_loaded"], 16)
                sp.dma_start(wkv[d, 1, d], a["WvT"]).then_inc(s["consts_loaded"], 16)
                sp.dma_start(wq[d, d], a["WqT"]).then_inc(s["consts_loaded"], 16)
            for dst, src in (
                (out_w[:, :, :], a["out_w"].rearrange("(t p) n -> p t n", p=P)),
                (w_txt[:, 0:2, :], a["W0"].rearrange("(t p) n -> p t n", p=P)),
                (w_txt[0:64, 2, :], a["W1"]), (w_txt[64:128, 2, :], a["W2"]),
                (w_qkv[:, :, :], a["w_qkv"].rearrange("(t p) n -> p t n", p=P)),
                (w_proj[:, :, :], a["w_proj"].rearrange("(t p) n -> p t n", p=P)),
                (w_r[:, :, :], a["router_w"].rearrange("(t p) n -> p t n", p=P)),
            ):
                sp.dma_start(dst, src).then_inc(s["consts_loaded"], 16)
            sp.wait_ge(s["stacks_zeroed"], 2)
            for i in range(2):
                sp.dma_start(xe_dram[i * TOK // 2:(i + 1) * TOK // 2, :].rearrange("(p r) d -> p (r d)", p=32),
                             qst[96:P, :, :, :].bitcast(F32).rearrange("p a b c -> p (a b c)")).then_inc(s["xe_cleared"], 16)

            def load_maxima(b, par, half):
                wait_apart(sp, "m_taken", 2 * b + half + 1)
                for part in range(2):
                    sp.dma_start(qst[64 + part:65 + part, 2 * par + half, :, :].bitcast(F32),
                                 mT[part * HALF:(part + 1) * HALF, half, :].bitcast(F32)).then_inc(m_loaded[par][half], 16)

            def body(it, par, pair, fusion, shift, attend, finish):
                b = it + 2
                if finish:
                    bf = it - 1
                    wait_apart(sp, "h1_stored", bf * 16)
                    wait_apart(sp, "xn_done", bf)
                    sp.dma_start(h1[:, :, :], hb_dram[bf].rearrange("(t p) d -> p t d", p=P)).then_inc(s["hb_back"], 16)
                if attend:
                    load_maxima(it, par, 1)
                if fusion and not (isinstance(b, int) and b + 1 >= B):
                    after = b + 1 if isinstance(b, int) else (b + 1) % B
                    wait_apart(sp, "fusion_full", N_FUSION * b + FUSION_AT["q"] + 1)
                    sp.dma_start(xc[:, :, :], x_cl[after].rearrange("(t p) l -> p t l", p=P)).then_inc(s["xc_loaded"], 16)
                    wait_apart(sp, "fusion_taken", N_FUSION * b + FUSION_AT["aft"] + 1)
                    sp.dma_start(xr[:, :, :], x_lc[after].rearrange("(t p) c -> p t c", p=P)).then_inc(s["xr_loaded"], 16)
                if finish:
                    wait_apart(sp, "finish_taken", N_FINISH * bf + FINISH_AT["proj1"] + 1)
                    sp.dma_start(h1_dram[bass.ds(bf * N, N), :].rearrange("(t p) d -> p t d", p=P), h1[:, :, :]).then_inc(s["h1_stored"], 16)
                if fusion:
                    wait_apart(sp, "hb_done", b + 1)
                    sp.dma_start(hb_dram[b].rearrange("(t p) d -> p t d", p=P), hb[:, :, :]).then_inc(s["hb_stored"], 16)

                def load_stacks(half):
                    if attend:
                        wait_apart(sp, "t_full", NH * NT * it + (half + 1) * HALF * NT)
                    sl = 2 * par + half
                    q_rows, k_rows = (qk_dram[par, half, i].rearrange("s (d h) n -> (s d) h n", h=HALF) for i in range(2))
                    for stack, r0, r1, src in ((qst, 0, 32, q_rows), (qst, 32, 64, q_rows), (kst, 0, 32, k_rows),
                                               (kst, 32, 48, k_rows[16:32]), (kst, 48, 64, k_rows[0:16])):
                        sp.dma_start(stack[r0:r1, sl, :, :].bitcast(F32), src).then_inc(qk_loaded[par][half], 16)
                    sp.dma_start(qst[64:66, sl, :, :].bitcast(F32), kst[66:68, sl, :, :].bitcast(F32)).then_inc(qk_loaded[par][half], 16)

                def store_parts(half):
                    for n in (2 * half, 2 * half + 1):
                        wait_apart(sp, "hi_done", 4 * b + n + 1)
                        sp.dma_start(qk_dram[par, half, n % 2, 0], hi[:, n % 2, :].bitcast(F32)).then_inc(part_stored[n % 2], 16)
                        wait_apart(sp, "fusion_taken", N_FUSION * b + FUSION_AT[f"qk{n}"] + 1)
                        sp.dma_start(qk_dram[par, half, n % 2, 1], lo[:, n % 2, :].bitcast(F32)).then_inc(part_stored[n % 2], 16)
                    for n in range(2):
                        wait_apart(sp, part_stored[n], 64 * b + 32 * (half + 1))

                if fusion:
                    store_parts(0)
                    sp.wait_ge(s["stacks_ready"], 1)
                    load_stacks(0)
                if shift:
                    load_maxima(it + 1, 1 - par, 0)
                if fusion:
                    store_parts(1)
                    load_stacks(1)

            pipeline(sp, body)

            sp.wait_ge(s["t_full"], B * NH * NT)
            sp.wait_ge(s["h1_stored"], 16 * B)
            sp.dma_start(h1f[:, :, :], h1_dram.rearrange("(n p) d -> p n d", p=P)).then_inc(s["h1_loaded"], 16)
            sp.wait_ge(s["scattered"], 16 * B * NT)

            def expert(e, par, pair):
                if is_real(e):
                    wait_apart(sp, "xeT_full", 2 * (e - 1))
                    sp.dma_start(xe[par], xe_dram[bass.ds(e * CAP, CAP), :].rearrange("(t p) d -> p t d", p=P)).then_inc(xe_loaded[par], 16)
                    wait_apart(sp, "hid_full", FT * (e - 1))
                    sp.dma_start(w1s[par][:, :, :], a["w1"][e].rearrange("(t p) f -> p t f", p=P)).then_inc(w1_loaded[par], 16)
                    wait_apart(sp, "y_full", 2 * (e - 1))
                    sp.dma_start(w2s[par][:, :, :], a["w2"][e].rearrange("(t p) d -> p t d", p=P)).then_inc(w2_loaded[par], 16)
                if is_real(e - 2) and not (isinstance(e, int) and e < 2):
                    wait_apart(sp, "y_taken", 2 * (e - 1))
                    sp.dma_start(ye_dram[bass.ds((e - 2) * CAP, CAP), :].rearrange("(t p) d -> p t d", p=P), ye).then_inc(s["ye_stored"], 16)

            over_experts(sp, expert)
            for b in range(B):
                sp.wait_ge(s["combined"], (b + 1) * NT)
                sp.dma_start(out[b].rearrange("(t p) d -> p t d", p=P), h1f[:, b * NT:(b + 1) * NT, :]).then_inc(s["out_stored"], 16)
            sp.wait_ge(s["out_stored"], 16 * B)

        @block.gpsimd
        def _(pool):
            pool.memset(wkv[:, :, :], 0.0).then_inc(s["zeroed"], 1)
            pool.memset(wq[:, :], 0.0).then_inc(s["zeroed"], 1)
            pool.memset(ident[:, :], 0.0).then_inc(s["zeroed"], 1)
            pool.memset(ones[:, :], 1.0).then_inc(s["zeroed"], 1)
            pool.memset(mhalf[:, :], -0.5).then_inc(s["mhalf_done"], 1)
            pool.wait_ge(s["zeroed"], 4)
            pool.affine_select(out=ident[:, :], in_=ident[:, :], compare_op=ALU.not_equal, fill=1.0, base=0,
                               pattern=[[-1, P]], channel_multiplier=1).then_inc(s["ident_done"], 1)
            pool.affine_select(out=upper[:, :], in_=ones[:, :], compare_op=ALU.is_ge, fill=0.0, base=0,
                               pattern=[[1, P]], channel_multiplier=-1).then_inc(s["upper_done"], 1)
            pool.iota(iota8[:, :], pattern=[[1, EXPERTS]], base=0, channel_multiplier=0,
                      allow_small_or_imprecise_dtypes=True).then_inc(s["iota_done"], 1)
            pool.iota(trash[:, :], pattern=[[P, B * NT]], base=TOK, channel_multiplier=1,
                      allow_small_or_imprecise_dtypes=True).then_inc(s["trash_done"], 1)
            pool.memset(run[:, NT, :], 0.0).then_inc(s["counts_zeroed"], 1)

            def gather(b):
                wait(pool, "bands_done", 1)
                wait_apart(pool, "emb_masked", 3 * b)
                wait_apart(pool, "fusion_full", N_FUSION * (b - 1) + FUSION_AT["text_t"] + 1)
                pool.tensor_copy(gi[:, :], rel_i[:, :, bass.ds(b, 1)].rearrange("p a b -> p (a b)")).then_inc(s["index_done"], 1)
                pool.tensor_copy(msk[:, :], band[:, :, bass.ds(b, 1)].rearrange("p a b -> p (a b)")).then_inc(s["index_done"], 1)
                wait_apart(pool, "index_done", 2 * b + 2)
                for i, (c0, c1) in enumerate(((0, 256), (256, 320), (320, 384))):
                    pool.indirect_dma_start(emb[:, c0:c1], None, E[i], bass.IndirectOffsetOnAxis(ap=gi[:, i:i + 1], axis=0))\
                        .then_inc(s["emb_loaded"], 16)

            pool.wait_ge(s["counts_zeroed"], 1)
            pool.memset(qst[64:P, :, :, :].bitcast(F32), 0.0).then_inc(s["stacks_zeroed"], 1)
            pool.memset(kst[64:P, :, :, :].bitcast(F32), 0.0).then_inc(s["stacks_zeroed"], 1)
            pool.wait_ge(s["stacks_zeroed"], 2)
            pool.memset(kst[64:66, :, :, :].bitcast(F32), 1.0).then_inc(s["stacks_ready"], 1)
            pool.wait_ge(s["stacks_ready"], 1)
            pool.memset(v_aug[:, :, :, :, HD:VC], 1.0).then_inc(s["v_ones_done"], 1)
            pool.wait_ge(s["consts_loaded"], 16 * N_CONSTS)
            pool.wait_ge(s["mhalf_done"], 1)

            def body(it, par, pair, fusion, shift, attend, finish):
                if fusion:
                    b = it + 2
                    gather(b)
                    wait(pool, "xr_loaded", 16 * (b + 1))
                    for t in range(LT):
                        pool.tensor_tensor(xr[:, t, :], xr[:, t, :], out_b, ALU.add).then_inc(s["xr_biased"], 1)
                    wait_apart(pool, "emb_loaded", 48 * (b + 1))
                    for i, (c0, c1) in enumerate(((0, 256), (256, 320), (320, 384))):
                        pool.tensor_scalar(emb[:, c0:c1], emb[:, c0:c1], msk[:, i:i + 1], None, ALU.mult).then_inc(s["emb_masked"], 1)
                    wait_apart(pool, "mv_a_done", LT * (b + 1))
                    pool.tensor_scalar(r_a[:, :], mv_a[:, :, 1], EPS, None, ALU.add).then_inc(s["r_a_step"], 1)
                    wait(pool, "r_a_step", b + 1)
                    pool.tensor_tensor(r_a[:, :], r_a[:, :], mhalf[:, 0:LT], ALU.pow).then_inc(s["r_a_done"], 1)
                if finish:
                    b = it - 1
                    wait(pool, "mv_d_done", NT * (b + 1))
                    wait_apart(pool, "xn_done", b)
                    pool.tensor_scalar(r_d[:, :], mv_d[:, :, 1], EPS, None, ALU.add).then_inc(s["r_d_step"], 1)
                    wait(pool, "r_d_step", b + 1)
                    pool.tensor_tensor(r_d[:, :], r_d[:, :], mhalf[:, :], ALU.pow).then_inc(s["r_d_done"], 1)
                if fusion:
                    b = it + 2
                    for t in range(LT):
                        wait(pool, "h_norm", LT * b + t + 1)
                        pool.tensor_tensor(h[:, t, :], h[:, t, :], ln_g, ALU.mult).then_inc(s["h_scaled"], 1)
                    for t in range(LT):
                        wait(pool, "h_scaled", LT * b + t + 1)
                        pool.tensor_tensor(h[:, t, :], h[:, t, :], ln_b, ALU.add).then_inc(s["h_gained"], 1)
                    wait_apart(pool, "mv_b_done", NT * (b + 1))
                    pool.tensor_scalar(r_b[:, :], mv_b[:, :, 1], EPS, None, ALU.add).then_inc(s["r_b_step"], 1)
                    wait(pool, "r_b_step", 6 * b + 1)
                    pool.tensor_tensor(r_b[:, :], r_b[:, :], mhalf[:, :], ALU.pow).then_inc(s["r_b_step"], 1)
                    wait(pool, "r_b_step", 6 * b + 2)
                    pool.tensor_tensor(r_c[:, :], r_b[:, :], r_b[:, :], ALU.mult).then_inc(s["r_b_step"], 1)
                    wait(pool, "r_b_step", 6 * b + 3)
                    pool.tensor_tensor(r_c[:, :], r_c[:, :], mv_b[:, :, 1], ALU.mult).then_inc(s["r_b_step"], 1)
                    wait_apart(pool, "r_b_step", 6 * b + 4)
                    pool.tensor_scalar(r_c[:, :], r_c[:, :], EPS, None, ALU.add).then_inc(s["r_b_step"], 1)
                    wait(pool, "r_b_step", 6 * b + 5)
                    pool.tensor_tensor(r_c[:, :], r_c[:, :], mhalf[:, :], ALU.pow).then_inc(s["r_b_step"], 1)
                    wait(pool, "r_b_step", 6 * b + 6)
                    wait(pool, "zn_done", NT * b)
                    pool.tensor_tensor(r_bc[:, :], r_b[:, :], r_c[:, :], ALU.mult).then_inc(s["r_b_done"], 1)
                    wait_apart(pool, "hb_stored", 16 * b)
                    for t in range(NT):
                        pool.tensor_scalar(hb[:, t, :], h[:, t, :], mv_b[:, t, 0:1], r_b[:, t:t + 1], ALU.subtract, ALU.mult)\
                            .then_inc(s["hb_step"], 1)
                    for t in range(NT):
                        wait(pool, "hb_step", 6 * b + t + 1)
                        pool.tensor_tensor(hb[:, t, :], hb[:, t, :], h[:, t, :], ALU.add).then_inc(s["hb_step"], 1)
                    for t in range(NT):
                        wait(pool, "hb_step", 6 * b + NT + t + 1)
                        last = pool.tensor_tensor(hb[:, t, :], hb[:, t, :], b_proj, ALU.add)
                    last.then_inc(s["hb_done"], 1)
                if finish:
                    b = it - 1
                    pool.wait_ge(s["xe_cleared"], 32)
                    wait_apart(pool, "slots_done", b + 1)
                    for t in range(NT):
                        pool.indirect_dma_start(xe_dram, bass.IndirectOffsetOnAxis(ap=si[:, t:t + 1], axis=0), xn[:, t, :], None)\
                            .then_inc(s["scattered"], 16)

            pipeline(pool, body)

            pool.wait_ge(s["o_full"], NG * B)
            pool.wait_ge(s["slots_done"], B)
            pool.wait_ge(s["ye_stored"], 16 * EXPERTS)
            for n in range(B * NT):
                wait_apart(pool, "combined", n - 3)
                pool.indirect_dma_start(yg[:, n % 4, :], None, ye_dram, bass.IndirectOffsetOnAxis(ap=gidx[:, n:n + 1], axis=0))\
                    .then_inc(gathered[n % 4], 16)

        @block.scalar
        def _(act):
            act.dma_start(ewT[:, :, :], a["w_biasT"].rearrange("(t p) l -> p t l", p=P)).then_inc(s["mask_loaded"], 16)
            act.dma_start(mask8[:, :, :], a["maskT"].rearrange("(t p) l -> p t l", p=P)).then_inc(s["mask_loaded"], 16)
            act.wait_ge(s["wmask_done"], 2)
            nc.scalar.activation(ewT[:, :, :], ewT[:, :, :], ACT.Exp).then_inc(s["ewT_done"], 1)
            act.wait_ge(s["nbq_done"], 1)
            act.wait_ge(s["v_ones_done"], 1)

            def fusion_task(name, b):
                base = N_FUSION * b + FUSION_AT[name]
                if name in ("kv0", "kv1"):
                    t = int(name[2])
                    wait(act, "fusion_taken", base + 1)
                    nc.scalar.activation(ekv[:, t, 0:D], kvs[:, 0:D], ACT.Exp).then_inc(s["ek_done"], 1)
                if name == "q":
                    wait(act, "fusion_full", base + 1)
                    nc.scalar.activation(eq[:, :, :].rearrange("p a b -> p (a b)"), f_bank[:, :], ACT.Exp, bias=nbq[:, 0:1], scale=-1.0)\
                        .then_inc(s["fusion_taken"], 1)
                if name == "text_t":
                    wait(act, "fusion_full", base + 1)
                    wait(act, "ekv_done", LT * (b + 1))
                    nc.scalar.copy(embT, f_bank[:, 0:N]).then_inc(s["fusion_taken"], 1)
                if name == "text":
                    wait(act, "fusion_full", base + 1)
                    wait(act, "hb_done", b)
                    nc.scalar.copy(h[:, 2, :], f_bank[:, 0:D]).then_inc(s["fusion_taken"], 1)
                if name in ("zt0", "zt1"):
                    i = int(name[2])
                    wait(act, "fusion_full", base + 1)
                    wait(act, "v_full", 2 * b)
                    nc.scalar.activation(zT[:, i, :], f_bank[:, 0:N], ACT.Identity, bias=cols[:, 1, i:i + 1], scale=cols[:, 0, i:i + 1])\
                        .then_inc(s["fusion_taken"], 1)
                if name[:2] == "qk":
                    n = int(name[2])
                    wait(act, "fusion_full", base + 1)
                    wait(act, part_stored[n % 2], 64 * b + 32 * (n // 2))
                    nc.scalar.copy(hi[:, n % 2, :], f_bank[:, 0:N]).then_inc(s["hi_done"], 1)

            def finish_task(name, b):
                if name in ("ont0", "ont1", "xt0", "xt1"):
                    wait(act, "finish_full", N_FINISH * b + FINISH_AT[name] + 1)
                    nc.scalar.copy(tT[:, int(name[-1]), :], n_bank[:, 0:N]).then_inc(s["finish_taken"], 1)
                if name == "best":
                    wait(act, "df_done", b + 1)
                    nc.scalar.activation(ex[:, :, :], df[:, :, :], ACT.Exp).then_inc(s["ex_done"], 1)

            def body(it, par, pair, fusion, shift, attend, finish):
                def take_v(i):
                    t0, t1 = ((0, 2), (2, 3))[i]
                    wait(act, "v_full", 2 * (it + 1) + i + 1)
                    wait(act, "o_full", NG * it)
                    nc.scalar.copy(v_aug[:, 1 - par, t0:t1, :, 0:HD],
                                   v_bank[:, 0:(t1 - t0) * D].rearrange("p (t h d) -> p t h d", t=t1 - t0, d=HD)).then_inc(s["v_taken"], 1)

                def take_o(b, g):
                    wait(act, "o_full", NG * b + g + 1)
                    if g == 0:
                        wait(act, "finish_full", N_FINISH * (b - 1) + FINISH_AT["ot3"] + 1)
                    nc.scalar.copy(oS[:, g, :], o_bank[:, 0:N]).then_inc(s["o_taken"], 1)

                for n in range(STEPS):
                    if attend:
                        wait(act, "t_full", STEPS * it + n + 1)
                        wait(act, "o_full", NG * it + (n - PRING) // (GRP * NT) + 1)
                        nc.scalar.activation(probs[:, n % PRING, :], t_bank[n % TRING][:, 0:N], ACT.Exp, scale=SCALE)\
                            .then_inc(s["p_ready"], 1)
                    if n == NT + LAG and finish:
                        take_o(it - 1, NG - 1)
                    if n > NT + LAG and n % (GRP * NT) == NT + LAG and attend:
                        take_o(it, n // (GRP * NT) - 1)
                    if shift and n - LAG in V_AT:
                        take_v(V_AT.index(n - LAG))
                    if fusion and n - LAG in FUSION_SLOTS:
                        fusion_task(FUSION_SLOTS[n - LAG], it + 2)
                    if finish and n - LAG in FINISH_SLOTS:
                        finish_task(FINISH_SLOTS[n - LAG], it - 1)

            pipeline(act, body)

            def expert(e, par, pair):
                if is_real(e):
                    wait(act, "y_full", 2 * (e - 1))
                    for f in range(FT):
                        wait(act, "hid_full", FT * e + f + 1)
                        nc.scalar.activation(hid[par][:, f, :], t_bank[f % 2][:, 0:CAP], ACT.Gelu_apprx_tanh).then_inc(s["hid_taken"], 1)

            over_experts(act, expert)

        @block.tensor
        def _(pe):
            pe.wait_ge(s["consts_loaded"], 16 * N_CONSTS)
            pe.wait_ge(s["ident_done"], 1)
            pe.wait_ge(s["upper_done"], 1)
            pe.wait_ge(s["ewT_done"], 1)
            pe.wait_ge(s["o_bank_cleared"], 1)

            def transpose3(to, src):
                for t in range(NT):
                    last = pe.transpose(to[0:src(t).shape[1], t * P:(t + 1) * P], src(t), ident[:, :])
                return last

            def fusion_task(name, b):
                base = N_FUSION * b + FUSION_AT[name]
                if name in NOT_IN_BANK:
                    return
                wait(pe, "fusion_taken", base)
                if name == "kv0":
                    wait(pe, "xc_loaded", 16 * (b + 1))
                if name in ("kv0", "kv1"):
                    t = int(name[2])
                    for i in range(DT):
                        last = pe.matmul(f_bank[:, :].rearrange("p (k c) -> p k c", k=2)[:, :, i * P:(i + 1) * P],
                                         xc[:, i, t * P:(t + 1) * P], wkv[:, :, :], start=True, stop=True)
                    last.then_inc(s["fusion_full"], 1)
                if name == "q":
                    for i in range(DT):
                        last = pe.matmul(f_bank[:, i * L:(i + 1) * L], wq[:, :], xc[:, i, :], start=True, stop=True)
                    last.then_inc(s["fusion_full"], 1)
                if name in ("den", "num"):
                    c0 = D if name == "num" else 0
                    wait(pe, "ekv_done" if name == "num" else "ek_done", LT * (b + 1))
                    for i in range(DT):
                        for t in range(LT):
                            last = pe.matmul(f_bank[:, i * L:(i + 1) * L], ekv[:, t, c0 + i * P:c0 + (i + 1) * P], ewT[:, t, :],
                                             start=t == 0, stop=t == LT - 1)
                    last.then_inc(s["fusion_full"], 1)
                if name == "aft":
                    for t in range(LT):
                        for i in range(DT):
                            last = pe.matmul(f_bank[:, t * D:(t + 1) * D], yT[:, i, t * P:(t + 1) * P], out_w[:, i, :],
                                             start=i == 0, stop=i == DT - 1)
                    last.then_inc(s["fusion_full"], 1)
                if name == "text_t":
                    wait(pe, "emb_masked", 3 * (b + 1))
                    transpose3(f_bank, lambda t: emb[:, t * P:(t + 1) * P]).then_inc(s["fusion_full"], 1)
                if name == "text":
                    for i in range(3):
                        last = pe.matmul(f_bank[:, 0:D], embT[:, i * P:(i + 1) * P], w_txt[:, i, :], start=i == 0, stop=i == 2)
                    last.then_inc(s["fusion_full"], 1)
                if name in ("zt0", "zt1"):
                    i = int(name[2])
                    wait(pe, "zn_done", NT * (b + 1))
                    transpose3(f_bank, lambda t: zn[:, t, i * P:(i + 1) * P]).then_inc(s["fusion_full"], 1)
                if name[:2] == "qk":
                    n = int(name[2])
                    for i in range(DT):
                        last = pe.matmul(f_bank[:, 0:N], w_qkv[:, i, n * P:(n + 1) * P], zT[:, i, :], start=i == 0, stop=i == DT - 1)
                    last.then_inc(s["fusion_full"], 1)

            def finish_task(name, b):
                base = N_FINISH * b + FINISH_AT[name]
                if name in NOT_IN_BANK:
                    return
                wait(pe, "finish_taken", base)
                if name[:2] == "ot":
                    g = int(name[2])
                    wait(pe, "o_taken", NG * b + g + 1)
                    transpose3(n_bank, lambda t: oS[:, g, t * P:(t + 1) * P]).then_inc(s["finish_full"], 1)
                if name[:3] == "ont":
                    i = int(name[3])
                    transpose3(n_bank, lambda t: oN[:, t, i * P:(i + 1) * P]).then_inc(s["finish_full"], 1)
                if name[:4] == "proj":
                    t0, t1 = ((0, 2), (2, 3))[int(name[4])]
                    for t in range(t0, t1):
                        for i in range(DT):
                            last = pe.matmul(n_bank[:, (t - t0) * D:(t - t0 + 1) * D], tT[:, i, t * P:(t + 1) * P], w_proj[:, i, :],
                                             start=i == 0, stop=i == DT - 1)
                    last.then_inc(s["finish_full"], 1)
                if name[:2] == "xt":
                    i = int(name[2])
                    wait(pe, "xn_done", b + 1)
                    transpose3(n_bank, lambda t: xn[:, t, i * P:(i + 1) * P]).then_inc(s["finish_full"], 1)
                if name == "route":
                    for t in range(NT):
                        for i in range(DT):
                            last = pe.matmul(n_bank[:, t * EXPERTS:(t + 1) * EXPERTS], tT[:, i, t * P:(t + 1) * P], w_r[:, i, :],
                                             start=i == 0, stop=i == DT - 1)
                    last.then_inc(s["finish_full"], 1)
                if name == "count":
                    wait(pe, "run_done", (NT + 1) * (b + 1))
                    pe.matmul(n_bank[:, 0:NT * EXPERTS], upper[:, :], oh[:, :, :], start=True, stop=False)
                    pe.matmul(n_bank[:, 0:NT * EXPERTS], ones[:, :], run[:, 0:NT, :], start=False, stop=True).then_inc(s["finish_full"], 1)

            def leave_v(b, i):
                t0, t1 = ((0, 2), (2, 3))[i]
                wait(pe, "fusion_taken", N_FUSION * b + FUSION_AT["zt1"] + 1)
                wait(pe, "m_taken", 2 * b)
                wait(pe, "v_taken", 2 * b + i)
                for t in range(t0, t1):
                    for k in range(DT):
                        last = pe.matmul(v_bank[:, (t - t0) * D:(t - t0 + 1) * D], zT[:, k, t * P:(t + 1) * P],
                                         w_qkv[:, k, 2 * D:3 * D], start=k == 0, stop=k == DT - 1)
                last.then_inc(s["v_full"], 1)

            def leave_maxima(b, half):
                wait(pe, "v_taken", 2 * (b + 1))
                wait(pe, "m_taken", 2 * b + half)
                wait(pe, "nmx_done", 2 * b + half + 1)
                transpose3(v_bank, lambda t: nmx[:, t, half, :, :].rearrange("p a h -> p (a h)")).then_inc(s["m_full"], 1)

            def attend_v(b, par, g, t):
                if t == 0:
                    wait(pe, "p_ready", STEPS * b + (g + 1) * GRP * NT)
                    wait(pe, "v_taken", 2 * (b + 1))
                    wait(pe, "o_taken", NG * b + g)
                for k in range(GRP):
                    head = g * GRP + k
                    last = pe.matmul(o_bank[32 * k:32 * k + VC, 0:N], v_aug[:, par, t, head, :], probs[:, (head * NT + t) % PRING, :],
                                     start=t == 0, stop=t == NT - 1)
                if t == NT - 1:
                    last.then_inc(s["o_full"], 1)

            def body(it, par, pair, fusion, shift, attend, finish):
                for n in range(STEPS):
                    step, t = n // NT, n % NT
                    half, head = step // HALF, step % HALF
                    if shift:
                        b, sl = it + 1, 2 * (1 - par) + half
                        if head == 0 and t == 0:
                            wait(pe, qk_loaded[1 - par][half], 96 * (pair(1) + 1))
                        wait(pe, "s_taken", STEPS * b + n + 1 - SRING)
                        pe.matmul(s_bank[n % SRING][:, 0:N], qst[:, sl, head, t * P:(t + 1) * P], kst[:, sl, head, :],
                                  start=True, stop=True).then_inc(s["s_full"], 1)
                    if attend:
                        sl = 2 * par + half
                        if head == 0 and t == 0:
                            wait(pe, m_loaded[par][half], 32 * (pair(0) + 1))
                        wait(pe, "p_ready", STEPS * it + n + 1 - TRING)
                        pe.matmul(t_bank[n % TRING][:, 0:N], kst[:, sl, head, t * P:(t + 1) * P], qst[:, sl, head, :],
                                  start=True, stop=True).then_inc(s["t_full"], 1)
                    group, tile = n // (GRP * NT) - 1, n % (GRP * NT) - 1
                    if 0 <= tile < NT:
                        if group < 0 and finish:
                            attend_v(it - 1, 1 - par, NG - 1, tile)
                        if group >= 0 and attend:
                            attend_v(it, par, group, tile)
                    if attend and n == MAX1_AT:
                        leave_maxima(it, 1)
                    if shift and n in V_AT:
                        leave_v(it + 1, V_AT.index(n))
                    if shift and n == MAX0_AT:
                        leave_maxima(it + 1, 0)
                    if fusion and n in FUSION_SLOTS:
                        fusion_task(FUSION_SLOTS[n], it + 2)
                    if finish and n in FINISH_SLOTS:
                        finish_task(FINISH_SLOTS[n], it - 1)

            pipeline(pe, body)
            pe.wait_ge(s["p_ready"], B * NH * NT)
            pe.wait_ge(s["s_taken"], B * NH * NT)

            def expert(e, par, pair):
                if is_real(e):
                    for i in range(DT):
                        wait(pe, "xeT_taken", 2 * e + i)
                        wait(pe, xe_loaded[par], 16 * (pair + 1))
                        transpose3(f_bank, lambda t: xe[par][:, t, i * P:(i + 1) * P]).then_inc(s["xeT_full"], 1)
                    wait(pe, "xeT_taken", 2 * e + 2)
                    wait(pe, w1_loaded[par], 16 * (pair + 1))
                    for f in range(FT):
                        wait(pe, "hid_taken", FT * e + f - 1)
                        for i in range(DT):
                            last = pe.matmul(t_bank[f % 2][:, 0:CAP], w1s[par][:, i, f * P:(f + 1) * P], xeT[:, i, :],
                                             start=i == 0, stop=i == DT - 1)
                        last.then_inc(s["hid_full"], 1)
                if is_real(e - 1):
                    wait(pe, w2_loaded[1 - par], 16 * (pair + par))
                    wait(pe, "hid_taken", FT * e)
                    for part, (t0, t1) in enumerate(((0, 2), (2, 3))):
                        wait(pe, "y_taken", 2 * (e - 2) + part + 1)
                        for t in range(t0, t1):
                            for f in range(FT):
                                last = pe.matmul(s_bank[part][:, (t - t0) * D:(t - t0 + 1) * D], hid[1 - par][:, f, t * P:(t + 1) * P],
                                                 w2s[1 - par][:, f, :], start=f == 0, stop=f == FT - 1)
                        last.then_inc(s["y_full"], 1)

            over_experts(pe, expert)

        @block.vector
        def _(dve):
            nc.vector.memset(o_bank[:, :], 0.0).then_inc(s["o_bank_cleared"], 1)
            dve.wait_ge(s["tok_loaded"], 16)
            nc.vector.tensor_copy(tok_f[:, :], tok_i[:, :]).then_inc(s["band_steps"], 1)
            dve.wait_ge(s["band_steps"], 1)
            for i in range(3):
                low, high = float(BANDS[i]), float(BANDS[i + 1])
                nc.vector.tensor_scalar(rel_f[:, i, :], tok_f[:, :], low, 0.0, ALU.subtract, ALU.max).then_inc(s["band_steps"], 1)
                nc.vector.tensor_scalar(band[:, i, :], tok_f[:, :], low, None, ALU.is_ge).then_inc(s["band_steps"], 1)
                nc.vector.tensor_scalar(band_t[:, i, :], tok_f[:, :], high, None, ALU.is_lt).then_inc(s["band_steps"], 1)
            dve.wait_ge(s["band_steps"], 10)
            for i in range(3):
                nc.vector.tensor_scalar(rel_i[:, i, :], rel_f[:, i, :], float(BANDS[i + 1] - BANDS[i] - 1), None, ALU.min)
            nc.vector.tensor_tensor(band[:, :, :], band[:, :, :], band_t[:, :, :], ALU.mult).then_inc(s["bands_done"], 1)
            dve.wait_ge(s["mask_loaded"], 32)
            nc.vector.tensor_copy(eq[:, :, :], mask8[:, :, :]).then_inc(s["wmask_done"], 1)
            dve.wait_ge(s["wmask_done"], 1)
            nc.vector.tensor_tensor(ewT[:, :, :], ewT[:, :, :], eq[:, :, :], ALU.mult).then_inc(s["wmask_done"], 1)
            dve.wait_ge(s["consts_loaded"], 16 * N_CONSTS)
            nc.vector.tensor_scalar(nbq[:, :], nbq[:, :], -1.0, None, ALU.mult).then_inc(s["nbq_done"], 1)
            dve.wait_ge(s["iota_done"], 1)
            dve.wait_ge(s["trash_done"], 1)
            dve.wait_ge(s["counts_zeroed"], 1)
            flat = lambda v: v.rearrange("p a b -> p (a b)")

            def fusion_task(name, b):
                base = N_FUSION * b + FUSION_AT[name]
                if name in ("kv0", "kv1"):
                    t = int(name[2])
                    wait(dve, "fusion_full", base + 1)
                    if t == 1:
                        wait(dve, "ek_done", LT * b + 1)
                        wait(dve, "ekv_done", LT * b + 1)
                    nc.vector.tensor_tensor(kvs[:, :], f_bank[:, :], kv_bias, ALU.add).then_inc(s["fusion_taken"], 1)
                if name in ("ekv0", "ekv1"):
                    t = int(name[3])
                    wait(dve, "ek_done", LT * b + t + 1)
                    nc.vector.tensor_tensor(ekv[:, t, D:2 * D], ekv[:, t, 0:D], kvs[:, D:2 * D], ALU.mult).then_inc(s["ekv_done"], 1)
                if name == "den":
                    wait(dve, "fusion_full", base + 1)
                    nc.vector.scalar_tensor_tensor(out=flat(eq[:, :, :]), in0=flat(eq[:, :, :]), scalar=1.0, in1=f_bank[:, :],
                                                   op0=ALU.add, op1=ALU.mult).then_inc(s["fusion_taken"], 1)
                if name[:3] == "inv":
                    i, half = int(name[3]) // 2, slice(int(name[3]) % 2 * P, int(name[3]) % 2 * P + P)
                    wait(dve, "fusion_taken", N_FUSION * b + FUSION_AT["den"] + 1)
                    nc.vector.reciprocal(eq[:, i, half], eq[:, i, half]).then_inc(s["den_inverted"], 1)
                if name == "num":
                    wait(dve, "fusion_full", base + 1)
                    wait(dve, "den_inverted", 4 * (b + 1))
                    nc.vector.tensor_tensor(flat(yT[:, :, :]), f_bank[:, :], flat(eq[:, :, :]), ALU.mult).then_inc(s["fusion_taken"], 1)
                if name == "aft":
                    wait(dve, "fusion_full", base + 1)
                    wait(dve, "xr_biased", LT * (b + 1))
                    wait(dve, "hb_done", b)
                    nc.vector.tensor_tensor(flat(h[:, 0:LT, :]), f_bank[:, :], flat(xr[:, :, :]), ALU.add).then_inc(s["fusion_taken"], 1)
                if name == "aft_stats":
                    wait(dve, "fusion_taken", N_FUSION * b + FUSION_AT["aft"] + 1)
                    for t in range(LT):
                        nc.vector.bn_stats(st_a[:, t, :], h[:, t, :]).then_inc(s["st_a_done"], 1)
                    for t in range(LT):
                        wait_apart(dve, "st_a_done", LT * b + t + 1)
                        nc.vector.bn_aggr(mv_a[:, t, :], st_a[:, t, :]).then_inc(s["mv_a_done"], 1)
                if name in ("aft_norm0", "aft_norm1"):
                    t = int(name[8])
                    wait(dve, "r_a_done", b + 1)
                    nc.vector.tensor_scalar(h[:, t, :], h[:, t, :], mv_a[:, t, 0:1], r_a[:, t:t + 1], ALU.subtract, ALU.mult)\
                        .then_inc(s["h_norm"], 1)
                if name[:5] == "stats":
                    t = int(name[5])
                    if t == 2:
                        wait(dve, "fusion_taken", N_FUSION * b + FUSION_AT["text"] + 1)
                    else:
                        wait(dve, "h_gained", LT * b + t + 1)
                    nc.vector.bn_stats(st_b[:, t, :], h[:, t, :]).then_inc(s["st_b_done"], 1)
                    if t == 1:
                        wait(dve, "hb_step", 6 * b)
                        wait_apart(dve, "st_b_done", NT * (b + 1))
                        for t in range(NT):
                            nc.vector.bn_aggr(mv_b[:, t, :], st_b[:, t, :]).then_inc(s["mv_b_done"], 1)
                if name[:2] == "zn":
                    t = int(name[2])
                    wait(dve, "r_b_done", b + 1)
                    wait(dve, "fusion_full", N_FUSION * b + FUSION_AT["num"] + 1)
                    nc.vector.tensor_scalar(zn[:, t, :], h[:, t, :], mv_b[:, t, 0:1], r_bc[:, t:t + 1], ALU.subtract, ALU.mult)\
                        .then_inc(s["zn_done"], 1)
                if name[:2] == "qk":
                    n = int(name[2])
                    wait(dve, "hi_done", 4 * b + n + 1)
                    nc.vector.tensor_tensor(lo[:, n % 2, :], f_bank[:, 0:N], hi[:, n % 2, :].bitcast(F32), ALU.subtract).then_inc(s["fusion_taken"], 1)

            def finish_task(name, b):
                base = N_FINISH * b + FINISH_AT[name]
                if name[:2] == "ot":
                    g = int(name[2])
                    v = n_bank[:, 0:N].rearrange("p (t k c) -> p t k c", t=NT, k=GRP)
                    wait(dve, "finish_full", base + 1)
                    nc.vector.reciprocal(rden[:, :, :], v[:, :, :, HD]).then_inc(s["rden_done"], 1)
                    wait(dve, "rden_done", NG * b + g + 1)
                    nc.vector.tensor_tensor(oN[:, :, g * GRP * HD:(g + 1) * GRP * HD].rearrange("p t (k d) -> p t k d", k=GRP), v[:, :, :, 0:HD],
                                            rden[:, :, :, None].broadcast_to([P, NT, GRP, HD]), ALU.mult).then_inc(s["finish_taken"], 1)
                if name[:4] == "proj":
                    t0, t1 = ((0, 2), (2, 3))[int(name[4])]
                    wait(dve, "finish_full", base + 1)
                    wait(dve, "hb_back", 16 * (b + 1))
                    nc.vector.tensor_tensor(h1[:, t0:t1, :], n_bank[:, 0:(t1 - t0) * D].rearrange("p (t d) -> p t d", d=D), h1[:, t0:t1, :], ALU.add)\
                        .then_inc(s["finish_taken"], 1)
                    wait(dve, "finish_taken", base + 1)
                    for t in range(t0, t1):
                        nc.vector.bn_stats(st_d[:, t, :], h1[:, t, :]).then_inc(s["st_d_done"], 1)
                    for t in range(t0, t1):
                        wait_apart(dve, "st_d_done", NT * b + t + 1)
                        nc.vector.bn_aggr(mv_d[:, t, :], st_d[:, t, :]).then_inc(s["mv_d_done"], 1)
                if name[:2] == "xn":
                    t = int(name[2])
                    wait(dve, "r_d_done", b + 1)
                    wait(dve, "scattered", 16 * NT * b)
                    last = nc.vector.tensor_scalar(xn[:, t, :], h1[:, t, :], mv_d[:, t, 0:1], r_d[:, t:t + 1], ALU.subtract, ALU.mult)
                    if t == NT - 1:
                        last.then_inc(s["xn_done"], 1)
                if name == "route":
                    wait(dve, "finish_full", base + 1)
                    nc.vector.tensor_copy(flat(lg[:, :, :]), n_bank[:, 0:NT * EXPERTS]).then_inc(s["finish_taken"], 1)
                    wait_apart(dve, "finish_taken", base + 1)
                    for t in range(NT):
                        last = nc.vector.max(m8[:, t, :], lg[:, t, :])
                    last.then_inc(s["m8_done"], 1)
                if name == "best":
                    wait(dve, "m8_done", b + 1)
                    nc.vector.tensor_tensor(df[:, :, :], lg[:, :, :], m8[:, :, 0:1].broadcast_to([P, NT, EXPERTS]), ALU.subtract).then_inc(s["df_done"], 1)
                    for t in range(NT):
                        last = nc.vector.max_index(i8[:, t, :], m8[:, t, :], lg[:, t, :])
                    last.then_inc(s["i8_done"], 1)
                if name == "chosen":
                    wait(dve, "i8_done", b + 1)
                    nc.vector.tensor_copy(ei[:, :], i8[:, :, 0]).then_inc(s["ei_done"], 1)
                    wait(dve, "ei_done", b + 1)
                    nc.vector.tensor_tensor(oh[:, :, :], iota8[:, None, :].broadcast_to([P, NT, EXPERTS]),
                                            ei[:, :, None].broadcast_to([P, NT, EXPERTS]), ALU.is_equal).then_inc(s["oh_done"], 1)
                if name == "totals":
                    wait(dve, "run_done", (NT + 1) * b)
                    nc.vector.tensor_copy(run[:, 0, :], run[:, NT, :]).then_inc(s["run_done"], 1)
                    wait(dve, "oh_done", b + 1)
                    for t in range(NT):
                        wait(dve, "run_done", (NT + 1) * b + t + 1)
                        nc.vector.tensor_tensor(run[:, t + 1, :], run[:, t, :], oh[:, t, :], ALU.add).then_inc(s["run_done"], 1)
                if name == "pick":
                    wait(dve, "ex_done", b + 1)
                    nc.vector.reduce_sum(se[:, :], ex[:, :, :], axis=AX.X).then_inc(s["se_done"], 1)
                    wait(dve, "se_done", 2 * b + 1)
                    nc.vector.reciprocal(se[:, :], se[:, :]).then_inc(s["se_done"], 1)
                if name == "count":
                    wait(dve, "finish_full", base + 1)
                    nc.vector.tensor_tensor(cp[:, :, :], n_bank[:, 0:NT * EXPERTS].rearrange("p (t e) -> p t e", e=EXPERTS), oh[:, :, :], ALU.mult)\
                        .then_inc(s["finish_taken"], 1)
                if name == "slots":
                    def done(i):
                        return 6 * b + i
                    wait(dve, "finish_taken", base)
                    nc.vector.reduce_sum(pos[:, :], cp[:, :, :], axis=AX.X).then_inc(s["slot_step"], 1)
                    wait(dve, "slot_step", done(1))
                    nc.vector.tensor_scalar(keep[:, :], pos[:, :], float(CAP), None, ALU.is_le).then_inc(s["slot_step"], 1)
                    nc.vector.scalar_tensor_tensor(out=slot[:, :], in0=ei[:, :], scalar=float(CAP), in1=pos[:, :], op0=ALU.mult, op1=ALU.add)\
                        .then_inc(s["slot_step"], 1)
                    wait(dve, "slot_step", done(3))
                    nc.vector.scalar_tensor_tensor(out=sk[:, :], in0=slot[:, :], scalar=-1.0, in1=keep[:, :], op0=ALU.add, op1=ALU.mult)\
                        .then_inc(s["slot_step"], 1)
                    nc.vector.tensor_scalar(drop[:, :], keep[:, :], -1.0, 1.0, ALU.mult, ALU.add).then_inc(s["slot_step"], 1)
                    wait(dve, "slot_step", done(5))
                    nc.vector.tensor_tensor(drop[:, :], drop[:, :], trash[:, bass.ds(b * NT, NT)], ALU.mult).then_inc(s["slot_step"], 1)
                    nc.vector.tensor_copy(gidx[:, bass.ds(b * NT, NT)], sk[:, :])
                    wait(dve, "se_done", 2 * b + 2)
                    nc.vector.tensor_tensor(gate[:, bass.ds(b * NT, NT)], keep[:, :], se[:, :], ALU.mult).then_inc(s["gate_done"], 1)
                    wait(dve, "slot_step", done(6))
                    nc.vector.tensor_tensor(si[:, :], sk[:, :], drop[:, :], ALU.add).then_inc(s["slots_done"], 1)

            def split_maxima(b, half):
                hs = slice(half * HALF, (half + 1) * HALF)
                wait(dve, "s_taken", STEPS * b + (half + 1) * HALF * NT)
                wait(dve, "m_full", 2 * (b - 1) + half + 1)
                nc.vector.tensor_scalar(nmx[:, :, half, 0, :].bitcast(F32R), mx[:, :, hs], -1.0, None, ALU.mult).then_inc(s["nmx_hi"], 1)
                wait(dve, "nmx_hi", 2 * b + half + 1)
                nc.vector.scalar_tensor_tensor(out=nmx[:, :, half, 1, :].bitcast(F32R), in0=mx[:, :, hs], scalar=-1.0, in1=nmx[:, :, half, 0, :],
                                               op0=ALU.mult, op1=ALU.subtract).then_inc(s["nmx_done"], 1)

            def take_maxima(b, half, before, samples):
                wait(dve, "m_full", 2 * b + half + 1)
                wait(dve, before, 32 * samples)
                nc.vector.tensor_copy(mT[:, half, :], v_bank[0:2 * HALF, 0:N]).then_inc(s["m_taken"], 1)

            def body(it, par, pair, fusion, shift, attend, finish):
                for n in range(STEPS):
                    if shift:
                        wait(dve, "s_full", STEPS * (it + 1) + n + 1)
                        nc.vector.reduce_max(mx[:, n % NT, n // NT:n // NT + 1], s_bank[n % SRING][:, 0:N], axis=AX.X).then_inc(s["s_taken"], 1)
                    if n == 0 and attend:
                        split_maxima(it, 1)
                    if n == MAX1_AT + LAG and attend:
                        take_maxima(it, 1, m_loaded[1 - par][1], pair(1))
                    if n == MAX0_AT - 2 and shift:
                        split_maxima(it + 1, 0)
                    if n == MAX0_AT + LAG and shift:
                        take_maxima(it + 1, 0, m_loaded[par][0], pair(0) + 1)
                    if fusion and n - LAG in FUSION_SLOTS:
                        fusion_task(FUSION_SLOTS[n - LAG], it + 2)
                    if finish and n - LAG in FINISH_SLOTS:
                        finish_task(FINISH_SLOTS[n - LAG], it - 1)

            pipeline(dve, body)

            def expert(e, par, pair):
                if is_real(e):
                    for i in range(DT):
                        wait(dve, "xeT_full", 2 * e + i + 1)
                        wait(dve, "hid_full", FT * e)
                        nc.vector.tensor_copy(xeT[:, i, :], f_bank[:, 0:CAP]).then_inc(s["xeT_taken"], 1)
                if is_real(e - 1):
                    for part, (t0, t1) in enumerate(((0, 2), (2, 3))):
                        wait(dve, "y_full", 2 * (e - 1) + part + 1)
                        wait(dve, "ye_stored", 16 * (e - 1))
                        nc.vector.tensor_copy(ye[:, t0:t1, :], s_bank[part][:, 0:(t1 - t0) * D].rearrange("p (t d) -> p t d", d=D))\
                            .then_inc(s["y_taken"], 1)

            over_experts(dve, expert)
            dve.wait_ge(s["h1_loaded"], 16)
            dve.wait_ge(s["gate_done"], B)
            for n in range(B * NT):
                dve.wait_ge(gathered[n % 4], 16 * (n // 4 + 1))
                nc.vector.scalar_tensor_tensor(out=h1f[:, n, :], in0=yg[:, n % 4, :], scalar=gate[:, n:n + 1], in1=h1f[:, n, :],
                                               op0=ALU.mult, op1=ALU.add).then_inc(s["combined"], 1)


def kernel(**inputs):
    import numpy as np

    import concourse.bacc as bacc
    from concourse.bass_utils import run_bass_kernel_spmd

    g = {k: np.asarray(v) for k, v in inputs.items()}
    heads = D // C
    x = g["x"]
    row = np.concatenate([np.tile(g["L0_tok_Wk_b"], heads), np.tile(g["L0_tok_Wv_b"], heads), g["L0_tok_out_b"], g["L0_tok_ln_g"],
                          g["L0_tok_ln_b"], g["L0_attn_b_proj"]])
    w5 = g["L0_attn_w_qkv"].reshape(D, NH, HD, 3)
    halves = w5[..., 0:2].reshape(D, 2, HALF, HD, 2).transpose(0, 1, 4, 3, 2).reshape(D, 2 * D)
    w_qkv = np.concatenate([halves, w5[..., 2].reshape(D, D)], axis=1)
    arrays = {
        "x_cl": x.transpose(0, 3, 1, 2).reshape(B, D, L),
        "x_lc": x.transpose(0, 2, 3, 1).reshape(B, L, D),
        "tokens": g["x_txt"].T,
        "rows": np.broadcast_to(row, (P, row.size)),
        "cols": np.stack([g["L0_attn_ln_scale"].reshape(DT, P).T, g["L0_attn_ln_bias"].reshape(DT, P).T], axis=1),
        "bq": g["L0_tok_Wq_b"].reshape(C, 1),
        "WkT": g["L0_tok_Wk_w"].T, "WvT": g["L0_tok_Wv_w"].T, "WqT": g["L0_tok_Wq_w"].T,
        "w_biasT": g["L0_tok_w_bias"].T, "maskT": g["L0_tok_local_mask"].T,
        "out_w": g["L0_tok_out_w"],
        "E0": g["L0_txt_E0"], "E1": g["L0_txt_E1"], "E2": g["L0_txt_E2"],
        "W0": g["L0_txt_W0"], "W1": g["L0_txt_W1"], "W2": g["L0_txt_W2"],
        "w_qkv": w_qkv, "w_proj": g["L0_attn_w_proj"],
        "router_w": g["L0_ffn_router_w"], "w1": g["L0_ffn_w1"], "w2": g["L0_ffn_w2"],
    }
    nc = bacc.Bacc("TRN2", target_bir_lowering=False, num_devices=1)
    nc.disable_value_cache = True
    feeds, aps = {}, {}
    for name, array in arrays.items():
        array = np.ascontiguousarray(array)
        feeds[f"in_{name}"] = array
        aps[name] = nc.dram_tensor(f"in_{name}", list(array.shape), mybir.dt.from_np(array.dtype), kind="ExternalInput").ap()
    out = nc.dram_tensor("out", [B, N, D], F32, kind="ExternalOutput").ap()
    early_fusion_kernel(nc, aps, out)
    result = run_bass_kernel_spmd(nc, [feeds], core_ids=[0])
    return result.results[0]["out"]
```

```python
from contextlib import ExitStack

import concourse.bass as bass
from concourse import mybir

F32 = mybir.dt.float32
F32R = mybir.dt.float32r
I32 = mybir.dt.int32
U32 = mybir.dt.uint32
U8 = mybir.dt.uint8
ALU = mybir.AluOpType
ACT = mybir.ActivationFunctionType
AX = mybir.AxisListType

P = 128
B = 8
L = 256
LT = L // P
C = 64
D = 256
DT = D // P
N = 384
NT = N // P
NH = 16
HD = 16
HALF = NH // 2
GRP = 4
NG = NH // GRP
VC = HD + 1
EXPERTS = 8
FF = 1024
FT = FF // P
TOK = B * N
CAP = TOK // EXPERTS
CT = CAP // P
EPS = 1e-5
BANDS = [0, 5000, 10000, 50257]
SCALE = 1.0 / (D / NH) ** 0.5
PRING = 16
SRING = 2
W_CHUNKS = 4
PASSES = (("hi", "hi"), ("hi", "lo"), ("lo", "hi"))
GRING = 6
TRING = 2

STEPS = NH * NT
LAG = 1
FUSION_SLOTS = {0: "kv0", 1: "ekv0", 2: "kv1", 3: "ekv1", 4: "q", 6: "den", 7: "inv0", 8: "inv1", 9: "inv2", 10: "inv3",
                11: "num", 13: "aft", 14: "aft_stats", 15: "text_t", 16: "aft_gain0", 17: "aft_gain1", 18: "text",
                19: "aft_norm0", 20: "aft_norm1", 21: "stats0", 22: "stats2", 23: "stats1", 26: "zn0", 27: "zn1", 28: "zn2",
                30: "zt0", 32: "zt1", 34: "qk0", 35: "qk1", 37: "qk2", 38: "qk3"}
FINISH_SLOTS = {1: "ot0", 3: "ot1", 5: "ot2", 9: "ot3", 11: "ont0", 13: "ont1", 16: "proj0", 19: "proj1", 24: "xn0", 25: "xn1",
                26: "xn2", 31: "xt0", 33: "xt1", 39: "route", 40: "best", 41: "chosen", 42: "totals", 43: "pick", 45: "count",
                46: "slots"}
NOT_IN_BANK = ("qk1", "qk3", "ekv0", "ekv1", "inv0", "inv1", "inv2", "inv3", "aft_stats", "aft_gain0", "aft_gain1", "aft_norm0", "aft_norm1", "stats0", "stats1", "stats2",
               "zn0", "zn1", "zn2", "xn0", "xn1", "xn2", "best", "chosen", "totals", "pick", "slots")
MAX1_AT, V_AT, MAX0_AT = 3, (10, 12), 29


def bank_positions(slots):
    place, at = {}, 0
    for name in slots.values():
        place[name] = at
        at += name not in NOT_IN_BANK
    return place, at


FUSION_AT, N_FUSION = bank_positions(FUSION_SLOTS)
FINISH_AT, N_FINISH = bank_positions(FINISH_SLOTS)


def early_fusion_kernel(nc, a, out):
    x_cl, x_lc, tokens = a["x_cl"], a["x_lc"], a["tokens"]
    E = [a["E0"], a["E1"], a["E2"]]

    qk_dram = nc.dram_tensor("qk_parts", [2, 2, 2, 2, P, N], F32, kind="Internal").ap()
    hb_dram = nc.dram_tensor("residual_in", [B, N, D], F32, kind="Internal").ap()
    h1_dram = nc.dram_tensor("residual_out", [TOK, D], F32, kind="Internal").ap()
    xe_dram = nc.dram_tensor("expert_in", [2 * TOK, D], F32, kind="Internal").ap()
    ye_dram = nc.dram_tensor("expert_out", [TOK, D], F32, kind="Internal").ap()

    with ExitStack() as ctx:
        def sb(name, shape, dt=F32):
            return ctx.enter_context(nc.sbuf_tensor(name, shape, dt))

        def bank(name):
            return ctx.enter_context(nc.psum_tensor(name, [P, 512], F32))

        def sem(name):
            return ctx.enter_context(nc.semaphore(name))

        ident = sb("ident", [P, P])
        upper = sb("upper", [P, P])
        ones = sb("ones", [P, P])
        wkv = sb("wkv", [P, 2, P])
        wq = sb("wq", [P, P])
        nbq = sb("nbq", [P, 1])
        rows = sb("rows", [P, 1536])
        kv_bias, out_b = rows[:, 0:512], rows[:, 512:768]
        ln_g, ln_b, b_proj = rows[:, 768:1024], rows[:, 1024:1280], rows[:, 1280:1536]
        ewT = sb("ewT", [P, LT, L])
        out_w = sb("out_w", [P, DT, D])
        w_txt = sb("w_txt", [P, 3, D])
        cols = sb("cols", [P, 2, DT])
        w_qkv = sb("w_qkv", [P, DT, 3 * D])
        w_proj = sb("w_proj", [P, DT, D])
        w_r = sb("w_r", [P, DT, EXPERTS])
        mhalf = sb("mhalf", [P, NT])
        zero = sb("zero", [P, 1])
        iota8 = sb("iota8", [P, EXPERTS])
        trash = sb("trash", [P, B * NT])
        mask8 = sb("mask8", [P, LT, L], U8)
        gi = sb("gi", [P, 3], I32)
        msk = sb("msk", [P, 3])
        tok_i = sb("tok_i", [P, B], I32)
        tok_f = sb("tok_f", [P, B])
        rel_f = sb("rel_f", [P, 3, B])
        rel_i = sb("rel_i", [P, 3, B], I32)
        band = sb("band", [P, 3, B])
        band_t = sb("band_t", [P, 3, B])
        xc = sb("xc", [P, DT, L])
        xr = sb("xr", [P, LT, D])
        emb = sb("emb", [P, N])
        kvs = sb("kvs", [P, 512])
        embT = kvs[:, 0:N]
        ekv = sb("ekv", [P, LT, 512])
        zn = ekv[:, :, :].rearrange("p a b -> p (a b)")[:, 0:NT * D].rearrange("p (t d) -> p t d", t=NT)
        eq = sb("eq", [P, DT, L])
        yT = sb("yT", [P, DT, L])
        h = sb("h", [P, NT, D])
        hb = sb("hb", [P, NT, D])
        st_a = sb("st_a", [P, LT, 6])
        mv_a = sb("mv_a", [P, LT, 2])
        r_a = sb("r_a", [P, LT])
        st_b = sb("st_b", [P, NT, 6])
        mv_b = sb("mv_b", [P, NT, 2])
        r_b = sb("r_b", [P, NT])
        r_c = sb("r_c", [P, NT])
        r_bc = sb("r_bc", [P, NT])
        zT = sb("zT", [P, DT, N])
        hi = sb("hi", [P, 2, N], F32R)
        lo = sb("lo", [P, 2, N], F32R)
        v_aug = sb("v_aug", [P, 2, NT, NH, VC])
        mx = sb("mx", [P, NT, NH])
        nmx = sb("nmx", [P, NT, 2, 2, HALF])
        mT = sb("mT", [2 * HALF, 2, N], F32R)
        probs = sb("probs", [P, PRING, N])
        oS = sb("oS", [P, NG, N])
        rden = sb("rden", [P, NT, GRP])
        oN = sb("oN", [P, NT, D])
        tT = sb("tT", [P, DT, N])
        h1 = sb("h1", [P, NT, D])
        st_d = sb("st_d", [P, NT, 6])
        mv_d = sb("mv_d", [P, NT, 2])
        r_d = sb("r_d", [P, NT])
        xn = sb("xn", [P, NT, D])
        lg = sb("lg", [P, NT, EXPERTS])
        m8 = sb("m8", [P, NT, 8])
        i8 = sb("i8", [P, NT, 8], U32)
        ei = sb("ei", [P, NT])
        oh = sb("oh", [P, NT, EXPERTS])
        df = sb("df", [P, NT, EXPERTS])
        ex = sb("ex", [P, NT, EXPERTS])
        se = sb("se", [P, NT])
        run = sb("run", [P, NT + 1, EXPERTS])
        cp = sb("cp", [P, NT, EXPERTS])
        pos = sb("pos", [P, NT])
        keep = sb("keep", [P, NT])
        slot = sb("slot", [P, NT])
        sk = sb("sk", [P, NT])
        drop = sb("drop", [P, NT])
        si = sb("si", [P, NT], I32)
        gate = sb("gate", [P, B * NT])
        gidx = sb("gidx", [P, B * NT], I32)
        stacks = ExitStack()
        qst = stacks.enter_context(nc.sbuf_tensor("qst", [P, 4, HALF, N], F32R))
        kst = stacks.enter_context(nc.sbuf_tensor("kst", [P, 4, HALF, N], F32R))
        stacks.close()
        w1s = sb("w1s", [P, DT, FF])
        w2s = sb("w2s", [P, FT, D])
        w1_hi, w1_lo = sb("w1_hi", [P, DT, FF], F32R), sb("w1_lo", [P, DT, FF], F32R)
        w2_hi, w2_lo = sb("w2_hi", [P, FT, D], F32R), sb("w2_lo", [P, FT, D], F32R)
        act_out = sb("act_out", [P, 2, CAP])
        hid_hi, hid_lo = sb("hid_hi", [P, FT, CAP], F32R), sb("hid_lo", [P, FT, CAP], F32R)
        xeT_hi, xeT_lo = sb("xeT_hi", [P, DT, CAP], F32R), sb("xeT_lo", [P, DT, CAP], F32R)
        xe = sb("xe", [P, CT, D])
        ye = sb("ye", [P, CT, D])
        yg = sb("yg", [P, GRING, D])
        h1f = probs[:, :, :].rearrange("p a b -> p (a b)").rearrange("p (n d) -> p n d", d=D)

        s_bank = [bank(f"s_bank{i}") for i in range(SRING)]
        t_bank = [bank(f"t_bank{i}") for i in range(TRING)]
        o_bank = bank("o_bank")
        f_bank = bank("f_bank")
        v_bank = bank("v_bank")
        n_bank = bank("n_bank")
        qk_bank = [f_bank, v_bank]
        xeT_bank, hid_bank = [f_bank, n_bank], [t_bank[0], t_bank[1], o_bank, v_bank]

        names = """waits_apart zero_done consts_loaded tok_loaded mask_loaded zeroed mhalf_done ident_done upper_done iota_done trash_done counts_zeroed
        stacks_zeroed stacks_ready v_ones_done o_bank_cleared wmask_done ewT_done nbq_done band_steps bands_done xe_cleared
        xc_loaded xr_loaded xr_biased emb_loaded emb_masked index_done
        ek_done ekv_done den_inverted st_a_done mv_a_done r_a_step r_a_done h_scaled h_gained
        st_b_done mv_b_done r_b_step r_b_done zn_done hb_step hb_done hb_stored hi_done
        fusion_full fusion_taken side_full side_taken v_full v_taken s_full s_taken nmx_hi nmx_done m_full m_taken
        t_full p_ready o_full o_taken
        finish_full finish_taken rden_done hb_back h1_stored st_d_done mv_d_done r_d_step r_d_done xn_done
        m8_done df_done ex_done i8_done ei_done oh_done run_done se_done slot_step gate_done slots_done scattered
        w1_loaded w2_loaded xe_loaded w1_hi_done w1_split w2_hi_done w2_split
        xeT_full xeT_hi_done xeT_split hid_full hid_taken hid_hi_done hid_split y_full y_taken ye_stored h1_loaded combined out_stored""".split()
        s = {n: sem(n) for n in names}
        part_stored = [sem("part_stored0"), sem("part_stored1")]
        qk_loaded = [[sem(f"qk_loaded{p}{q}") for q in range(2)] for p in range(2)]
        m_loaded = [[sem(f"m_loaded{p}{q}") for q in range(2)] for p in range(2)]
        gathered = [sem(f"gathered{i}") for i in range(GRING)]
        N_CONSTS = 17

        block = ctx.enter_context(nc.Block())

        def wait(eng, name, value):
            if not (isinstance(value, int) and value <= 0):
                eng.wait_ge(s[name] if isinstance(name, str) else name, value)

        def wait_apart(eng, name, value):
            wait(eng, name, value)
            if not isinstance(value, int):
                eng.sem_inc(s["waits_apart"], 1)

        def pipeline(eng, body):
            def one(it):
                body(it, it % 2, lambda k: (it + k) // 2, it + 2 < B, 0 <= it + 1 < B, 0 <= it < B, it >= 1)
            for it in range(-2, 2):
                one(it)
            with eng.Fori(1, (B - 2) // 2) as j:
                for i in range(2):
                    body(j * 2 + i, i, lambda k, i=i: j + (i + k) // 2, True, True, True, True)
            for it in range(B - 2, B + 1):
                one(it)

        def over_experts(eng, body):
            body(0, True)
            with eng.Fori(1, EXPERTS - 1) as e:
                body(e, True)
            body(EXPERTS - 1, False)

        @block.sync
        def _(sp):
            for dst, src in ((rows[:, :], a["rows"]), (cols[:, :, :], a["cols"]), (nbq[0:C, :], a["bq"]), (nbq[C:P, :], a["bq"])):
                sp.dma_start(dst, src).then_inc(s["consts_loaded"], 16)
            sp.dma_start(tok_i[:, :], tokens).then_inc(s["tok_loaded"], 16)
            sp.dma_start(xc[:, :, :], x_cl[0].rearrange("(t p) l -> p t l", p=P)).then_inc(s["xc_loaded"], 16)
            sp.dma_start(xr[:, :, :], x_lc[0].rearrange("(t p) c -> p t c", p=P)).then_inc(s["xr_loaded"], 16)
            sp.wait_ge(s["zeroed"], 2)
            for i in range(2):
                d = slice(C * i, C * i + C)
                sp.dma_start(wkv[d, 0, d], a["WkT"]).then_inc(s["consts_loaded"], 16)
                sp.dma_start(wkv[d, 1, d], a["WvT"]).then_inc(s["consts_loaded"], 16)
                sp.dma_start(wq[d, d], a["WqT"]).then_inc(s["consts_loaded"], 16)
            for dst, src in (
                (out_w[:, :, :], a["out_w"].rearrange("(t p) n -> p t n", p=P)),
                (w_txt[:, 0:2, :], a["W0"].rearrange("(t p) n -> p t n", p=P)),
                (w_txt[0:64, 2, :], a["W1"]), (w_txt[64:128, 2, :], a["W2"]),
                (w_qkv[:, :, :], a["w_qkv"].rearrange("(t p) n -> p t n", p=P)),
                (w_proj[:, :, :], a["w_proj"].rearrange("(t p) n -> p t n", p=P)),
                (w_r[:, :, :], a["router_w"].rearrange("(t p) n -> p t n", p=P)),
            ):
                sp.dma_start(dst, src).then_inc(s["consts_loaded"], 16)
            sp.wait_ge(s["stacks_zeroed"], 2)
            for i in range(2):
                sp.dma_start(xe_dram[i * TOK // 2:(i + 1) * TOK // 2, :].rearrange("(p r) d -> p (r d)", p=32),
                             qst[96:P, :, :, :].bitcast(F32).rearrange("p a b c -> p (a b c)")).then_inc(s["xe_cleared"], 16)

            def load_maxima(b, par, half):
                wait_apart(sp, "m_taken", 2 * b + half + 1)
                for part in range(2):
                    sp.dma_start(qst[64 + part:65 + part, 2 * par + half, :, :].bitcast(F32),
                                 mT[part * HALF:(part + 1) * HALF, half, :].bitcast(F32)).then_inc(m_loaded[par][half], 16)

            def body(it, par, pair, fusion, shift, attend, finish):
                b = it + 2
                if finish:
                    bf = it - 1
                    wait_apart(sp, "h1_stored", bf * 16)
                    wait_apart(sp, "xn_done", bf)
                    sp.dma_start(h1[:, :, :], hb_dram[bf].rearrange("(t p) d -> p t d", p=P)).then_inc(s["hb_back"], 16)
                if attend:
                    load_maxima(it, par, 1)
                if fusion and not (isinstance(b, int) and b + 1 >= B):
                    after = b + 1 if isinstance(b, int) else (b + 1) % B
                    wait_apart(sp, "fusion_full", N_FUSION * b + FUSION_AT["q"] + 1)
                    sp.dma_start(xc[:, :, :], x_cl[after].rearrange("(t p) l -> p t l", p=P)).then_inc(s["xc_loaded"], 16)
                    wait_apart(sp, "fusion_taken", N_FUSION * b + FUSION_AT["aft"] + 1)
                    sp.dma_start(xr[:, :, :], x_lc[after].rearrange("(t p) c -> p t c", p=P)).then_inc(s["xr_loaded"], 16)
                if finish:
                    wait_apart(sp, "finish_taken", N_FINISH * bf + FINISH_AT["proj1"] + 1)
                    sp.dma_start(h1_dram[bass.ds(bf * N, N), :].rearrange("(t p) d -> p t d", p=P), h1[:, :, :]).then_inc(s["h1_stored"], 16)
                def load_stacks(half):
                    if attend:
                        wait_apart(sp, "t_full", NH * NT * it + (half + 1) * HALF * NT)
                    sl = 2 * par + half
                    q_rows, k_rows = (qk_dram[par, half, i].rearrange("s (d h) n -> (s d) h n", h=HALF) for i in range(2))
                    for stack, r0, r1, src in ((qst, 0, 32, q_rows), (qst, 32, 64, q_rows), (kst, 0, 32, k_rows),
                                               (kst, 32, 48, k_rows[16:32]), (kst, 48, 64, k_rows[0:16])):
                        sp.dma_start(stack[r0:r1, sl, :, :].bitcast(F32), src).then_inc(qk_loaded[par][half], 16)
                    sp.dma_start(qst[64:66, sl, :, :].bitcast(F32), kst[66:68, sl, :, :].bitcast(F32)).then_inc(qk_loaded[par][half], 16)

                def store_parts(half):
                    for n in (2 * half, 2 * half + 1):
                        wait_apart(sp, "hi_done", 4 * b + n + 1)
                        sp.dma_start(qk_dram[par, half, n % 2, 0], hi[:, n % 2, :].bitcast(F32)).then_inc(part_stored[n % 2], 16)
                        if n % 2:
                            wait_apart(sp, "side_taken", 2 * b + half + 1)
                        else:
                            wait_apart(sp, "fusion_taken", N_FUSION * b + FUSION_AT[f"qk{n}"] + 1)
                        sp.dma_start(qk_dram[par, half, n % 2, 1], lo[:, n % 2, :].bitcast(F32)).then_inc(part_stored[n % 2], 16)
                    for n in range(2):
                        wait_apart(sp, part_stored[n], 64 * b + 32 * (half + 1))

                if fusion:
                    store_parts(0)
                    sp.wait_ge(s["stacks_ready"], 1)
                    load_stacks(0)
                    wait_apart(sp, "hb_done", b + 1)
                    sp.dma_start(hb_dram[b].rearrange("(t p) d -> p t d", p=P), hb[:, :, :]).then_inc(s["hb_stored"], 16)
                if shift:
                    load_maxima(it + 1, 1 - par, 0)
                if fusion:
                    store_parts(1)
                    load_stacks(1)

            pipeline(sp, body)

            sp.wait_ge(s["t_full"], B * NH * NT)

            def load_w1(e):
                sp.dma_start(w1s[:, :, :], a["w1"][e].rearrange("(t p) f -> p t f", p=P)).then_inc(s["w1_loaded"], 16)

            def load_w2(e):
                sp.dma_start(w2s[:, :, :], a["w2"][e].rearrange("(t p) d -> p t d", p=P)).then_inc(s["w2_loaded"], 16)

            def load_xe(e):
                sp.dma_start(xe[:, :, :], xe_dram[bass.ds(e * CAP, CAP), :].rearrange("(t p) d -> p t d", p=P)).then_inc(s["xe_loaded"], 16)

            load_w1(0)
            load_w2(0)
            sp.wait_ge(s["scattered"], 16 * B * NT)
            load_xe(0)
            sp.wait_ge(s["o_full"], NG * B)
            sp.wait_ge(s["h1_stored"], 16 * B)
            sp.dma_start(h1f[:, :, :], h1_dram.rearrange("(n p) d -> p n d", p=P)).then_inc(s["h1_loaded"], 16)

            def expert(e, another):
                if another:
                    wait_apart(sp, "xeT_full", DT * (e + 1))
                    load_xe(e + 1)
                    wait_apart(sp, "w1_split", W_CHUNKS * (e + 1))
                    load_w1(e + 1)
                    wait_apart(sp, "w2_split", W_CHUNKS * (e + 1))
                    load_w2(e + 1)
                wait_apart(sp, "y_taken", 2 * (e + 1))
                sp.dma_start(ye_dram[bass.ds(e * CAP, CAP), :].rearrange("(t p) d -> p t d", p=P), ye[:, :, :]).then_inc(s["ye_stored"], 16)

            over_experts(sp, expert)
            for b in range(B):
                sp.wait_ge(s["combined"], (b + 1) * NT)
                sp.dma_start(out[b].rearrange("(t p) d -> p t d", p=P), h1f[:, b * NT:(b + 1) * NT, :]).then_inc(s["out_stored"], 16)
            sp.wait_ge(s["out_stored"], 16 * B)

        @block.gpsimd
        def _(pool):
            pool.memset(wkv[:, :, :], 0.0).then_inc(s["zeroed"], 1)
            pool.memset(wq[:, :], 0.0).then_inc(s["zeroed"], 1)
            pool.memset(ident[:, :], 0.0).then_inc(s["zeroed"], 1)
            pool.memset(ones[:, :], 1.0).then_inc(s["zeroed"], 1)
            pool.memset(mhalf[:, :], -0.5).then_inc(s["mhalf_done"], 1)
            pool.wait_ge(s["zeroed"], 4)
            pool.affine_select(out=ident[:, :], in_=ident[:, :], compare_op=ALU.not_equal, fill=1.0, base=0,
                               pattern=[[-1, P]], channel_multiplier=1).then_inc(s["ident_done"], 1)
            pool.affine_select(out=upper[:, :], in_=ones[:, :], compare_op=ALU.is_ge, fill=0.0, base=0,
                               pattern=[[1, P]], channel_multiplier=-1).then_inc(s["upper_done"], 1)
            pool.iota(iota8[:, :], pattern=[[1, EXPERTS]], base=0, channel_multiplier=0,
                      allow_small_or_imprecise_dtypes=True).then_inc(s["iota_done"], 1)
            pool.iota(trash[:, :], pattern=[[P, B * NT]], base=TOK, channel_multiplier=1,
                      allow_small_or_imprecise_dtypes=True).then_inc(s["trash_done"], 1)
            pool.memset(run[:, NT, :], 0.0).then_inc(s["counts_zeroed"], 1)

            def gather(b):
                wait(pool, "bands_done", 1)
                wait_apart(pool, "emb_masked", 3 * b)
                wait_apart(pool, "fusion_full", N_FUSION * (b - 1) + FUSION_AT["text_t"] + 1)
                pool.tensor_copy(gi[:, :], rel_i[:, :, bass.ds(b, 1)].rearrange("p a b -> p (a b)")).then_inc(s["index_done"], 1)
                pool.tensor_copy(msk[:, :], band[:, :, bass.ds(b, 1)].rearrange("p a b -> p (a b)")).then_inc(s["index_done"], 1)
                wait_apart(pool, "index_done", 2 * b + 2)
                for i, (c0, c1) in enumerate(((0, 256), (256, 320), (320, 384))):
                    pool.indirect_dma_start(emb[:, c0:c1], None, E[i], bass.IndirectOffsetOnAxis(ap=gi[:, i:i + 1], axis=0))\
                        .then_inc(s["emb_loaded"], 16)

            pool.wait_ge(s["counts_zeroed"], 1)
            pool.memset(v_aug[:, :, :, :, HD:VC], 1.0).then_inc(s["v_ones_done"], 1)
            pool.wait_ge(s["v_ones_done"], 1)
            pool.memset(kst[64:P, :, :, :].bitcast(F32), 0.0).then_inc(s["stacks_zeroed"], 1)
            pool.wait_ge(s["stacks_zeroed"], 2)
            pool.memset(kst[64:66, :, :, :].bitcast(F32), 1.0).then_inc(s["stacks_ready"], 1)
            pool.wait_ge(s["stacks_ready"], 1)
            pool.wait_ge(s["consts_loaded"], 16 * N_CONSTS)
            pool.wait_ge(s["mhalf_done"], 1)

            def body(it, par, pair, fusion, shift, attend, finish):
                if fusion:
                    b = it + 2
                    gather(b)
                    wait(pool, "xr_loaded", 16 * (b + 1))
                    for t in range(LT):
                        pool.tensor_tensor(xr[:, t, :], xr[:, t, :], out_b, ALU.add).then_inc(s["xr_biased"], 1)
                    wait_apart(pool, "emb_loaded", 48 * (b + 1))
                    for i, (c0, c1) in enumerate(((0, 256), (256, 320), (320, 384))):
                        pool.tensor_scalar(emb[:, c0:c1], emb[:, c0:c1], msk[:, i:i + 1], None, ALU.mult).then_inc(s["emb_masked"], 1)
                    wait_apart(pool, "mv_a_done", LT * (b + 1))
                    pool.tensor_scalar(r_a[:, :], mv_a[:, :, 1], EPS, None, ALU.add).then_inc(s["r_a_step"], 1)
                    wait(pool, "r_a_step", b + 1)
                    pool.tensor_tensor(r_a[:, :], r_a[:, :], mhalf[:, 0:LT], ALU.pow).then_inc(s["r_a_done"], 1)
                if finish:
                    b = it - 1
                    wait(pool, "mv_d_done", NT * (b + 1))
                    wait_apart(pool, "xn_done", b)
                    pool.tensor_scalar(r_d[:, :], mv_d[:, :, 1], EPS, None, ALU.add).then_inc(s["r_d_step"], 1)
                    wait(pool, "r_d_step", b + 1)
                    pool.tensor_tensor(r_d[:, :], r_d[:, :], mhalf[:, :], ALU.pow).then_inc(s["r_d_done"], 1)
                if fusion:
                    b = it + 2
                    wait_apart(pool, "mv_b_done", NT * (b + 1))
                    pool.tensor_scalar(r_b[:, :], mv_b[:, :, 1], EPS, None, ALU.add).then_inc(s["r_b_step"], 1)
                    wait(pool, "r_b_step", 6 * b + 1)
                    pool.tensor_tensor(r_b[:, :], r_b[:, :], mhalf[:, :], ALU.pow).then_inc(s["r_b_step"], 1)
                    wait(pool, "r_b_step", 6 * b + 2)
                    pool.tensor_tensor(r_c[:, :], r_b[:, :], r_b[:, :], ALU.mult).then_inc(s["r_b_step"], 1)
                    wait(pool, "r_b_step", 6 * b + 3)
                    pool.tensor_tensor(r_c[:, :], r_c[:, :], mv_b[:, :, 1], ALU.mult).then_inc(s["r_b_step"], 1)
                    wait_apart(pool, "r_b_step", 6 * b + 4)
                    pool.tensor_scalar(r_c[:, :], r_c[:, :], EPS, None, ALU.add).then_inc(s["r_b_step"], 1)
                    wait(pool, "r_b_step", 6 * b + 5)
                    pool.tensor_tensor(r_c[:, :], r_c[:, :], mhalf[:, :], ALU.pow).then_inc(s["r_b_step"], 1)
                    wait(pool, "r_b_step", 6 * b + 6)
                    wait(pool, "zn_done", NT * b)
                    pool.tensor_tensor(r_bc[:, :], r_b[:, :], r_c[:, :], ALU.mult).then_inc(s["r_b_done"], 1)
                    wait_apart(pool, "hb_stored", 16 * b)
                    for t in range(NT):
                        pool.tensor_scalar(hb[:, t, :], h[:, t, :], mv_b[:, t, 0:1], r_b[:, t:t + 1], ALU.subtract, ALU.mult)\
                            .then_inc(s["hb_step"], 1)
                    for t in range(NT):
                        wait(pool, "hb_step", 6 * b + t + 1)
                        pool.tensor_tensor(hb[:, t, :], hb[:, t, :], h[:, t, :], ALU.add).then_inc(s["hb_step"], 1)
                    for t in range(NT):
                        wait(pool, "hb_step", 6 * b + NT + t + 1)
                        last = pool.tensor_tensor(hb[:, t, :], hb[:, t, :], b_proj, ALU.add)
                    last.then_inc(s["hb_done"], 1)
                if finish:
                    b = it - 1
                    pool.wait_ge(s["xe_cleared"], 32)
                    wait_apart(pool, "slots_done", b + 1)
                    for t in range(NT):
                        pool.indirect_dma_start(xe_dram, bass.IndirectOffsetOnAxis(ap=si[:, t:t + 1], axis=0), xn[:, t, :], None)\
                            .then_inc(s["scattered"], 16)

            pipeline(pool, body)

            pool.wait_ge(s["slots_done"], B)
            pool.wait_ge(s["ye_stored"], 16 * EXPERTS)
            for n in range(B * NT):
                wait_apart(pool, "combined", n - GRING + 1)
                pool.indirect_dma_start(yg[:, n % GRING, :], None, ye_dram, bass.IndirectOffsetOnAxis(ap=gidx[:, n:n + 1], axis=0))\
                    .then_inc(gathered[n % GRING], 16)

        @block.scalar
        def _(act):
            act.dma_start(ewT[:, :, :], a["w_biasT"].rearrange("(t p) l -> p t l", p=P)).then_inc(s["mask_loaded"], 16)
            act.dma_start(mask8[:, :, :], a["maskT"].rearrange("(t p) l -> p t l", p=P)).then_inc(s["mask_loaded"], 16)
            act.wait_ge(s["wmask_done"], 2)
            nc.scalar.activation(ewT[:, :, :], ewT[:, :, :], ACT.Exp).then_inc(s["ewT_done"], 1)
            act.wait_ge(s["zero_done"], 1)
            for i in range(4):
                last = nc.scalar.copy(qst[64:P, i, :, :], zero[64:P, 0:1, None].broadcast_to([P - 64, HALF, N]))
            last.then_inc(s["stacks_zeroed"], 1)
            act.wait_ge(s["nbq_done"], 1)
            act.wait_ge(s["v_ones_done"], 1)

            def fusion_task(name, b):
                base = N_FUSION * b + FUSION_AT[name]
                if name in ("kv0", "kv1"):
                    t = int(name[2])
                    wait(act, "fusion_taken", base + 1)
                    nc.scalar.activation(ekv[:, t, 0:D], kvs[:, 0:D], ACT.Exp).then_inc(s["ek_done"], 1)
                if name == "q":
                    wait(act, "fusion_full", base + 1)
                    nc.scalar.activation(eq[:, :, :].rearrange("p a b -> p (a b)"), f_bank[:, :], ACT.Exp, bias=nbq[:, 0:1], scale=-1.0)\
                        .then_inc(s["fusion_taken"], 1)
                if name == "text_t":
                    wait(act, "fusion_full", base + 1)
                    wait(act, "ekv_done", LT * (b + 1))
                    nc.scalar.copy(embT, f_bank[:, 0:N]).then_inc(s["fusion_taken"], 1)
                if name == "text":
                    wait(act, "fusion_full", base + 1)
                    wait(act, "hb_done", b)
                    nc.scalar.copy(h[:, 2, :], f_bank[:, 0:D]).then_inc(s["fusion_taken"], 1)
                if name in ("zt0", "zt1"):
                    i = int(name[2])
                    wait(act, "fusion_full", base + 1)
                    wait(act, "v_full", 2 * b)
                    nc.scalar.activation(zT[:, i, :], f_bank[:, 0:N], ACT.Identity, bias=cols[:, 1, i:i + 1], scale=cols[:, 0, i:i + 1])\
                        .then_inc(s["fusion_taken"], 1)
                if name[:2] == "qk":
                    n = int(name[2])
                    if n % 2:
                        wait(act, "side_full", 2 * b + n // 2 + 1)
                    else:
                        wait(act, "fusion_full", base + 1)
                    wait(act, part_stored[n % 2], 64 * b + 32 * (n // 2))
                    nc.scalar.copy(hi[:, n % 2, :], qk_bank[n % 2][:, 0:N]).then_inc(s["hi_done"], 1)

            def finish_task(name, b):
                if name in ("ont0", "ont1", "xt0", "xt1"):
                    wait(act, "finish_full", N_FINISH * b + FINISH_AT[name] + 1)
                    nc.scalar.copy(tT[:, int(name[-1]), :], n_bank[:, 0:N]).then_inc(s["finish_taken"], 1)
                if name == "best":
                    wait(act, "df_done", b + 1)
                    nc.scalar.activation(ex[:, :, :], df[:, :, :], ACT.Exp).then_inc(s["ex_done"], 1)

            def body(it, par, pair, fusion, shift, attend, finish):
                def take_v(i):
                    t0, t1 = ((0, 2), (2, 3))[i]
                    wait(act, "v_full", 2 * (it + 1) + i + 1)
                    wait(act, "o_full", NG * it)
                    nc.scalar.copy(v_aug[:, 1 - par, t0:t1, :, 0:HD],
                                   v_bank[:, 0:(t1 - t0) * D].rearrange("p (t h d) -> p t h d", t=t1 - t0, d=HD)).then_inc(s["v_taken"], 1)

                def take_o(b, g):
                    wait(act, "o_full", NG * b + g + 1)
                    if g == 0:
                        wait(act, "finish_full", N_FINISH * (b - 1) + FINISH_AT["ot3"] + 1)
                    nc.scalar.copy(oS[:, g, :], o_bank[:, 0:N]).then_inc(s["o_taken"], 1)

                for n in range(STEPS):
                    if attend:
                        wait(act, "t_full", STEPS * it + n + 1)
                        wait(act, "o_full", NG * it + (n - PRING) // (GRP * NT) + 1)
                        nc.scalar.activation(probs[:, n % PRING, :], t_bank[n % TRING][:, 0:N], ACT.Exp, scale=SCALE)\
                            .then_inc(s["p_ready"], 1)
                    if n == NT + LAG and finish:
                        take_o(it - 1, NG - 1)
                    if n > NT + LAG and n % (GRP * NT) == NT + LAG and attend:
                        take_o(it, n // (GRP * NT) - 1)
                    if shift and n - LAG in V_AT:
                        take_v(V_AT.index(n - LAG))
                    if fusion and n - LAG in FUSION_SLOTS:
                        fusion_task(FUSION_SLOTS[n - LAG], it + 2)
                    if finish and n - LAG in FINISH_SLOTS:
                        finish_task(FINISH_SLOTS[n - LAG], it - 1)

            pipeline(act, body)

            act.wait_ge(s["t_full"], B * NH * NT)

            def split_w1(e, c):
                f = slice(c * FF // W_CHUNKS, (c + 1) * FF // W_CHUNKS)
                if c == 0:
                    wait(act, "w1_loaded", 16 * (e + 1))
                    wait(act, "hid_full", FT * e)
                nc.scalar.copy(w1_hi[:, :, f], w1s[:, :, f]).then_inc(s["w1_hi_done"], 1)

            def split_w2(e, c):
                f = slice(c * FT // W_CHUNKS, (c + 1) * FT // W_CHUNKS)
                if c == 0:
                    wait(act, "w2_loaded", 16 * (e + 1))
                    wait(act, "y_full", 2 * e)
                nc.scalar.copy(w2_hi[:, f, :], w2s[:, f, :]).then_inc(s["w2_hi_done"], 1)

            def split_inputs(e):
                for i in range(DT):
                    wait(act, "xeT_full", DT * e + i + 1)
                    wait(act, "hid_full", FT * e)
                    nc.scalar.copy(xeT_hi[:, i, :], xeT_bank[i][:, 0:CAP]).then_inc(s["xeT_hi_done"], 1)

            for c in range(W_CHUNKS):
                split_w1(0, c)
            split_inputs(0)

            def expert(e, another):
                for f in range(FT):
                    wait(act, "hid_full", FT * e + f + 1)
                    wait(act, "hid_split", FT * e + f - 1)
                    nc.scalar.activation(act_out[:, f % 2, :], hid_bank[f % 4][:, 0:CAP], ACT.Gelu_apprx_tanh).then_inc(s["hid_taken"], 1)
                    if f < W_CHUNKS:
                        split_w2(e, f)
                    wait(act, "hid_taken", FT * e + f + 1)
                    wait(act, "y_full", 2 * e)
                    nc.scalar.copy(hid_hi[:, f, :], act_out[:, f % 2, :]).then_inc(s["hid_hi_done"], 1)
                if another:
                    split_inputs(e + 1)
                    for c in range(W_CHUNKS):
                        split_w1(e + 1, c)

            over_experts(act, expert)

        @block.tensor
        def _(pe):
            pe.wait_ge(s["consts_loaded"], 16 * N_CONSTS)
            pe.wait_ge(s["ident_done"], 1)
            pe.wait_ge(s["upper_done"], 1)
            pe.wait_ge(s["ewT_done"], 1)
            pe.wait_ge(s["o_bank_cleared"], 1)

            def transpose3(to, src):
                for t in range(NT):
                    last = pe.transpose(to[0:src(t).shape[1], t * P:(t + 1) * P], src(t), ident[:, :])
                return last

            def fusion_task(name, b):
                base = N_FUSION * b + FUSION_AT[name]
                if name in ("qk1", "qk3"):
                    wait(pe, "m_taken", 2 * b - 1)
                    wait(pe, "side_taken", 2 * b + (name == "qk3"))
                    wait(pe, "fusion_taken", N_FUSION * b + FUSION_AT["zt1"] + 1)
                elif name in NOT_IN_BANK:
                    return
                else:
                    wait(pe, "fusion_taken", base)
                if name == "kv0":
                    wait(pe, "xc_loaded", 16 * (b + 1))
                if name in ("kv0", "kv1"):
                    t = int(name[2])
                    for i in range(DT):
                        last = pe.matmul(f_bank[:, :].rearrange("p (k c) -> p k c", k=2)[:, :, i * P:(i + 1) * P],
                                         xc[:, i, t * P:(t + 1) * P], wkv[:, :, :], start=True, stop=True)
                    last.then_inc(s["fusion_full"], 1)
                if name == "q":
                    for i in range(DT):
                        last = pe.matmul(f_bank[:, i * L:(i + 1) * L], wq[:, :], xc[:, i, :], start=True, stop=True)
                    last.then_inc(s["fusion_full"], 1)
                if name in ("den", "num"):
                    c0 = D if name == "num" else 0
                    wait(pe, "ekv_done" if name == "num" else "ek_done", LT * (b + 1))
                    for i in range(DT):
                        for t in range(LT):
                            last = pe.matmul(f_bank[:, i * L:(i + 1) * L], ekv[:, t, c0 + i * P:c0 + (i + 1) * P], ewT[:, t, :],
                                             start=t == 0, stop=t == LT - 1)
                    last.then_inc(s["fusion_full"], 1)
                if name == "aft":
                    for t in range(LT):
                        for i in range(DT):
                            last = pe.matmul(f_bank[:, t * D:(t + 1) * D], yT[:, i, t * P:(t + 1) * P], out_w[:, i, :],
                                             start=i == 0, stop=i == DT - 1)
                    last.then_inc(s["fusion_full"], 1)
                if name == "text_t":
                    wait(pe, "emb_masked", 3 * (b + 1))
                    transpose3(f_bank, lambda t: emb[:, t * P:(t + 1) * P]).then_inc(s["fusion_full"], 1)
                if name == "text":
                    for i in range(3):
                        last = pe.matmul(f_bank[:, 0:D], embT[:, i * P:(i + 1) * P], w_txt[:, i, :], start=i == 0, stop=i == 2)
                    last.then_inc(s["fusion_full"], 1)
                if name in ("zt0", "zt1"):
                    i = int(name[2])
                    wait(pe, "zn_done", NT * (b + 1))
                    transpose3(f_bank, lambda t: zn[:, t, i * P:(i + 1) * P]).then_inc(s["fusion_full"], 1)
                if name[:2] == "qk":
                    n = int(name[2])
                    for i in range(DT):
                        last = pe.matmul(qk_bank[n % 2][:, 0:N], w_qkv[:, i, n * P:(n + 1) * P], zT[:, i, :], start=i == 0, stop=i == DT - 1)
                    last.then_inc(s["side_full" if n % 2 else "fusion_full"], 1)

            def finish_task(name, b):
                base = N_FINISH * b + FINISH_AT[name]
                if name in NOT_IN_BANK:
                    return
                wait(pe, "finish_taken", base)
                if name[:2] == "ot":
                    g = int(name[2])
                    wait(pe, "o_taken", NG * b + g + 1)
                    transpose3(n_bank, lambda t: oS[:, g, t * P:(t + 1) * P]).then_inc(s["finish_full"], 1)
                if name[:3] == "ont":
                    i = int(name[3])
                    transpose3(n_bank, lambda t: oN[:, t, i * P:(i + 1) * P]).then_inc(s["finish_full"], 1)
                if name[:4] == "proj":
                    t0, t1 = ((0, 2), (2, 3))[int(name[4])]
                    for t in range(t0, t1):
                        for i in range(DT):
                            last = pe.matmul(n_bank[:, (t - t0) * D:(t - t0 + 1) * D], tT[:, i, t * P:(t + 1) * P], w_proj[:, i, :],
                                             start=i == 0, stop=i == DT - 1)
                    last.then_inc(s["finish_full"], 1)
                if name[:2] == "xt":
                    i = int(name[2])
                    wait(pe, "xn_done", b + 1)
                    transpose3(n_bank, lambda t: xn[:, t, i * P:(i + 1) * P]).then_inc(s["finish_full"], 1)
                if name == "route":
                    for t in range(NT):
                        for i in range(DT):
                            last = pe.matmul(n_bank[:, t * EXPERTS:(t + 1) * EXPERTS], tT[:, i, t * P:(t + 1) * P], w_r[:, i, :],
                                             start=i == 0, stop=i == DT - 1)
                    last.then_inc(s["finish_full"], 1)
                if name == "count":
                    wait(pe, "run_done", (NT + 1) * (b + 1))
                    pe.matmul(n_bank[:, 0:NT * EXPERTS], upper[:, :], oh[:, :, :], start=True, stop=False)
                    pe.matmul(n_bank[:, 0:NT * EXPERTS], ones[:, :], run[:, 0:NT, :], start=False, stop=True).then_inc(s["finish_full"], 1)

            def leave_v(b, i):
                t0, t1 = ((0, 2), (2, 3))[i]
                wait(pe, "fusion_taken", N_FUSION * b + FUSION_AT["zt1"] + 1)
                wait(pe, "side_taken", 2 * (b + 1))
                wait(pe, "m_taken", 2 * b)
                wait(pe, "v_taken", 2 * b + i)
                for t in range(t0, t1):
                    for k in range(DT):
                        last = pe.matmul(v_bank[:, (t - t0) * D:(t - t0 + 1) * D], zT[:, k, t * P:(t + 1) * P],
                                         w_qkv[:, k, 2 * D:3 * D], start=k == 0, stop=k == DT - 1)
                last.then_inc(s["v_full"], 1)

            def leave_maxima(b, half):
                wait(pe, "v_taken", 2 * (b + 1))
                if half:
                    wait(pe, "side_taken", 2 * min(b + 2, B) if isinstance(b, int) else 2 * (b + 2))
                wait(pe, "m_taken", 2 * b + half)
                wait(pe, "nmx_done", 2 * b + half + 1)
                transpose3(v_bank, lambda t: nmx[:, t, half, :, :].rearrange("p a h -> p (a h)")).then_inc(s["m_full"], 1)

            def attend_v(b, par, g, t):
                if t == 0:
                    wait(pe, "p_ready", STEPS * b + (g + 1) * GRP * NT)
                    wait(pe, "v_taken", 2 * (b + 1))
                    wait(pe, "o_taken", NG * b + g)
                for k in range(GRP):
                    head = g * GRP + k
                    last = pe.matmul(o_bank[32 * k:32 * k + VC, 0:N], v_aug[:, par, t, head, :], probs[:, (head * NT + t) % PRING, :],
                                     start=t == 0, stop=t == NT - 1)
                if t == NT - 1:
                    last.then_inc(s["o_full"], 1)

            def body(it, par, pair, fusion, shift, attend, finish):
                for n in range(STEPS):
                    step, t = n // NT, n % NT
                    half, head = step // HALF, step % HALF
                    if shift:
                        b, sl = it + 1, 2 * (1 - par) + half
                        if head == 0 and t == 0:
                            wait(pe, qk_loaded[1 - par][half], 96 * (pair(1) + 1))
                        wait(pe, "s_taken", STEPS * b + n + 1 - SRING)
                        pe.matmul(s_bank[n % SRING][:, 0:N], qst[:, sl, head, t * P:(t + 1) * P], kst[:, sl, head, :],
                                  start=True, stop=True).then_inc(s["s_full"], 1)
                    if attend:
                        sl = 2 * par + half
                        if head == 0 and t == 0:
                            wait(pe, m_loaded[par][half], 32 * (pair(0) + 1))
                        wait(pe, "p_ready", STEPS * it + n + 1 - TRING)
                        pe.matmul(t_bank[n % TRING][:, 0:N], kst[:, sl, head, t * P:(t + 1) * P], qst[:, sl, head, :],
                                  start=True, stop=True).then_inc(s["t_full"], 1)
                    group, tile = n // (GRP * NT) - 1, n % (GRP * NT) - 1
                    if 0 <= tile < NT:
                        if group < 0 and finish:
                            attend_v(it - 1, 1 - par, NG - 1, tile)
                        if group >= 0 and attend:
                            attend_v(it, par, group, tile)
                    if attend and n == MAX1_AT:
                        leave_maxima(it, 1)
                    if shift and n in V_AT:
                        leave_v(it + 1, V_AT.index(n))
                    if shift and n == MAX0_AT:
                        leave_maxima(it + 1, 0)
                    if fusion and n in FUSION_SLOTS:
                        fusion_task(FUSION_SLOTS[n], it + 2)
                    if finish and n in FINISH_SLOTS:
                        finish_task(FINISH_SLOTS[n], it - 1)

            pipeline(pe, body)
            pe.wait_ge(s["p_ready"], B * NH * NT)
            pe.wait_ge(s["s_taken"], B * NH * NT)

            pe.wait_ge(s["o_taken"], B * NG)
            pe.wait_ge(s["v_taken"], B * 2)
            pe.wait_ge(s["m_taken"], B * 2)
            pe.wait_ge(s["side_taken"], B * 2)
            pe.wait_ge(s["fusion_taken"], B * N_FUSION)
            pe.wait_ge(s["finish_taken"], B * N_FINISH)

            def leave_inputs(e):
                wait(pe, "xe_loaded", 16 * (e + 1))
                for i in range(DT):
                    wait(pe, "xeT_split", DT * e)
                    transpose3(xeT_bank[i], lambda t: xe[:, t, i * P:(i + 1) * P]).then_inc(s["xeT_full"], 1)

            leave_inputs(0)

            def expert(e, another):
                wait(pe, "xeT_split", DT * (e + 1))
                w1, xT = {"hi": w1_hi, "lo": w1_lo}, {"hi": xeT_hi, "lo": xeT_lo}
                for f in range(FT):
                    wait(pe, "w1_split", W_CHUNKS * e + f * W_CHUNKS // FT + 1)
                    wait(pe, "hid_taken", FT * e + f - 3)
                    for i in range(DT):
                        for n, (l, r) in enumerate(PASSES):
                            last = pe.matmul(hid_bank[f % 4][:, 0:CAP], w1[l][:, i, f * P:(f + 1) * P], xT[r][:, i, :],
                                             start=i == 0 and n == 0, stop=i == DT - 1 and n == len(PASSES) - 1)
                    last.then_inc(s["hid_full"], 1)
                if another:
                    leave_inputs(e + 1)
                hT, w2 = {"hi": hid_hi, "lo": hid_lo}, {"hi": w2_hi, "lo": w2_lo}
                for part, (t0, t1) in enumerate(((0, 2), (2, 3))):
                    wait(pe, "y_taken", 2 * (e - 1) + part + 1)
                    for t in range(t0, t1):
                        for f in range(FT):
                            if t == 0:
                                wait(pe, "w2_split", W_CHUNKS * e + f * W_CHUNKS // FT + 1)
                                wait(pe, "hid_split", FT * e + f + 1)
                            for n, (l, r) in enumerate(PASSES):
                                last = pe.matmul(s_bank[part][:, (t - t0) * D:(t - t0 + 1) * D], hT[l][:, f, t * P:(t + 1) * P], w2[r][:, f, :],
                                                 start=f == 0 and n == 0, stop=f == FT - 1 and n == len(PASSES) - 1)
                    last.then_inc(s["y_full"], 1)

            over_experts(pe, expert)

        @block.vector
        def _(dve):
            nc.vector.memset(zero[:, :], 0.0).then_inc(s["zero_done"], 1)
            nc.vector.memset(o_bank[:, :], 0.0).then_inc(s["o_bank_cleared"], 1)
            dve.wait_ge(s["tok_loaded"], 16)
            nc.vector.tensor_copy(tok_f[:, :], tok_i[:, :]).then_inc(s["band_steps"], 1)
            dve.wait_ge(s["band_steps"], 1)
            for i in range(3):
                low, high = float(BANDS[i]), float(BANDS[i + 1])
                nc.vector.tensor_scalar(rel_f[:, i, :], tok_f[:, :], low, 0.0, ALU.subtract, ALU.max).then_inc(s["band_steps"], 1)
                nc.vector.tensor_scalar(band[:, i, :], tok_f[:, :], low, None, ALU.is_ge).then_inc(s["band_steps"], 1)
                nc.vector.tensor_scalar(band_t[:, i, :], tok_f[:, :], high, None, ALU.is_lt).then_inc(s["band_steps"], 1)
            dve.wait_ge(s["band_steps"], 10)
            for i in range(3):
                nc.vector.tensor_scalar(rel_i[:, i, :], rel_f[:, i, :], float(BANDS[i + 1] - BANDS[i] - 1), None, ALU.min)
            nc.vector.tensor_tensor(band[:, :, :], band[:, :, :], band_t[:, :, :], ALU.mult).then_inc(s["bands_done"], 1)
            dve.wait_ge(s["mask_loaded"], 32)
            nc.vector.tensor_copy(eq[:, :, :], mask8[:, :, :]).then_inc(s["wmask_done"], 1)
            dve.wait_ge(s["wmask_done"], 1)
            nc.vector.tensor_tensor(ewT[:, :, :], ewT[:, :, :], eq[:, :, :], ALU.mult).then_inc(s["wmask_done"], 1)
            dve.wait_ge(s["consts_loaded"], 16 * N_CONSTS)
            nc.vector.tensor_scalar(nbq[:, :], nbq[:, :], -1.0, None, ALU.mult).then_inc(s["nbq_done"], 1)
            dve.wait_ge(s["iota_done"], 1)
            dve.wait_ge(s["trash_done"], 1)
            dve.wait_ge(s["counts_zeroed"], 1)
            flat = lambda v: v.rearrange("p a b -> p (a b)")

            def fusion_task(name, b):
                base = N_FUSION * b + FUSION_AT[name]
                if name in ("kv0", "kv1"):
                    t = int(name[2])
                    wait(dve, "fusion_full", base + 1)
                    if t == 1:
                        wait(dve, "ek_done", LT * b + 1)
                        wait(dve, "ekv_done", LT * b + 1)
                    nc.vector.tensor_tensor(kvs[:, :], f_bank[:, :], kv_bias, ALU.add).then_inc(s["fusion_taken"], 1)
                if name in ("ekv0", "ekv1"):
                    t = int(name[3])
                    wait(dve, "ek_done", LT * b + t + 1)
                    nc.vector.tensor_tensor(ekv[:, t, D:2 * D], ekv[:, t, 0:D], kvs[:, D:2 * D], ALU.mult).then_inc(s["ekv_done"], 1)
                if name == "den":
                    wait(dve, "fusion_full", base + 1)
                    nc.vector.scalar_tensor_tensor(out=flat(eq[:, :, :]), in0=flat(eq[:, :, :]), scalar=1.0, in1=f_bank[:, :],
                                                   op0=ALU.add, op1=ALU.mult).then_inc(s["fusion_taken"], 1)
                if name[:3] == "inv":
                    i, half = int(name[3]) // 2, slice(int(name[3]) % 2 * P, int(name[3]) % 2 * P + P)
                    wait(dve, "fusion_taken", N_FUSION * b + FUSION_AT["den"] + 1)
                    nc.vector.reciprocal(eq[:, i, half], eq[:, i, half]).then_inc(s["den_inverted"], 1)
                if name == "num":
                    wait(dve, "fusion_full", base + 1)
                    wait(dve, "den_inverted", 4 * (b + 1))
                    nc.vector.tensor_tensor(flat(yT[:, :, :]), f_bank[:, :], flat(eq[:, :, :]), ALU.mult).then_inc(s["fusion_taken"], 1)
                if name == "aft":
                    wait(dve, "fusion_full", base + 1)
                    wait(dve, "xr_biased", LT * (b + 1))
                    wait(dve, "hb_done", b)
                    nc.vector.tensor_tensor(flat(h[:, 0:LT, :]), f_bank[:, :], flat(xr[:, :, :]), ALU.add).then_inc(s["fusion_taken"], 1)
                if name == "aft_stats":
                    wait(dve, "fusion_taken", N_FUSION * b + FUSION_AT["aft"] + 1)
                    for t in range(LT):
                        nc.vector.bn_stats(st_a[:, t, :], h[:, t, :]).then_inc(s["st_a_done"], 1)
                    for t in range(LT):
                        wait_apart(dve, "st_a_done", LT * b + t + 1)
                        nc.vector.bn_aggr(mv_a[:, t, :], st_a[:, t, :]).then_inc(s["mv_a_done"], 1)
                if name in ("aft_gain0", "aft_gain1"):
                    t = int(name[8])
                    wait(dve, "mv_a_done", LT * b + t + 1)
                    nc.vector.scalar_tensor_tensor(out=h[:, t, :], in0=h[:, t, :], scalar=mv_a[:, t, 0:1], in1=ln_g, op0=ALU.subtract, op1=ALU.mult)\
                        .then_inc(s["h_scaled"], 1)
                if name in ("aft_norm0", "aft_norm1"):
                    t = int(name[8])
                    wait(dve, "r_a_done", b + 1)
                    wait(dve, "h_scaled", LT * b + t + 1)
                    nc.vector.scalar_tensor_tensor(out=h[:, t, :], in0=h[:, t, :], scalar=r_a[:, t:t + 1], in1=ln_b, op0=ALU.mult, op1=ALU.add)\
                        .then_inc(s["h_gained"], 1)
                if name[:5] == "stats":
                    t = int(name[5])
                    if t == 2:
                        wait(dve, "fusion_taken", N_FUSION * b + FUSION_AT["text"] + 1)
                    else:
                        wait(dve, "h_gained", LT * b + t + 1)
                    nc.vector.bn_stats(st_b[:, t, :], h[:, t, :]).then_inc(s["st_b_done"], 1)
                    if t == 1:
                        wait(dve, "hb_step", 6 * b)
                        wait_apart(dve, "st_b_done", NT * (b + 1))
                        for t in range(NT):
                            nc.vector.bn_aggr(mv_b[:, t, :], st_b[:, t, :]).then_inc(s["mv_b_done"], 1)
                if name[:2] == "zn":
                    t = int(name[2])
                    wait(dve, "r_b_done", b + 1)
                    wait(dve, "fusion_full", N_FUSION * b + FUSION_AT["num"] + 1)
                    nc.vector.tensor_scalar(zn[:, t, :], h[:, t, :], mv_b[:, t, 0:1], r_bc[:, t:t + 1], ALU.subtract, ALU.mult)\
                        .then_inc(s["zn_done"], 1)
                if name[:2] == "qk":
                    n = int(name[2])
                    wait(dve, "hi_done", 4 * b + n + 1)
                    nc.vector.tensor_tensor(lo[:, n % 2, :], qk_bank[n % 2][:, 0:N], hi[:, n % 2, :].bitcast(F32), ALU.subtract)\
                        .then_inc(s["side_taken" if n % 2 else "fusion_taken"], 1)

            def finish_task(name, b):
                base = N_FINISH * b + FINISH_AT[name]
                if name[:2] == "ot":
                    g = int(name[2])
                    v = n_bank[:, 0:N].rearrange("p (t k c) -> p t k c", t=NT, k=GRP)
                    wait(dve, "finish_full", base + 1)
                    nc.vector.reciprocal(rden[:, :, :], v[:, :, :, HD]).then_inc(s["rden_done"], 1)
                    wait(dve, "rden_done", NG * b + g + 1)
                    nc.vector.tensor_tensor(oN[:, :, g * GRP * HD:(g + 1) * GRP * HD].rearrange("p t (k d) -> p t k d", k=GRP), v[:, :, :, 0:HD],
                                            rden[:, :, :, None].broadcast_to([P, NT, GRP, HD]), ALU.mult).then_inc(s["finish_taken"], 1)
                if name[:4] == "proj":
                    t0, t1 = ((0, 2), (2, 3))[int(name[4])]
                    wait(dve, "finish_full", base + 1)
                    wait(dve, "hb_back", 16 * (b + 1))
                    nc.vector.tensor_tensor(h1[:, t0:t1, :], n_bank[:, 0:(t1 - t0) * D].rearrange("p (t d) -> p t d", d=D), h1[:, t0:t1, :], ALU.add)\
                        .then_inc(s["finish_taken"], 1)
                    wait(dve, "finish_taken", base + 1)
                    for t in range(t0, t1):
                        nc.vector.bn_stats(st_d[:, t, :], h1[:, t, :]).then_inc(s["st_d_done"], 1)
                    for t in range(t0, t1):
                        wait_apart(dve, "st_d_done", NT * b + t + 1)
                        nc.vector.bn_aggr(mv_d[:, t, :], st_d[:, t, :]).then_inc(s["mv_d_done"], 1)
                if name[:2] == "xn":
                    t = int(name[2])
                    wait(dve, "r_d_done", b + 1)
                    wait(dve, "scattered", 16 * NT * b)
                    last = nc.vector.tensor_scalar(xn[:, t, :], h1[:, t, :], mv_d[:, t, 0:1], r_d[:, t:t + 1], ALU.subtract, ALU.mult)
                    if t == NT - 1:
                        last.then_inc(s["xn_done"], 1)
                if name == "route":
                    wait(dve, "finish_full", base + 1)
                    nc.vector.tensor_copy(flat(lg[:, :, :]), n_bank[:, 0:NT * EXPERTS]).then_inc(s["finish_taken"], 1)
                    wait_apart(dve, "finish_taken", base + 1)
                    for t in range(NT):
                        last = nc.vector.max(m8[:, t, :], lg[:, t, :])
                    last.then_inc(s["m8_done"], 1)
                if name == "best":
                    wait(dve, "m8_done", b + 1)
                    nc.vector.tensor_tensor(df[:, :, :], lg[:, :, :], m8[:, :, 0:1].broadcast_to([P, NT, EXPERTS]), ALU.subtract).then_inc(s["df_done"], 1)
                    for t in range(NT):
                        last = nc.vector.max_index(i8[:, t, :], m8[:, t, :], lg[:, t, :])
                    last.then_inc(s["i8_done"], 1)
                if name == "chosen":
                    wait(dve, "i8_done", b + 1)
                    nc.vector.tensor_copy(ei[:, :], i8[:, :, 0]).then_inc(s["ei_done"], 1)
                    wait(dve, "ei_done", b + 1)
                    nc.vector.tensor_tensor(oh[:, :, :], iota8[:, None, :].broadcast_to([P, NT, EXPERTS]),
                                            ei[:, :, None].broadcast_to([P, NT, EXPERTS]), ALU.is_equal).then_inc(s["oh_done"], 1)
                if name == "totals":
                    wait(dve, "run_done", (NT + 1) * b)
                    nc.vector.tensor_copy(run[:, 0, :], run[:, NT, :]).then_inc(s["run_done"], 1)
                    wait(dve, "oh_done", b + 1)
                    for t in range(NT):
                        wait(dve, "run_done", (NT + 1) * b + t + 1)
                        nc.vector.tensor_tensor(run[:, t + 1, :], run[:, t, :], oh[:, t, :], ALU.add).then_inc(s["run_done"], 1)
                if name == "pick":
                    wait(dve, "ex_done", b + 1)
                    nc.vector.reduce_sum(se[:, :], ex[:, :, :], axis=AX.X).then_inc(s["se_done"], 1)
                    wait(dve, "se_done", 2 * b + 1)
                    nc.vector.reciprocal(se[:, :], se[:, :]).then_inc(s["se_done"], 1)
                if name == "count":
                    wait(dve, "finish_full", base + 1)
                    nc.vector.tensor_tensor(cp[:, :, :], n_bank[:, 0:NT * EXPERTS].rearrange("p (t e) -> p t e", e=EXPERTS), oh[:, :, :], ALU.mult)\
                        .then_inc(s["finish_taken"], 1)
                if name == "slots":
                    def done(i):
                        return 6 * b + i
                    wait(dve, "finish_taken", base)
                    nc.vector.reduce_sum(pos[:, :], cp[:, :, :], axis=AX.X).then_inc(s["slot_step"], 1)
                    wait(dve, "slot_step", done(1))
                    nc.vector.tensor_scalar(keep[:, :], pos[:, :], float(CAP), None, ALU.is_le).then_inc(s["slot_step"], 1)
                    nc.vector.scalar_tensor_tensor(out=slot[:, :], in0=ei[:, :], scalar=float(CAP), in1=pos[:, :], op0=ALU.mult, op1=ALU.add)\
                        .then_inc(s["slot_step"], 1)
                    wait(dve, "slot_step", done(3))
                    nc.vector.scalar_tensor_tensor(out=sk[:, :], in0=slot[:, :], scalar=-1.0, in1=keep[:, :], op0=ALU.add, op1=ALU.mult)\
                        .then_inc(s["slot_step"], 1)
                    nc.vector.tensor_scalar(drop[:, :], keep[:, :], -1.0, 1.0, ALU.mult, ALU.add).then_inc(s["slot_step"], 1)
                    wait(dve, "slot_step", done(5))
                    nc.vector.tensor_tensor(drop[:, :], drop[:, :], trash[:, bass.ds(b * NT, NT)], ALU.mult).then_inc(s["slot_step"], 1)
                    nc.vector.tensor_copy(gidx[:, bass.ds(b * NT, NT)], sk[:, :])
                    wait(dve, "se_done", 2 * b + 2)
                    nc.vector.tensor_tensor(gate[:, bass.ds(b * NT, NT)], keep[:, :], se[:, :], ALU.mult).then_inc(s["gate_done"], 1)
                    wait(dve, "slot_step", done(6))
                    nc.vector.tensor_tensor(si[:, :], sk[:, :], drop[:, :], ALU.add).then_inc(s["slots_done"], 1)

            def split_maxima(b, half):
                hs = slice(half * HALF, (half + 1) * HALF)
                wait(dve, "s_taken", STEPS * b + (half + 1) * HALF * NT)
                wait(dve, "m_full", 2 * (b - 1) + half + 1)
                nc.vector.tensor_scalar(nmx[:, :, half, 0, :].bitcast(F32R), mx[:, :, hs], -1.0, None, ALU.mult).then_inc(s["nmx_hi"], 1)
                wait(dve, "nmx_hi", 2 * b + half + 1)
                nc.vector.scalar_tensor_tensor(out=nmx[:, :, half, 1, :].bitcast(F32R), in0=mx[:, :, hs], scalar=-1.0, in1=nmx[:, :, half, 0, :],
                                               op0=ALU.mult, op1=ALU.subtract).then_inc(s["nmx_done"], 1)

            def take_maxima(b, half, before, samples):
                wait(dve, "m_full", 2 * b + half + 1)
                wait(dve, before, 32 * samples)
                nc.vector.tensor_copy(mT[:, half, :], v_bank[0:2 * HALF, 0:N]).then_inc(s["m_taken"], 1)

            def body(it, par, pair, fusion, shift, attend, finish):
                for n in range(STEPS):
                    if shift:
                        wait(dve, "s_full", STEPS * (it + 1) + n + 1)
                        nc.vector.reduce_max(mx[:, n % NT, n // NT:n // NT + 1], s_bank[n % SRING][:, 0:N], axis=AX.X).then_inc(s["s_taken"], 1)
                    if n == 0 and attend:
                        split_maxima(it, 1)
                    if n == MAX1_AT + LAG and attend:
                        take_maxima(it, 1, m_loaded[1 - par][1], pair(1))
                    if n == MAX0_AT - 2 and shift:
                        split_maxima(it + 1, 0)
                    if n == MAX0_AT + LAG and shift:
                        take_maxima(it + 1, 0, m_loaded[par][0], pair(0) + 1)
                    if fusion and n - LAG in FUSION_SLOTS:
                        fusion_task(FUSION_SLOTS[n - LAG], it + 2)
                    if finish and n - LAG in FINISH_SLOTS:
                        finish_task(FINISH_SLOTS[n - LAG], it - 1)

            pipeline(dve, body)

            dve.wait_ge(s["t_full"], B * NH * NT)

            def split_w1(e, c):
                f = slice(c * FF // W_CHUNKS, (c + 1) * FF // W_CHUNKS)
                wait(dve, "w1_hi_done", W_CHUNKS * e + c + 1)
                nc.vector.tensor_tensor(w1_lo[:, :, f], w1s[:, :, f], w1_hi[:, :, f].bitcast(F32), ALU.subtract).then_inc(s["w1_split"], 1)

            def split_w2(e, c):
                f = slice(c * FT // W_CHUNKS, (c + 1) * FT // W_CHUNKS)
                wait(dve, "w2_hi_done", W_CHUNKS * e + c + 1)
                nc.vector.tensor_tensor(w2_lo[:, f, :], w2s[:, f, :], w2_hi[:, f, :].bitcast(F32), ALU.subtract).then_inc(s["w2_split"], 1)

            def split_inputs(e):
                for i in range(DT):
                    wait(dve, "xeT_hi_done", DT * e + i + 1)
                    nc.vector.tensor_tensor(xeT_lo[:, i, :], xeT_bank[i][:, 0:CAP], xeT_hi[:, i, :].bitcast(F32), ALU.subtract)\
                        .then_inc(s["xeT_split"], 1)

            for c in range(W_CHUNKS):
                split_w1(0, c)
            split_inputs(0)

            def expert(e, another):
                for f in range(FT):
                    if f < W_CHUNKS:
                        split_w2(e, f)
                    wait(dve, "hid_hi_done", FT * e + f + 1)
                    nc.vector.tensor_tensor(hid_lo[:, f, :], act_out[:, f % 2, :], hid_hi[:, f, :].bitcast(F32), ALU.subtract)\
                        .then_inc(s["hid_split"], 1)
                if another:
                    split_inputs(e + 1)
                    for c in range(W_CHUNKS):
                        split_w1(e + 1, c)
                for part, (t0, t1) in enumerate(((0, 2), (2, 3))):
                    wait(dve, "y_full", 2 * e + part + 1)
                    wait(dve, "ye_stored", 16 * e)
                    nc.vector.tensor_copy(ye[:, t0:t1, :], s_bank[part][:, 0:(t1 - t0) * D].rearrange("p (t d) -> p t d", d=D))\
                        .then_inc(s["y_taken"], 1)

            over_experts(dve, expert)
            dve.wait_ge(s["h1_loaded"], 16)
            dve.wait_ge(s["gate_done"], B)
            for n in range(B * NT):
                dve.wait_ge(gathered[n % GRING], 16 * (n // GRING + 1))
                nc.vector.scalar_tensor_tensor(out=h1f[:, n, :], in0=yg[:, n % GRING, :], scalar=gate[:, n:n + 1], in1=h1f[:, n, :],
                                               op0=ALU.mult, op1=ALU.add).then_inc(s["combined"], 1)


def kernel(**inputs):
    import numpy as np

    import concourse.bacc as bacc
    from concourse.bass_utils import run_bass_kernel_spmd

    g = {k: np.asarray(v) for k, v in inputs.items()}
    heads = D // C
    x = g["x"]
    row = np.concatenate([np.tile(g["L0_tok_Wk_b"], heads), np.tile(g["L0_tok_Wv_b"], heads), g["L0_tok_out_b"], g["L0_tok_ln_g"],
                          g["L0_tok_ln_b"], g["L0_attn_b_proj"]])
    w5 = g["L0_attn_w_qkv"].reshape(D, NH, HD, 3)
    halves = w5[..., 0:2].reshape(D, 2, HALF, HD, 2).transpose(0, 1, 4, 3, 2).reshape(D, 2 * D)
    w_qkv = np.concatenate([halves, w5[..., 2].reshape(D, D)], axis=1)
    arrays = {
        "x_cl": x.transpose(0, 3, 1, 2).reshape(B, D, L),
        "x_lc": x.transpose(0, 2, 3, 1).reshape(B, L, D),
        "tokens": g["x_txt"].T,
        "rows": np.broadcast_to(row, (P, row.size)),
        "cols": np.stack([g["L0_attn_ln_scale"].reshape(DT, P).T, g["L0_attn_ln_bias"].reshape(DT, P).T], axis=1),
        "bq": g["L0_tok_Wq_b"].reshape(C, 1),
        "WkT": g["L0_tok_Wk_w"].T, "WvT": g["L0_tok_Wv_w"].T, "WqT": g["L0_tok_Wq_w"].T,
        "w_biasT": g["L0_tok_w_bias"].T, "maskT": g["L0_tok_local_mask"].T,
        "out_w": g["L0_tok_out_w"],
        "E0": g["L0_txt_E0"], "E1": g["L0_txt_E1"], "E2": g["L0_txt_E2"],
        "W0": g["L0_txt_W0"], "W1": g["L0_txt_W1"], "W2": g["L0_txt_W2"],
        "w_qkv": w_qkv, "w_proj": g["L0_attn_w_proj"],
        "router_w": g["L0_ffn_router_w"], "w1": g["L0_ffn_w1"], "w2": g["L0_ffn_w2"],
    }
    nc = bacc.Bacc("TRN2", target_bir_lowering=False, num_devices=1)
    nc.disable_value_cache = True
    feeds, aps = {}, {}
    for name, array in arrays.items():
        array = np.ascontiguousarray(array)
        feeds[f"in_{name}"] = array
        aps[name] = nc.dram_tensor(f"in_{name}", list(array.shape), mybir.dt.from_np(array.dtype), kind="ExternalInput").ap()
    out = nc.dram_tensor("out", [B, N, D], F32, kind="ExternalOutput").ap()
    early_fusion_kernel(nc, aps, out)
    result = run_bass_kernel_spmd(nc, [feeds], core_ids=[0])
    return result.results[0]["out"]
```
